# Optimizing a Trainium2 kernel written in Bass

```python
import numpy as np
import jax
import jax.numpy as jnp

def _softmax(x, axis=-1):
    return jax.nn.softmax(x, axis=axis)

def _gelu(x):
    return jax.nn.gelu(x, approximate=True)

def _silu(x):
    return jax.nn.silu(x)

def _sigmoid(x):
    return jax.nn.sigmoid(x)

def _layernorm(x, axis=-1, eps=1e-05):
    m = jnp.mean(x, axis=axis, keepdims=True)
    v = jnp.var(x, axis=axis, keepdims=True)
    return (x - m) / jnp.sqrt(v + eps)

def _scatter_add(tgt, idx, src, axis=0):
    return tgt.at[idx].add(src)

def _segment_sum(src, seg, n):
    return jax.ops.segment_sum(src, seg, n)
kernel_name = 'mk_vit_tower_cls_d1_tok_img768_r4_f1ec3d'

def setup_inputs(seed: int=0):
    np.random.seed(seed)
    _w = jnp.asarray

    def _rec_inputs():
        import jax
        import jax.numpy as jnp
        _rk = jax.random.key(seed)
        x = -0.00016672 + 0.999947 * jax.random.normal(jax.random.fold_in(_rk, 1), (64, 3, 96, 96), jnp.float32)
        cls_tok = 0.02 * jax.random.normal(jax.random.fold_in(_rk, 5), (1, 1, 192), jnp.float32)
        return (x, cls_tok)
    x, cls_tok = _rec_inputs()

    def _L0_tok_setup():
        import jax, jax.numpy as jnp
        import numpy as np
        PATCH = 16

        def _patchify(x, p):
            B, C, H, W = x.shape
            Hp, Wp = (H // p, W // p)
            xu = x.reshape(B, C, Hp, p, Wp, p).transpose(0, 1, 2, 4, 3, 5)
            num_patches = Hp * Wp
            return xu.reshape(B, num_patches, -1)
        key = jax.random.key(seed)
        k1, k2, k3 = jax.random.split(key, 3)
        B, C, H = (64, 3, 96)
        hidden = 192
        d = C * PATCH * PATCH
        x = jax.random.normal(k1, (B, C, H, H), dtype=jnp.float32)
        W = jax.random.normal(k2, (hidden, d), dtype=jnp.float32) * 0.02
        b = jax.random.normal(k3, (hidden,), dtype=jnp.float32) * 0.02
        return {'x': x, 'W': W, 'b': b}
    _L0_tok_all = _L0_tok_setup()
    _L0_tok_in = {k: v for k, v in _L0_tok_all.items() if k in ('W', 'b')}
    del _L0_tok_all

    def _L0_attn_setup():
        import jax, jax.numpy as jnp
        import numpy as np
        from jax import lax
        NUM_HEADS = 12
        BETA = 0.2
        KS = 3
        LN_EPS = 1e-05
        key = jax.random.key(seed)
        k1, k2 = jax.random.split(key)
        B, N, C = (4, 256, 192)
        x = jax.random.normal(k1, (B, N, C), dtype=jnp.float32)
        qkv_w = jax.random.normal(k2, (3 * C, C), dtype=jnp.float32) * 0.02
        qkv_b = jnp.zeros((3 * C,), dtype=jnp.float32)
        ln_g = jnp.ones((C,), dtype=jnp.float32)
        ln_b = jnp.zeros((C,), dtype=jnp.float32)
        return {'x': x, 'qkv_w': qkv_w, 'qkv_b': qkv_b, 'ln_g': ln_g, 'ln_b': ln_b}
    _L0_attn_all = _L0_attn_setup()
    _L0_attn_in = {k: v for k, v in _L0_attn_all.items() if k in ('qkv_w', 'qkv_b', 'ln_g', 'ln_b')}
    del _L0_attn_all

    def _L0_ffn_setup():
        import jax, jax.numpy as jnp
        import numpy as np
        B, S, D = (2, 256, 192)
        NF, NR, R, DS, K = (128, 128, 128, 64, 4)

        @jax.checkpoint
        def feature_fn(x, neurons, weights):
            all_h = jnp.einsum('bsd,ndr->bsnr', x, neurons)
            return jnp.einsum('bsnr,bsn->bsr', all_h, weights)

        @jax.checkpoint
        def restore_fn(h, neurons, weights):
            all_out = jnp.einsum('bsr,nrd->bsnd', h, neurons)
            return jnp.einsum('bsnd,bsn->bsd', all_out, weights)

        def topk_sparsify(weights, k):
            topk_vals, topk_idx = jax.lax.top_k(weights, k)
            N = weights.shape[-1]
            one_hot_mask = jax.nn.one_hot(topk_idx, N, dtype=weights.dtype)
            sparse = (one_hot_mask * topk_vals[..., jnp.newaxis]).sum(axis=-2)
            sparse = sparse / (sparse.sum(axis=-1, keepdims=True) + 1e-08)
            return (sparse, topk_idx)
        key = jax.random.key(seed)
        ks = jax.random.split(key, 8)
        x = jax.random.normal(ks[0], (B, S, D), jnp.float32)
        f_know = jax.random.normal(ks[1], (NF, D, R), jnp.float32) * 0.02
        r_know = jax.random.normal(ks[2], (NR, R, D), jnp.float32) * 0.02
        W_fk = jax.random.normal(ks[3], (D, DS), jnp.float32) * 0.02
        b_fk = jnp.zeros((DS,), jnp.float32)
        W_rk = jax.random.normal(ks[4], (D, DS), jnp.float32) * 0.02
        b_rk = jnp.zeros((DS,), jnp.float32)
        emb_fk = jax.random.normal(ks[5], (NF, DS), jnp.float32) * 0.02
        emb_rk = jax.random.normal(ks[6], (NR, DS), jnp.float32) * 0.02
        return {'x': x, 'f_know': f_know, 'r_know': r_know, 'W_fk': W_fk, 'b_fk': b_fk, 'W_rk': W_rk, 'b_rk': b_rk, 'emb_fk': emb_fk, 'emb_rk': emb_rk}
    _L0_ffn_all = _L0_ffn_setup()
    _L0_ffn_in = {k: v for k, v in _L0_ffn_all.items() if k in ('f_know', 'r_know', 'W_fk', 'b_fk', 'W_rk', 'b_rk', 'emb_fk', 'emb_rk')}
    del _L0_ffn_all
    return {'x': x, 'cls_tok': cls_tok, 'L0_tok_W': _L0_tok_in['W'], 'L0_tok_b': _L0_tok_in['b'], 'L0_attn_qkv_w': _L0_attn_in['qkv_w'], 'L0_attn_qkv_b': _L0_attn_in['qkv_b'], 'L0_attn_ln_g': _L0_attn_in['ln_g'], 'L0_attn_ln_b': _L0_attn_in['ln_b'], 'L0_ffn_f_know': _L0_ffn_in['f_know'], 'L0_ffn_r_know': _L0_ffn_in['r_know'], 'L0_ffn_W_fk': _L0_ffn_in['W_fk'], 'L0_ffn_b_fk': _L0_ffn_in['b_fk'], 'L0_ffn_W_rk': _L0_ffn_in['W_rk'], 'L0_ffn_b_rk': _L0_ffn_in['b_rk'], 'L0_ffn_emb_fk': _L0_ffn_in['emb_fk'], 'L0_ffn_emb_rk': _L0_ffn_in['emb_rk']}

def reference(x, cls_tok, L0_tok_W, L0_tok_b, L0_attn_qkv_w, L0_attn_qkv_b, L0_attn_ln_g, L0_attn_ln_b, L0_ffn_f_know, L0_ffn_r_know, L0_ffn_W_fk, L0_ffn_b_fk, L0_ffn_W_rk, L0_ffn_b_rk, L0_ffn_emb_fk, L0_ffn_emb_rk):
    import jax
    import jax.numpy as jnp

    def _L0_tok_ref(x, W, b):
        import jax, jax.numpy as jnp
        import numpy as np
        PATCH = 16

        def _patchify(x, p):
            B, C, H, W = x.shape
            Hp, Wp = (H // p, W // p)
            xu = x.reshape(B, C, Hp, p, Wp, p).transpose(0, 1, 2, 4, 3, 5)
            num_patches = Hp * Wp
            return xu.reshape(B, num_patches, -1)
        patches = _patchify(x, PATCH)
        return jnp.einsum('bnd,hd->bnh', patches, W) + b

    def _L0_attn_ref(x, qkv_w, qkv_b, ln_g, ln_b):
        import jax, jax.numpy as jnp
        import numpy as np
        from jax import lax
        NUM_HEADS = 12
        BETA = 0.2
        KS = 3
        LN_EPS = 1e-05
        B, N, C = x.shape
        H = NUM_HEADS
        D = C // H
        mu = jnp.mean(x, axis=-1, keepdims=True)
        var = jnp.mean(jnp.square(x - mu), axis=-1, keepdims=True)
        xn = (x - mu) * lax.rsqrt(var + LN_EPS) * ln_g + ln_b
        qkv = xn @ qkv_w.T + qkv_b
        qkv = qkv.reshape(B, N, 3, H, D).transpose(2, 0, 3, 1, 4)
        q, k, v = (qkv[0], qkv[1], qkv[2])
        attn = jnp.einsum('bhnd,bhmd->bhnm', q, k) * D ** (-0.5)
        kernel = jnp.ones((KS, KS), dtype=attn.dtype).at[KS // 2, KS // 2].set(0.0)
        kernel = kernel.reshape(1, 1, KS, KS)
        neigh = lax.conv_general_dilated(attn.reshape(B * H, 1, N, N), kernel, window_strides=(1, 1), padding='SAME', dimension_numbers=('NCHW', 'OIHW', 'NCHW'))
        attn = attn - BETA * neigh.reshape(B, H, N, N)
        attn = jax.nn.softmax(attn - jnp.max(attn, axis=-1, keepdims=True), axis=-1)
        out = jnp.einsum('bhnm,bhmd->bhnd', attn, v)
        return out.transpose(0, 2, 1, 3).reshape(B, N, C)

    def _L0_ffn_ref(x, f_know, r_know, W_fk, b_fk, W_rk, b_rk, emb_fk, emb_rk):
        import jax, jax.numpy as jnp
        import numpy as np
        B, S, D = (2, 256, 192)
        NF, NR, R, DS, K = (128, 128, 128, 64, 4)

        @jax.checkpoint
        def feature_fn(x, neurons, weights):
            all_h = jnp.einsum('bsd,ndr->bsnr', x, neurons)
            return jnp.einsum('bsnr,bsn->bsr', all_h, weights)

        @jax.checkpoint
        def restore_fn(h, neurons, weights):
            all_out = jnp.einsum('bsr,nrd->bsnd', h, neurons)
            return jnp.einsum('bsnd,bsn->bsd', all_out, weights)

        def topk_sparsify(weights, k):
            topk_vals, topk_idx = jax.lax.top_k(weights, k)
            N = weights.shape[-1]
            one_hot_mask = jax.nn.one_hot(topk_idx, N, dtype=weights.dtype)
            sparse = (one_hot_mask * topk_vals[..., jnp.newaxis]).sum(axis=-2)
            sparse = sparse / (sparse.sum(axis=-1, keepdims=True) + 1e-08)
            return (sparse, topk_idx)
        emb_fk_n = emb_fk / (jnp.linalg.norm(emb_fk, axis=-1, keepdims=True) + 1e-08)
        emb_rk_n = emb_rk / (jnp.linalg.norm(emb_rk, axis=-1, keepdims=True) + 1e-08)
        logits_fk = jnp.einsum('bsd,nd->bsn', x @ W_fk + b_fk, emb_fk_n)
        logits_rk = jnp.einsum('bsd,nd->bsn', x @ W_rk + b_rk, emb_rk_n)
        w_fk, _ = topk_sparsify(jax.nn.softmax(logits_fk, axis=-1), K)
        w_rk, _ = topk_sparsify(jax.nn.softmax(logits_rk, axis=-1), K)
        h = feature_fn(x, f_know, w_fk)
        out = restore_fn(h, r_know, w_rk)
        return out
    h = _L0_tok_ref(x, L0_tok_W, L0_tok_b)
    h = jnp.concatenate([jnp.broadcast_to(cls_tok, (h.shape[0], 1, h.shape[2])), h], axis=1)
    h = h + _L0_attn_ref(_layernorm(h, axis=-1), L0_attn_qkv_w, L0_attn_qkv_b, L0_attn_ln_g, L0_attn_ln_b)
    h = h + _L0_ffn_ref(_layernorm(h, axis=-1), L0_ffn_f_know, L0_ffn_r_know, L0_ffn_W_fk, L0_ffn_b_fk, L0_ffn_W_rk, L0_ffn_b_rk, L0_ffn_emb_fk, L0_ffn_emb_rk)
    return h

_drawn_inputs = setup_inputs


def setup_inputs(seed=0):
    import zlib

    import numpy as np

    out = dict(_drawn_inputs(seed))
    spreads = {'L0_attn_qkv_b': (0.0, 0.1),
     'L0_attn_ln_g': (1.0, 0.6),
     'L0_attn_ln_b': (0.0, 0.1),
     'L0_ffn_b_fk': (0.0, 0.364),
     'L0_ffn_b_rk': (0.0, 0.364)}
    factors = {'cls_tok': 3.455}
    for name, (base, spread) in spreads.items():
        noise = np.random.default_rng([zlib.crc32(name.encode()), seed]).standard_normal(out[name].shape)
        drawn = base * np.exp(spread * noise) if base else spread * noise
        out[name] = jnp.asarray(drawn.astype(out[name].dtype))
    for name, factor in factors.items():
        out[name] = (out[name] * factor).astype(out[name].dtype)
    return out
```

```python
import numpy as np
import concourse.bass as bass
from concourse import mybir
from contextlib import ExitStack

F32 = mybir.dt.float32
BF16 = mybir.dt.bfloat16
I32 = mybir.dt.int32
U32 = mybir.dt.uint32
ALU = mybir.AluOpType
ACT = mybir.ActivationFunctionType
AX = mybir.AxisListType

BATCH, CH, IMG, PATCH = 64, 3, 96, 16
HP = IMG // PATCH
TOK = HP * HP + 1
D = 192
DH = D // 2
HEADS, HD = 12, 16
HEADS_PER_QUAD = 4
QUADS = HEADS // HEADS_PER_QUAD
HALVES = 2
LN_EPS = 1e-5
BETA = 0.2
SCALE = HD ** -0.5

G_IMG = 8
GROUPS = BATCH // G_IMG
TILES = G_IMG // 2
SPAN = 64 + TOK
PAD = TOK + 2
SUB = G_IMG // 2 * CH * HP
LINE = PATCH * IMG
VG = 3
VGROUPS = HEADS // VG
VW = HD + 1

EXPERTS, RANK, DS, TOPK = 128, 128, 64, 4
TOKENS = BATCH * TOK
ROWS = 128
TTILES = -(-TOKENS // ROWS)
PTOK = TTILES * ROWS
LAST = TOKENS - (TTILES - 1) * ROWS
PAIRS = TTILES // 2
MAX_BLOCKS = (PTOK * TOPK + EXPERTS * (ROWS - 1)) // ROWS
SB = 4
RING = 3
BODY = SB * RING
STEPS = -(-MAX_BLOCKS // BODY)
BLOCKS = STEPS * BODY
SLOTS = BLOCKS * ROWS


def tower(nc, x, cls_tok, tok_w, tok_b, qkv_w, qkv_b, ln_g, ln_b,
          f_know, r_know, w_fk, b_fk, w_rk, b_rk, emb_fk, emb_rk, out):
    ctx = ExitStack()
    with ctx:
        phase = [ctx]

        def sb(name, shape, dt=F32):
            return phase[0].enter_context(nc.sbuf_tensor(name, shape, dt))

        def sem(name):
            return ctx.enter_context(nc.semaphore(name))

        bank = [ctx.enter_context(nc.psum_tensor(f"bank{i}", [128, 512], F32)) for i in range(8)]

        h2_dram = nc.dram_tensor("h2_dram", [PTOK, D], F32, kind="Internal").ap()
        x2_dram = nc.dram_tensor("x2_dram", [PTOK, D], F32, kind="Internal").ap()
        wide_dram = nc.dram_tensor("wide_dram", [SLOTS, D], F32, kind="Internal").ap()
        mid_dram = nc.dram_tensor("mid_dram", [SLOTS, RANK], F32, kind="Internal").ap()
        mid2_dram = nc.dram_tensor("mid2_dram", [SLOTS, RANK], F32, kind="Internal").ap()

        ident = sb("ident", [128, 128])
        ones = sb("ones", [128, 128])
        before = sb("before", [128, 128], BF16)
        after = sb("after", [128, 128], BF16)
        upto = sb("upto", [128, 128], BF16)
        ones_bf = sb("ones_bf", [128, 1], BF16)
        zeros_bf = sb("zeros_bf", [128, 256], BF16)
        head_mask = sb("head_mask", [VG * TOK, VG, VW])
        iota_n = sb("iota_n", [128, EXPERTS])
        iota_blk = sb("iota_blk", [128, BLOCKS])
        ZW = 1632
        magic = sb("magic", [128, TILES], I32)
        zeros = sb("zeros", [128, ZW])
        part_i = sb("part_i", [128, 1], I32)
        part_b = sb("part_b", [128, 1], I32)
        neigh = sb("neigh", [128, 1])
        qk_scale = sb("qk_scale", [128, 2])
        tmp_col = sb("tmp_col", [128, 1])

        tok_nat = sb("tok_nat", [DH, 2, CH * PATCH * PATCH])
        tok_wT = sb("tok_wT", [128, CH * HALVES, D])
        tok_bias = sb("tok_bias", [SPAN, D])
        qkv_nat = sb("qkv_nat", [DH, 6, D])
        w_qkT = sb("w_qkT", [DH, 2, 2 * HEADS, 2, HD])
        w_vT = sb("w_vT", [DH, 2, D])
        g_col = sb("g_col", [DH, 2])
        b_col = sb("b_col", [DH, 2])
        qk_brow = sb("qk_brow", [1, 2 * HEADS, 2, HD])
        v_brow = sb("v_brow", [1, D])
        qk_bias = sb("qk_bias", [128, 2 * QUADS])
        v_bias = sb("v_bias", [SPAN, D])
        emb = sb("emb", [128, 2, DS])
        emb_sq = sb("emb_sq", [128, 2, DS])
        emb_n2 = sb("emb_n2", [128, 2])
        emb_a = sb("emb_a", [128, 2])
        emb_y = sb("emb_y", [128, 2])
        emb_t = sb("emb_t", [128, 2])
        emb_n1 = sb("emb_n1", [128, 2])
        emb_inv = sb("emb_inv", [128, 2])
        emb_nrm = sb("emb_nrm", [128, 2, DS])
        embT = sb("embT", [DS, 2, EXPERTS])
        wr_nat = sb("wr_nat", [DH, 2, 2, DS])
        wrT = sb("wrT", [DS, 2, D])
        br_col = sb("br_col", [DS, 2])
        r_mat = sb("r_mat", [DH, 2, 2 * EXPERTS])
        r_bias = sb("r_bias", [128, 2 * EXPERTS])

        x2t = [sb(f"x2t{i}", [ROWS, D]) for i in range(2)]
        x2T = [sb(f"x2T{i}", [DH, 2, ROWS]) for i in range(2)]
        logit = [sb(f"logit{i}", [ROWS, 2, EXPERTS]) for i in range(2)]
        escr = [sb(f"escr{i}", [ROWS, 2, EXPERTS]) for i in range(2)]
        top8 = [sb(f"top8_{i}", [ROWS, 2, 8]) for i in range(2)]
        idx8 = [sb(f"idx8_{i}", [ROWS, 2, 8], U32) for i in range(2)]
        nmax = [sb(f"nmax{i}", [ROWS, 2]) for i in range(2)]
        etop = [sb(f"etop{i}", [ROWS, 2, TOPK]) for i in range(2)]
        zsum = [sb(f"zsum{i}", [ROWS, 2]) for i in range(2)]
        s4 = [sb(f"s4_{i}", [ROWS, 2]) for i in range(2)]
        den = [sb(f"den{i}", [ROWS, 2]) for i in range(2)]
        iden = [sb(f"iden{i}", [ROWS, 2]) for i in range(2)]
        hot = [sb(f"hot{i}", [ROWS, 2, TOPK, EXPERTS], BF16) for i in range(2)]
        idxf = sb("idxf", [ROWS, TTILES, 2, TOPK])
        wts = sb("wts", [ROWS, TTILES, 2, TOPK])
        rank = sb("rank", [ROWS, TTILES, 2 * EXPERTS])
        cnt_i = sb("cnt_i", [128, 2], I32)
        nblk_i = sb("nblk_i", [128, 2], I32)
        nblk = sb("nblk", [128, 2], BF16)
        cum = sb("cum", [128, 2])
        base_c = sb("base_c", [128, 2])
        diag = sb("diag", [128, 2, 128])
        base_b = sb("base_b", [128, 2 * EXPERTS])
        passed = sb("passed", [128, 2, BLOCKS], BF16)
        owner = sb("owner", [1, 2, BLOCKS], I32)
        srank = [sb(f"srank{i}", [ROWS, 2 * EXPERTS]) for i in range(2)]
        pick = sb("pick", [ROWS, 2 * TOPK, EXPERTS])
        slotf = [sb(f"slotf{i}", [ROWS, 2 * TOPK]) for i in range(2)]
        slot_now = [sb(f"slot_now{i}", [ROWS, 2 * TOPK], I32) for i in range(2)]
        slot_get = [sb(f"slot_get{i}", [ROWS, 2 * TOPK], I32) for i in range(2)]
        slot_put = [sb(f"slot_put{i}", [ROWS, 2 * TOPK], I32) for i in range(2)]
        acc = [sb(f"acc{i}", [ROWS, 2, D]) for i in range(2)]
        slots = sb("slots", [ROWS, TTILES, 2 * TOPK], I32)

        phase[0] = ExitStack()
        lines = [sb(f"lines{s}", [SUB, LINE]) for s in range(2)]
        patches = [sb(f"patches{s}", [SUB, HALVES, HP, 128]) for s in range(2)]
        pixT = sb("pixT", [128, HALVES, CH, G_IMG, 64])
        h = sb("h", [SPAN, TILES, D])
        h_res = sb("h_res", [SPAN, TILES, D])
        st = sb("st", [SPAN, TILES, 6])
        mv = sb("mv", [SPAN, TILES, 2])
        va = sb("va", [SPAN, TILES])
        rr = sb("rr", [SPAN, TILES])
        rt = sb("rt", [SPAN, TILES])
        xn = sb("xn", [SPAN, TILES, D])
        xnT = sb("xnT", [DH, 2, G_IMG, TOK])
        xnT_rep = sb("xnT_rep", [DH, 2 * G_IMG, VG, TOK])
        qk_pad = sb("qk_pad", [128, 2 * QUADS * G_IMG, PAD])
        qk_sum = sb("qk_sum", [128, 2 * QUADS * G_IMG, TOK])
        qk = sb("qk", [128, 2 * QUADS, G_IMG, TOK])
        k_quad = sb("k_quad", [128, QUADS * G_IMG, HEADS_PER_QUAD, TOK])
        vals = sb("vals", [VG * TOK, G_IMG, VGROUPS, VG, VW])
        smax = sb("smax", [SPAN, 2, HEADS])
        probs = sb("probs", [SPAN, 2, HEADS, TOK])
        probsT = sb("probsT", [VG * TOK, 2, VGROUPS, SPAN])
        rsum = sb("rsum", [SPAN, HEADS])
        att = sb("att", [SPAN, HEADS, HD])
        h2 = sb("h2", [SPAN, TILES, D])
        st2 = sb("st2", [SPAN, TILES, 6])
        mv2 = sb("mv2", [SPAN, TILES, 2])
        va2 = sb("va2", [SPAN, TILES])
        rs2 = sb("rs2", [SPAN, TILES])
        rt2 = sb("rt2", [SPAN, TILES])
        x2 = sb("x2", [SPAN, TILES, D])

        phase[0].close()

        phase[0] = ExitStack()
        xs = [sb(f"xs{r}", [ROWS, SB, D]) for r in range(RING)]
        fw = [sb(f"fw{r}", [128, SB, 256]) for r in range(RING)]
        xsT = [sb(f"xsT{i}", [128, 256]) for i in range(2)]
        os_ = [sb(f"os{r}", [ROWS, SB, D]) for r in range(2)]
        gat = [sb(f"gat{i}", [ROWS, TOPK, D]) for i in range(2)]
        comb = [sb(f"comb{i}", [ROWS, D]) for i in range(2)]
        h2t = [sb(f"h2t{i}", [ROWS, D]) for i in range(2)]

        phase[0].close()
        phase[0] = ctx
        w_loaded = sem("w_loaded")
        cls_loaded = sem("cls_loaded")
        pool_step = sem("pool_step")
        consts = sem("consts")
        zeroed = sem("zeroed")
        setup_ps = sem("setup_ps")
        setup_ev = sem("setup_ev")
        dve_step = sem("dve_step")
        embn_ready = sem("embn_ready")
        raw_used = sem("raw_used")
        lines_loaded = [sem(f"lines_loaded{s}") for s in range(2)]
        ring_filled = sem("ring_filled")
        ring_emptied = sem("ring_emptied")
        patch_done = sem("patch_done")
        patches_ready = sem("patches_ready")
        rep_ready = sem("rep_ready")
        st_ready = sem("st_ready")
        rr_step = sem("rr_step")
        rr_ready = sem("rr_ready")
        mv2_ready = sem("mv2_ready")
        rs2_ready = sem("rs2_ready")
        emb_a_ready = sem("emb_a_ready")
        emb_y_step = sem("emb_y_step")
        emb_y_ready = sem("emb_y_ready")
        rs2_step = sem("rs2_step")
        taken = sem("taken")
        smax_ready = sem("smax_ready")
        fin_step = sem("fin_step")
        nrm_step = sem("nrm_step")
        top_ready = sem("top_ready")
        wt_step = sem("wt_step")
        slot_step = sem("slot_step")
        comb_step = [sem(f"comb_step{p}") for p in range(2)]
        h_ready = sem("h_ready")
        res_ready = sem("res_ready")
        res_used = sem("res_used")
        xn_ready = sem("xn_ready")
        xn_transposed = sem("xn_transposed")
        xnT_copied = sem("xnT_copied")
        sums_ready = sem("sums_ready")
        cat_ready = sem("cat_ready")
        quad_ready = sem("quad_ready")
        v_filled = sem("v_filled")
        v_masked = sem("v_masked")
        scores_done = sem("scores_done")
        scores_read = sem("scores_read")
        probs_ready = sem("probs_ready")
        p_transposed = sem("p_transposed")
        pT_copied = sem("pT_copied")
        pv_done = sem("pv_done")
        o_read = sem("o_read")
        h2_ready = sem("h2_ready")
        x2_ready = sem("x2_ready")
        stored = sem("stored")

        x2t_loaded = [sem(f"x2t_loaded{i}") for i in range(2)]
        x2T_filled = sem("x2T_filled")
        x2T_copied = sem("x2T_copied")
        logit_filled = sem("logit_filled")
        logit_ready = sem("logit_ready")
        nmax_ready = sem("nmax_ready")
        exp_done = sem("exp_done")
        hot_ready = sem("hot_ready")
        rank_filled = sem("rank_filled")
        rank_copied = sem("rank_copied")
        hot_used = sem("hot_used")
        plan_ps = sem("plan_ps")
        plan_ev = sem("plan_ev")
        slot_ready = sem("slot_ready")
        scattered = [sem(f"scattered{i}") for i in range(2)]
        x2t_again = [sem(f"x2t_again{i}") for i in range(2)]
        scat_used = sem("scat_used")

        xs_loaded = [[sem(f"xs_loaded{p}_{r}") for r in range(RING)] for p in range(2)]
        fw_loaded = [[sem(f"fw_loaded{p}_{r}") for r in range(RING)] for p in range(2)]
        t_filled = [sem(f"t_filled{p}") for p in range(2)]
        t_copied = [sem(f"t_copied{p}") for p in range(2)]
        y_filled = [sem(f"y_filled{p}") for p in range(2)]
        y_copied = [sem(f"y_copied{p}") for p in range(2)]
        y_stored = [[sem(f"y_stored{p}_{i}") for i in range(2)] for p in range(2)]

        idx_ready = [sem(f"idx_ready{p}") for p in range(2)]
        gathered = [[sem(f"gathered{p}_{i}") for i in range(2)] for p in range(2)]
        comb_ready = [sem(f"comb_ready{p}") for p in range(2)]
        comb_out = [[sem(f"comb_out{p}_{i}") for i in range(2)] for p in range(2)]
        h2t_loaded = [sem(f"h2t_loaded{i}") for i in range(2)]

        def take(engine):
            engine.sem_inc(taken, 1)

        block = ctx.enter_context(nc.Block())

        lines_view = x.rearrange("b c (hp r) w -> (b c hp) (r w)", r=PATCH)
        f_view = f_know.rearrange("n (p j) r -> (n p) (j r)", j=2)
        r_view = r_know.rearrange("n r d -> (n r) d")
        SUPERS = STEPS * RING
        W_LOADS = 16
        PAIRED = 2 * PAIRS

        @block.sync
        def _(sp):
            sp.dma_start(lines[0][:], lines_view[0:SUB, :]).then_inc(lines_loaded[0], 16)
            sp.dma_start(lines[1][:], lines_view[SUB:2 * SUB, :]).then_inc(lines_loaded[1], 16)
            n = 0
            for dst, src in (
                    (tok_nat[:], tok_w.rearrange("(c p) k -> p c k", p=DH)),
                    (qkv_nat[:], qkv_w.rearrange("(c p) k -> p c k", p=DH)),
                    (tok_bias[:], tok_b.partition_broadcast(SPAN)),
                    (g_col[:], ln_g.rearrange("(j p) -> p j", p=DH)),
                    (b_col[:], ln_b.rearrange("(j p) -> p j", p=DH)),
                    (qk_brow[:, :, 0, :], qkv_b[0:2 * D].rearrange("(o n j) -> o n j", o=1, j=HD)),
                    (qk_brow[:, :, 1, :], qkv_b[0:2 * D].rearrange("(o n j) -> o n j", o=1, j=HD)),
                    (v_brow[:], qkv_b[2 * D:3 * D].rearrange("(o n) -> o n", o=1)),
                    (emb[:, 0, :], emb_fk), (emb[:, 1, :], emb_rk),
                    (wr_nat[:, 0], w_fk.rearrange("(j p) k -> p j k", p=DH)),
                    (wr_nat[:, 1], w_rk.rearrange("(j p) k -> p j k", p=DH)),
                    (br_col[:, 0:1], b_fk.rearrange("(p o) -> p o", o=1)),
                    (br_col[:, 1:2], b_rk.rearrange("(p o) -> p o", o=1))):
                sp.dma_start(dst, src, allow_slow_non_contiguous=True).then_inc(w_loaded, 16)
                n += 1
            sp.wait_ge(w_loaded, 16 * n)
            for a in range(2):
                sp.dma_start(tok_bias[64 * a:64 * a + 1, :], cls_tok[0]).then_inc(cls_loaded, 16)
            sp.wait_ge(consts, 1)
            for dram, width in ((wide_dram, D), (mid2_dram, RANK)):
                k = SLOTS * width // 128 // ZW
                view = dram.rearrange("(p r) d -> p (r d)", p=128).rearrange("p (k z) -> p k z", z=ZW)
                sp.dma_start(view, zeros[:, None, :].to_broadcast([128, k, ZW])).then_inc(zeroed, 16)
            for dram in (h2_dram, x2_dram):
                sp.dma_start(dram[TOKENS:PTOK, :], zeros[0:PTOK - TOKENS, 0:D]).then_inc(zeroed, 16)

            def store_group(g):
                sp.wait_ge(h2_ready, TILES * (g + 1))
                sp.wait_ge(x2_ready, TILES * (g + 1))
                for dram, tile in ((h2_dram, h2), (x2_dram, x2)):
                    for a in range(2):
                        rows = dram[bass.ds((g * G_IMG + 0) * TOK, G_IMG * TOK), :]
                        view = rows.rearrange("(t a n) d -> n t a d", a=2, n=TOK)
                        sp.dma_start(view[:, :, a, :], tile[64 * a:64 * a + TOK]).then_inc(stored, 16)

            def load_lines(g1):
                for s in range(2):
                    sp.wait_ge(patches_ready, 2 * (g1 - 1) + s + 1)
                    row = g1 * (2 * SUB) + s * SUB
                    sp.dma_start(lines[s][:], lines_view[bass.ds(row, SUB), :]).then_inc(lines_loaded[s], 16)

            load_lines(1)
            with sp.Fori(0, GROUPS - 2) as g:
                load_lines(g + 2)
                store_group(g)
            store_group(GROUPS - 2)
            store_group(GROUPS - 1)

            sp.wait_ge(stored, 16 * 4 * GROUPS)
            sp.wait_ge(zeroed, 16 * 4)

            def load_x2(t, i):
                sp.wait_ge(x2T_filled, t + 1)
                sp.dma_start(x2t[i][:], x2_dram[bass.ds(t * ROWS, ROWS), :]).then_inc(x2t_loaded[i], 16)

            with sp.Fori(0, PAIRS) as p:
                for i in range(2):
                    load_x2(2 * p + i, i)
            load_x2(PAIRED, 0)

            sp.wait_ge(x2T_filled, TTILES + 2)
            def load_x2_again(t, i):
                sp.wait_ge(scat_used, t + 1)
                sp.dma_start(x2t[i][:], x2_dram[bass.ds(t * ROWS, ROWS), :]).then_inc(x2t_again[i], 16)

            with sp.Fori(0, PAIRS) as p:
                for i in range(2):
                    load_x2_again(2 * p + i, i)
            load_x2_again(PAIRED, 0)

            def expert_loads(layer):
                src = (wide_dram, mid2_dram)[layer]
                width = (D, RANK)[layer]
                with sp.Fori(0, STEPS) as s:
                    for r in range(RING):
                        sp.wait_ge(y_filled[layer], 2 * (s * RING + r) + 2)
                        rows = src[bass.ds((s * RING + r) * (SB * ROWS), SB * ROWS), :]
                        sp.dma_start(xs[r][:, :, 0:width], rows.rearrange("(k p) d -> p k d", p=ROWS))\
                          .then_inc(xs_loaded[layer][r], 16)
                        for k in range(SB):
                            e = sp.value_load(owner[0:1, layer, bass.ds((s * RING + r) * SB + k, 1)],
                                              min_val=0, max_val=EXPERTS - 1)
                            if layer == 0:
                                sp.dma_start(fw[r][0:DH, k, :], f_view[bass.ds(e * DH, DH), :])\
                                  .then_inc(fw_loaded[0][r], 16)
                            else:
                                sp.dma_start(fw[r][:, k, 0:D], r_view[bass.ds(e * RANK, RANK), :])\
                                  .then_inc(fw_loaded[1][r], 16)

            sp.wait_ge(plan_ev, 4)
            for i in range(2):
                sp.wait_ge(scattered[i], 64 * (PAIRS + (1 - i)))
            expert_loads(0)
            for i in range(2):
                sp.wait_ge(comb_out[0][i], 64 * (PAIRS + (1 - i)))
            expert_loads(1)

            def load_h2(t, i):
                sp.dma_start(h2t[i][:], h2_dram[bass.ds(t * ROWS, ROWS), :]).then_inc(h2t_loaded[i], 16)

            def store_out(t, i, n):
                sp.wait_ge(comb_ready[1], t + 1)
                sp.dma_start(out[bass.ds(t * ROWS, n), :], comb[i][0:n, :]).then_inc(comb_out[1][i], 16)

            for i in range(2):
                load_h2(i, i)
            with sp.Fori(0, PAIRS - 1) as p:
                for i in range(2):
                    store_out(2 * p + i, i, ROWS)
                for i in range(2):
                    load_h2(2 * p + 2 + i, i)
            for i in range(2):
                store_out(2 * PAIRS - 2 + i, i, ROWS)
            load_h2(PAIRED, 0)
            store_out(PAIRED, 0, LAST)
            for i in range(2):
                sp.wait_ge(comb_out[1][i], 16 * (PAIRS + (1 - i)))

        @block.gpsimd
        def _(pool):
            pool.sem_inc(scat_used, 2)
            step = [0]

            def link(ins):
                step[0] += 1
                ins.then_inc(pool_step, 1)
                pool.wait_ge(pool_step, step[0])

            pool.memset(zeros[:], 0.0).then_inc(consts, 1)
            link(pool.memset(ident[:], 0.0))
            link(pool.affine_select(out=ident[:], in_=ident[:], compare_op=ALU.not_equal, fill=1.0,
                                    base=0, pattern=[[-1, 128]], channel_multiplier=1))
            link(pool.memset(before[:], 1.0))
            link(pool.affine_select(out=before[:], in_=before[:], compare_op=ALU.is_gt, fill=0.0,
                                    base=0, pattern=[[1, 128]], channel_multiplier=-1))
            link(pool.memset(after[:], 1.0))
            link(pool.affine_select(out=after[:], in_=after[:], compare_op=ALU.is_ge, fill=0.0,
                                    base=0, pattern=[[-1, 128]], channel_multiplier=1))
            link(pool.memset(upto[:], 1.0))
            link(pool.affine_select(out=upto[:], in_=upto[:], compare_op=ALU.is_ge, fill=0.0,
                                    base=0, pattern=[[1, 128]], channel_multiplier=-1))
            link(pool.memset(head_mask[:], 1.0))
            link(pool.affine_select(out=head_mask[:], in_=head_mask[:], compare_op=ALU.is_ge, fill=0.0,
                                    base=0, pattern=[[-TOK, VG], [0, VW]], channel_multiplier=1))
            link(pool.affine_select(out=head_mask[:], in_=head_mask[:], compare_op=ALU.is_ge, fill=0.0,
                                    base=TOK - 1, pattern=[[TOK, VG], [0, VW]], channel_multiplier=-1))
            link(pool.iota(iota_n[:], pattern=[[1, EXPERTS]], base=0, channel_multiplier=0,
                           allow_small_or_imprecise_dtypes=True))
            link(pool.iota(iota_blk[:], pattern=[[1, BLOCKS]], base=0, channel_multiplier=0,
                           allow_small_or_imprecise_dtypes=True))
            link(pool.iota(part_i[:], pattern=[[0, 1]], base=0, channel_multiplier=1))
            link(pool.memset(pixT[:], 0.0))
            link(pool.memset(qk_pad[:], 0.0))
            link(pool.memset(k_quad[:], 0.0))
            link(pool.memset(magic[:], 0x5f3759df + 1))
            link(pool.memset(ones_bf[:], 1.0))
            link(pool.memset(zeros_bf[:], 0.0))
            pool.memset(ones[:], 1.0).then_inc(consts, 1)

            def regroup(g1):
                for s in range(2):
                    pool.wait_ge(lines_loaded[s], 16 * (g1 + 1))
                    take(pool)
                    if not (isinstance(g1, int) and g1 == 0):
                        pool.wait_ge(ring_filled, 10 * (g1 - 1) + 2 * s + 2)
                        take(pool)
                    for half in range(HALVES):
                        w = LINE // HALVES
                        src = lines[s][:, half * w:(half + 1) * w].rearrange("q (r w c) -> q w r c", r=8, c=PATCH)
                        dst = patches[s][:, half].rearrange("q w (r c) -> q w r c", c=PATCH)
                        last = pool.tensor_copy(dst, src)
                    last.then_inc(patches_ready, 1)

            STEPS_OF_ROOT = 12

            def inverse_root(y, a, t, steps, n, ready):
                pool.tensor_tensor(y.bitcast(I32), y.bitcast(I32), magic[0:y.shape[0], 0:y.shape[1]], ALU.add)\
                    .then_inc(steps, 1)
                for i in range(3):
                    pool.wait_ge(steps, n + 4 * i + 1)
                    pool.tensor_tensor(t, y, y, ALU.mult).then_inc(steps, 1)
                    pool.wait_ge(steps, n + 4 * i + 2)
                    pool.tensor_tensor(t, t, a, ALU.mult).then_inc(steps, 1)
                    pool.wait_ge(steps, n + 4 * i + 3)
                    take(pool)
                    pool.tensor_scalar(t, t, -0.5, 1.5, ALU.mult, ALU.add).then_inc(steps, 1)
                    pool.wait_ge(steps, n + 4 * i + 4)
                    pool.tensor_tensor(y, y, t, ALU.mult).then_inc(ready if i == 2 else steps, 1)

            def norm_factors(g1):
                pool.wait_ge(st_ready, 4 * (g1 + 1))
                inverse_root(rr[:], va[:], rt[:], rr_step, STEPS_OF_ROOT * g1, rr_ready)

            def group(g, more):
                pool.wait_ge(h_ready, 2 * (g + 1))
                pool.wait_ge(res_used, g + 1)
                pool.tensor_tensor(h_res[:], h[:], v_bias[:, None, :].to_broadcast([SPAN, TILES, D]),
                                   ALU.add).then_inc(res_ready, 1)
                pool.wait_ge(xnT_copied, 2 * (g + 1))
                take(pool)
                pool.tensor_copy(xnT_rep[:], xnT[:].rearrange("p k (i o) n -> p (k i) o n", o=1)
                                 .to_broadcast([DH, 2 * G_IMG, VG, TOK])).then_inc(rep_ready, 1)
                for q in range(2):
                    pool.wait_ge(ring_emptied, 2 + 4 + 10 * g + QUADS * (q + 1))
                    pool.wait_ge(cat_ready, 2 * g + q + 1)
                    n = QUADS * G_IMG
                    v = qk_pad[:, q * n:(q + 1) * n, :]
                    pool.tensor_tensor(qk_sum[:, q * n:(q + 1) * n, :], v[:, :, 0:TOK], v[:, :, 2:PAD],
                                       ALU.add).then_inc(sums_ready, 1)
                if more > 0:
                    norm_factors(g + 1)
                pool.wait_ge(mv2_ready, g + 1)
                inverse_root(rs2[:], va2[:], rt2[:], rs2_step, STEPS_OF_ROOT * g, rs2_ready)
                if more > 1:
                    regroup(g + 2)

            pool.wait_ge(emb_a_ready, 1)
            inverse_root(emb_y[:], emb_a[:], emb_t[:], emb_y_step, 0, emb_y_ready)
            regroup(0)
            regroup(1)
            norm_factors(0)
            with pool.Fori(0, GROUPS - 2) as g:
                group(g, 2)
            group(GROUPS - 2, 1)
            group(GROUPS - 1, 0)

            pool.wait_ge(zeroed, 16 * 4)

            def scatter_x2(t, i, k):
                pool.wait_ge(slot_ready, t + 1)
                pool.wait_ge(x2t_again[i], 16 * k)
                take(pool)
                for e in range(TOPK):
                    pool.indirect_dma_start(wide_dram, bass.IndirectOffsetOnAxis(ap=slot_now[i][:, e:e + 1], axis=0),
                                            x2t[i][:], None).then_inc(scattered[i], 16)

            with pool.Fori(0, PAIRS) as p:
                for i in range(2):
                    scatter_x2(2 * p + i, i, p + 1)
                for i in range(2):
                    pool.wait_ge(scattered[i], 64 * (p + 1))
                    pool.sem_inc(scat_used, 1)
            scatter_x2(PAIRED, 0, PAIRS + 1)
            pool.wait_ge(scattered[0], 64 * (PAIRS + 1))
            pool.sem_inc(scat_used, 1)

            def stores(layer):
                dst = (mid_dram, wide_dram)[layer]
                width = (RANK, D)[layer]

                def store(n, i, k):
                    pool.wait_ge(y_copied[layer], 2 * n + 4)
                    rows = dst[bass.ds(n * (SB * ROWS), SB * ROWS), :]
                    pool.dma_start(rows.rearrange("(k p) d -> p k d", p=ROWS), os_[i][:, :, 0:width])\
                        .then_inc(y_stored[layer][i], 16)

                with pool.Fori(0, SUPERS // 2) as s:
                    for i in range(2):
                        store(2 * s + i, i, s)
                if SUPERS % 2:
                    store(SUPERS - 1, 0, SUPERS // 2)
                for i in range(2):
                    pool.wait_ge(y_stored[layer][i], 16 * ((SUPERS + 1 - i) // 2))

            stores(0)

            def gather(layer, t, i):
                src = (mid_dram, wide_dram)[layer]
                width = (RANK, D)[layer]
                pool.wait_ge(idx_ready[layer], t + 1)
                take(pool)
                for e in range(TOPK):
                    pool.indirect_dma_start(
                        gat[i][:, e, 0:width], None, src,
                        bass.IndirectOffsetOnAxis(ap=slot_get[i][:, layer * TOPK + e:layer * TOPK + e + 1], axis=0))\
                        .then_inc(gathered[layer][i], 16)

            def scatter_mid(t, i, k):
                pool.wait_ge(comb_ready[0], t + 1)
                take(pool)
                for e in range(TOPK):
                    pool.indirect_dma_start(
                        mid2_dram, bass.IndirectOffsetOnAxis(ap=slot_put[i][:, TOPK + e:TOPK + e + 1], axis=0),
                        comb[i][:, 0:RANK], None).then_inc(comb_out[0][i], 16)

            with pool.Fori(0, PAIRS) as p:
                for i in range(2):
                    gather(0, 2 * p + i, i)
                for i in range(2):
                    scatter_mid(2 * p + i, i, p + 1)
            gather(0, PAIRED, 0)
            scatter_mid(PAIRED, 0, PAIRS + 1)

            stores(1)

            with pool.Fori(0, PAIRS) as p:
                for i in range(2):
                    gather(1, 2 * p + i, i)
            gather(1, PAIRED, 0)
            for i in range(2):
                pool.wait_ge(gathered[1][i], 64 * (PAIRS + (1 - i)))

        @block.tensor
        def _(pe):
            pe.sem_inc(x2T_filled, 2)
            pe.sem_inc(hot_used, 2)
            for layer in range(2):
                pe.sem_inc(y_filled[layer], 2 * RING)

            fills = [0]

            def filled(ins):
                fills[0] += 1
                ins.then_inc(setup_ps, 1)

            def room():
                if fills[0] >= 4:
                    pe.wait_ge(setup_ev, fills[0] - 3)
                return bank[fills[0] % 4]

            pe.wait_ge(consts, 2)
            pe.wait_ge(w_loaded, 16 * 14)
            for kt in range(CH * HALVES):
                b = room()
                for c in range(2):
                    last = pe.transpose(b[:, c * DH:(c + 1) * DH], tok_nat[:, c, kt * 128:(kt + 1) * 128],
                                        ident[0:DH, 0:DH])
                filled(last)
            for c in range(6):
                b = room()
                for j in range(2):
                    last = pe.transpose(b[0:DH, j * DH:(j + 1) * DH], qkv_nat[:, c, j * DH:(j + 1) * DH],
                                        ident[0:DH, 0:DH])
                filled(last)
            b = room()
            for r in range(2):
                for j in range(2):
                    last = pe.transpose(b[0:DS, (2 * r + j) * DH:(2 * r + j + 1) * DH], wr_nat[:, r, j, :],
                                        ident[0:DH, 0:DH])
            filled(last)
            b = room()
            pe.wait_ge(embn_ready, 1)
            for r in range(2):
                last = pe.transpose(b[0:DS, r * 128:(r + 1) * 128], emb_nrm[:, r, :], ident[:])
            filled(last)
            b = room()
            pe.wait_ge(setup_ev, 14)
            for n in range(2 * QUADS):
                q, i = divmod(n, QUADS)
                heads = slice(q * HEADS + i * 4, q * HEADS + i * 4 + 4)
                for j in range(2):
                    pe.matmul(b[:, n:n + 1], w_qkT[:, j, heads].rearrange("p a b c -> p (a b c)"),
                              b_col[:, j:j + 1], start=j == 0, stop=False)
                last = pe.matmul(b[:, n:n + 1], qk_brow[0:1, heads].rearrange("p a b c -> p (a b c)"),
                                 ones[0:1, 0:1], start=False, stop=True)
            filled(last)
            b = room()
            for j in range(2):
                pe.matmul(b[0:SPAN, 0:D], b_col[:, j:j + 1].to_broadcast([DH, SPAN]), w_vT[:, j, :],
                          start=j == 0, stop=False)
            filled(pe.matmul(b[0:SPAN, 0:D], ones[0:1, 0:SPAN], v_brow[:], start=False, stop=True))
            b = room()
            for r in range(2):
                for j in range(2):
                    last = pe.matmul(b[0:DH, j * 256 + r * 128:j * 256 + (r + 1) * 128],
                                     wrT[:, r, j * DH:(j + 1) * DH], embT[:, r, :], start=True, stop=True)
            filled(last)
            b = room()
            for r in range(2):
                last = pe.matmul(b[:, r * 128:(r + 1) * 128], br_col[:, r:r + 1].to_broadcast([DS, 128]),
                                 embT[:, r, :], start=True, stop=True)
            filled(last)
            pe.wait_ge(setup_ev, 19)

            def to_pixels(g1, u0):
                for s in range(2):
                    pe.wait_ge(patches_ready, 2 * g1 + s + 1)
                    for half in range(HALVES):
                        u = 2 * s + half
                        pe.wait_ge(ring_emptied, u0 + u + 1)
                        cols = bank[u % 2][:, 0:HP * SUB].rearrange("p (k b c y v) -> p k v b c y", k=CH, b=4, c=CH, y=HP)
                        for w in range(HP):
                            last = pe.transpose(cols[:, w % CH, w // CH], patches[s][:, half, w, :], ident[0:SUB, 0:SUB])
                        last.then_inc(ring_filled, 1)

            def embed(g1, first):
                pe.wait_ge(ring_emptied, 10 * g1 + 4 + 2)
                for j in range(TILES):
                    f, t = divmod(j, 2)
                    if t == 0 and not first:
                        pe.wait_ge(v_masked, 4 * g1 - 1 + f)
                    for kt in range(CH * HALVES):
                        c, half = divmod(kt, HALVES)
                        last = pe.matmul(bank[2 + 3 * f][:, t * D:(t + 1) * D],
                                         pixT[:, half, c, 2 * j:2 * j + 2, :].rearrange("p a n -> p (a n)"),
                                         tok_wT[:, kt, :], start=kt == 0, stop=kt == CH * HALVES - 1)
                    if t == 1:
                        last.then_inc(patch_done, 1)

            def project(g):
                for j in range(TILES):
                    f, t = divmod(j, 2)
                    pe.wait_ge(xn_ready, TILES * g + j + 1)
                    for k in range(2):
                        last = pe.transpose(bank[2 + 3 * f][0:DH, k * 256 + t * 128:k * 256 + t * 128 + SPAN],
                                            xn[:, j, k * DH:(k + 1) * DH], ident[0:SPAN, 0:SPAN])
                    if t == 1:
                        last.then_inc(xn_transposed, 1)
                pe.wait_ge(xnT_copied, 2 * (g + 1))
                for n in range(2 * QUADS):
                    q, i = divmod(n, QUADS)
                    heads = slice(q * HEADS + i * 4, q * HEADS + i * 4 + 4)
                    pe.wait_ge(ring_emptied, 4 + 10 * g + n + 1)
                    for j in range(2):
                        last = pe.matmul(bank[n % 2][:, 0:G_IMG * TOK],
                                         w_qkT[:, j, heads].rearrange("p a b c -> p (a b c)"),
                                         xnT[:, j].rearrange("p i n -> p (i n)"), start=j == 0, stop=j == 1)
                    last.then_inc(ring_filled, 1)
                pe.wait_ge(rep_ready, g + 1)
                for m in range(G_IMG):
                    f, t = divmod(m, 2)
                    if t == 0 and f >= 2:
                        pe.wait_ge(v_masked, 4 * g + f - 1)
                    for j in range(2):
                        last = pe.matmul(bank[2 + 3 * (f % 2)][0:VG * TOK, t * D:(t + 1) * D],
                                         xnT_rep[:, j * G_IMG + m].rearrange("p r n -> p (r n)"),
                                         w_vT[:, j, :], start=j == 0, stop=j == 1)
                    if t == 1:
                        last.then_inc(v_filled, 1)

            def scores(g, j):
                if j == 0:
                    pe.wait_ge(quad_ready, g + 1)
                pe.wait_ge(scores_read, TILES * g + j + 1)
                b = bank[4 + 2 * (j % 2)]
                for a in range(2):
                    for i in range(QUADS):
                        w = HEADS_PER_QUAD * TOK
                        last = pe.matmul(b[64 * a:64 * a + TOK, i * w:(i + 1) * w], qk[:, i, 2 * j + a, :],
                                         k_quad[:, i * G_IMG + 2 * j + a].rearrange("p a b -> p (a b)"),
                                         start=True, stop=True)
                last.then_inc(scores_done, 1)

            def attend(g, j):
                pe.wait_ge(probs_ready, TILES * g + j + 1)
                pe.wait_ge(pT_copied, TILES * g + j + 1)
                for v in range(VGROUPS):
                    last = pe.transpose(bank[7][0:VG * TOK, v * SPAN:(v + 1) * SPAN],
                                        probs[:, j % 2, VG * v:VG * (v + 1), :].rearrange("p a b -> p (a b)"),
                                        ident[0:SPAN, 0:SPAN])
                last.then_inc(p_transposed, 1)
                pe.wait_ge(pT_copied, TILES * g + j + 2)
                pe.wait_ge(o_read, TILES * g + j + 1)
                if j == 0:
                    pe.wait_ge(v_masked, 4 * (g + 1))
                for a in range(2):
                    for v in range(VGROUPS):
                        last = pe.matmul(bank[3][64 * a:64 * a + TOK, 256 + v * VG * VW:256 + (v + 1) * VG * VW],
                                         probsT[:, j % 2, v, 64 * a:64 * a + TOK],
                                         vals[:, 2 * j + a, v].rearrange("p a b -> p (a b)"),
                                         start=True, stop=True)
                last.then_inc(pv_done, 1)

            def attention(g, more):
                project(g)
                if more:
                    to_pixels(g + 1, 4 + 10 * g + 6)
                    embed(g + 1, False)
                scores(g, 0)
                scores(g, 1)
                for j in range(TILES):
                    attend(g, j)
                    if j + 2 < TILES:
                        scores(g, j + 2)

            to_pixels(0, 0)
            embed(0, True)
            with pe.Fori(0, GROUPS - 1) as g:
                attention(g, True)
            attention(GROUPS - 1, False)

            pe.wait_ge(o_read, TILES * GROUPS + 1)
            pe.wait_ge(scores_read, TILES * GROUPS + 2)
            pe.matmul(bank[4][:, 0:256], zeros_bf[:, 0:128], zeros_bf[:], start=True, stop=False,
                      skip_group_check=True)

            def route_transpose(t, i, k):
                pe.wait_ge(x2t_loaded[i], 16 * k)
                pe.wait_ge(x2T_copied, t + 1)
                for j in range(2):
                    last = pe.transpose(bank[i][0:DH, j * ROWS:(j + 1) * ROWS], x2t[i][:, j * DH:(j + 1) * DH],
                                        ident[:])
                last.then_inc(x2T_filled, 1)

            def route_logits(t, i):
                pe.wait_ge(x2T_copied, t + 3)
                pe.wait_ge(logit_ready, t + 1)
                for j in range(2):
                    last = pe.matmul(bank[2 + i][:, 0:256], x2T[i][:, j, :], r_mat[:, j, :],
                                     start=j == 0, stop=j == 1)
                last.then_inc(logit_filled, 1)

            def route_rank(t, i):
                pe.wait_ge(hot_ready, t + 1)
                for e in range(TOPK):
                    last = pe.matmul(bank[4][:, 0:256], before[:], hot[i][:, :, e, :], start=False, stop=False,
                                     skip_group_check=True)
                last.then_inc(rank_filled, 1)
                pe.wait_ge(rank_copied, t + 1)
                for e in range(TOPK):
                    last = pe.matmul(bank[4][:, 0:256], after[:], hot[i][:, :, e, :], start=False, stop=False,
                                     skip_group_check=True)
                last.then_inc(hot_used, 1)

            with pe.Fori(0, PAIRS) as p:
                for i in range(2):
                    route_transpose(2 * p + i, i, p + 1)
                for i in range(2):
                    route_logits(2 * p + i, i)
                for i in range(2):
                    route_rank(2 * p + i, i)
            route_transpose(PAIRED, 0, PAIRS + 1)
            route_logits(PAIRED, 0)
            route_rank(PAIRED, 0)

            pe.wait_ge(plan_ev, 1)
            for r in range(2):
                last = pe.matmul(bank[5][:, r:r + 1], upto[:], nblk[:, r:r + 1], start=True, stop=True)
            last.then_inc(plan_ps, 1)
            pe.wait_ge(plan_ev, 2)
            for r in range(2):
                last = pe.matmul(bank[6][:, r * 128:(r + 1) * 128], ones[:], diag[:, r, :], start=True, stop=True)
            last.then_inc(plan_ps, 1)
            pe.wait_ge(plan_ev, 3)
            for r in range(2):
                last = pe.matmul(bank[7][0:1, r * BLOCKS:(r + 1) * BLOCKS], ones_bf[:], passed[:, r, :],
                                 start=True, stop=True)
            last.then_inc(plan_ps, 1)
            pe.wait_ge(plan_ev, 4)

            def experts(layer):
                parts = (2, 1)[layer]
                kp = (DH, RANK)[layer]
                width = (RANK, D)[layer]
                filled_ = t_filled[layer]
                with pe.Fori(0, STEPS) as s:
                    def transposed(n):
                        r, k = divmod(n, SB)
                        if k == 0:
                            pe.wait_ge(xs_loaded[layer][r], 16 * (s + 1))
                        pe.wait_ge(t_copied[layer], s * BODY + n + 1)
                        for j in range(parts):
                            src = xs[r][:, k, j:D:2] if layer == 0 else xs[r][:, k, 0:RANK]
                            last = pe.transpose(bank[n % 2][0:kp, j * ROWS:(j + 1) * ROWS], src, ident[:])
                        last.then_inc(filled_, 1)

                    transposed(0)
                    for n in range(BODY):
                        r, k = divmod(n, SB)
                        if n + 1 < BODY:
                            transposed(n + 1)
                        if k == 0:
                            pe.wait_ge(fw_loaded[layer][r], 16 * SB * (s + 1))
                        if k % 2 == 0:
                            pe.wait_ge(y_copied[layer], s * (BODY // 2) + n // 2 + 1)
                        pe.wait_ge(t_copied[layer], s * BODY + n + 3)
                        dst = bank[2 + (n // 2) % 2][:, (k % 2) * 256:(k % 2) * 256 + width]
                        for j in range(parts):
                            w = fw[r][0:kp, k, j * 128:(j + 1) * 128] if layer == 0 else fw[r][:, k, 0:D]
                            last = pe.matmul(dst, xsT[n % 2][0:kp, j * ROWS:(j + 1) * ROWS], w,
                                             start=j == 0, stop=j == parts - 1)
                        if k % 2 == 1:
                            last.then_inc(y_filled[layer], 1)

            experts(0)
            experts(1)

        @block.scalar
        def _(act):
            act.sem_inc(ring_emptied, 2)
            act.sem_inc(pT_copied, 1)
            act.sem_inc(x2T_copied, 2)
            act.sem_inc(exp_done, 2)
            for layer in range(2):
                act.sem_inc(t_copied[layer], 2)
            act.wait_ge(consts, 2)

            def pixels(g1, u0):
                for u in range(4):
                    s, half = divmod(u, 2)
                    act.wait_ge(ring_filled, u0 + u + 1)
                    if u == 0:
                        act.wait_ge(patch_done, 2 * g1)
                    src = bank[u % 2][:, 0:HP * SUB].rearrange("p (k b n) -> p k b n", k=CH, b=4)
                    dst = pixT[:, half, :, s * 4:(s + 1) * 4, 1:TOK]
                    act.activation(dst, src, ACT.Copy).then_inc(ring_emptied, 1)

            def projections(g):
                for f in range(2):
                    act.wait_ge(xn_transposed, 2 * g + f + 1)
                    src = bank[2 + 3 * f][0:DH, :].rearrange("p (k a n) -> p k a n", k=2, a=4)[:, :, :, 0:TOK]
                    act.activation(xnT[:, :, 4 * f:4 * f + 4, :], src, ACT.Copy).then_inc(xnT_copied, 1)
                for n in range(2 * QUADS):
                    q = n // QUADS
                    act.wait_ge(ring_filled, 4 + 10 * g + n + 1)
                    if n % QUADS == 0:
                        act.wait_ge(cat_ready, 2 * g + q + 1)
                    act.activation(qk_pad[:, n * G_IMG:(n + 1) * G_IMG, 1:1 + TOK],
                                   bank[n % 2][:, 0:G_IMG * TOK].rearrange("p (i n) -> p i n", n=TOK),
                                   ACT.Identity, bias=qk_bias[:, n:n + 1], scale=qk_scale[:, q:q + 1])\
                       .then_inc(ring_emptied, 1)

            def quads(g):
                act.wait_ge(cat_ready, 2 * g + 4)
                for hh in range(HEADS_PER_QUAD):
                    rows = slice(32 * hh, 32 * hh + 32)
                    last = act.activation(k_quad[rows, :, hh, :],
                                          qk[rows, QUADS:].rearrange("p i m n -> p (i m) n"), ACT.Copy)
                last.then_inc(quad_ready, 1)

            def exps(g, j):
                act.wait_ge(scores_read, TILES * g + j + 3)
                p = probs[:, j % 2].rearrange("p a b -> p (a b)")
                act.activation(p, p, ACT.Exp).then_inc(probs_ready, 1)

            def copy_pT(g, j):
                act.wait_ge(p_transposed, TILES * g + j + 1)
                act.activation(probsT[:, j % 2].rearrange("p a b -> p (a b)"), bank[7][0:VG * TOK, 0:VGROUPS * SPAN],
                               ACT.Copy).then_inc(pT_copied, 1)

            def attention(g, more):
                projections(g)
                if more:
                    pixels(g + 1, 4 + 10 * g + 6)
                quads(g)
                exps(g, 0)
                exps(g, 1)
                for j in range(TILES):
                    copy_pT(g, j)
                    if j + 2 < TILES:
                        exps(g, j + 2)

            act.wait_ge(setup_ev, 19)
            pixels(0, 0)
            with act.Fori(0, GROUPS - 1) as g:
                attention(g, True)
            attention(GROUPS - 1, False)

            def route_T(t, i):
                act.wait_ge(x2T_filled, t + 3)
                act.activation(x2T[i][:].rearrange("p j n -> p (j n)"), bank[i][0:DH, 0:2 * ROWS], ACT.Copy)\
                   .then_inc(x2T_copied, 1)

            def route_exp(t, i):
                act.wait_ge(nmax_ready, t + 1)
                for r in range(2):
                    act.activation(escr[i][:, r, :], logit[i][:, r, :], ACT.Exp, bias=nmax[i][:, r:r + 1],
                                   accum_out=zsum[i][:, r:r + 1])
                    last = act.activation(etop[i][:, r, :], top8[i][:, r, 0:TOPK], ACT.Exp,
                                          bias=nmax[i][:, r:r + 1])
                last.then_inc(exp_done, 1)

            def route_rank(t, i):
                act.wait_ge(rank_filled, t + 1)
                act.activation(rank[:, bass.ds(t, 1), :].rearrange("p a b -> p (a b)"), bank[4][:, 0:256],
                               ACT.Copy).then_inc(rank_copied, 1)

            with act.Fori(0, PAIRS) as p:
                for i in range(2):
                    route_T(2 * p + i, i)
                for i in range(2):
                    route_exp(2 * p + i, i)
                for i in range(2):
                    route_rank(2 * p + i, i)
            route_T(PAIRED, 0)
            route_exp(PAIRED, 0)
            route_rank(PAIRED, 0)

            def experts(layer):
                cols = (256, 128)[layer]
                kp = (DH, RANK)[layer]
                with act.Fori(0, STEPS) as s:
                    for n in range(BODY):
                        act.wait_ge(t_filled[layer], s * BODY + n + 1)
                        act.activation(xsT[n % 2][0:kp, 0:cols], bank[n % 2][0:kp, 0:cols], ACT.Copy)\
                           .then_inc(t_copied[layer], 1)

            experts(0)
            experts(1)

        @block.vector
        def _(dve):
            step = [0]

            def link(ins):
                step[0] += 1
                ins.then_inc(dve_step, 1)
                dve.wait_ge(dve_step, step[0])

            dve.sem_inc(cat_ready, 2)
            dve.sem_inc(scores_read, 2)
            dve.sem_inc(o_read, 1)
            dve.sem_inc(res_used, 1)
            dve.sem_inc(logit_ready, 2)
            for layer in range(2):
                dve.sem_inc(y_copied[layer], 2)

            dve.wait_ge(consts, 2)
            dve.wait_ge(w_loaded, 16 * 14)
            link(dve.tensor_tensor(emb_sq[:], emb[:], emb[:], ALU.mult))
            link(dve.tensor_reduce(emb_n2[:], emb_sq[:], axis=AX.X, op=ALU.add))
            link(dve.tensor_scalar(emb_a[:], emb_n2[:], 1e-30, None, ALU.max))
            dve.tensor_scalar(emb_y[:].bitcast(I32), emb_a[:].bitcast(I32), 1, -1, ALU.logical_shift_right,
                              ALU.bitwise_xor).then_inc(emb_a_ready, 1)
            dve.wait_ge(emb_y_ready, 1)
            link(dve.tensor_tensor(emb_n1[:], emb_n2[:], emb_y[:], ALU.mult))
            link(dve.tensor_scalar(emb_n1[:], emb_n1[:], 1e-8, None, ALU.add))
            link(dve.reciprocal(emb_inv[:], emb_n1[:]))
            dve.tensor_tensor(emb_nrm[:], emb[:], emb_inv[:, :, None].to_broadcast([128, 2, DS]), ALU.mult)\
               .then_inc(embn_ready, 1)
            link(dve.tensor_scalar(part_b[:], part_i[:], 4, 1, ALU.logical_shift_right, ALU.bitwise_and))
            link(dve.tensor_copy(neigh[:], part_b[:]))
            link(dve.tensor_scalar(tmp_col[:], neigh[:], 0.0, SCALE * (1 + BETA), ALU.is_equal, ALU.mult))
            link(dve.scalar_tensor_tensor(qk_scale[:, 0:1], neigh[:], -SCALE * BETA, tmp_col[:], ALU.mult, ALU.add))
            link(dve.memset(qk_scale[:, 1:2], 1.0))

            fills = [0]

            def got():
                fills[0] += 1
                dve.wait_ge(setup_ps, fills[0])
                return bank[(fills[0] - 1) % 4]

            for kt in range(CH * HALVES):
                b = got()
                dve.tensor_copy(tok_wT[:, kt, :], b[:, 0:D]).then_inc(setup_ev, 1)
            for c in range(6):
                b = got()
                for j in range(2):
                    if c < 4:
                        src = b[0:DH, j * DH:(j + 1) * DH].rearrange("p (n o k) -> p n o k", o=1, k=HD)
                        last = dve.tensor_copy(w_qkT[:, j, c * 6:(c + 1) * 6], src.to_broadcast([DH, 6, 2, HD]))
                    else:
                        last = dve.tensor_copy(w_vT[:, j, (c - 4) * DH:(c - 3) * DH], b[0:DH, j * DH:(j + 1) * DH])
                last.then_inc(setup_ev, 1)
            b = got()
            dve.tensor_copy(wrT[:].rearrange("p r d -> p (r d)"), b[0:DS, 0:2 * D]).then_inc(setup_ev, 1)
            b = got()
            dve.tensor_copy(embT[:].rearrange("p r d -> p (r d)"), b[0:DS, 0:256]).then_inc(setup_ev, 1)
            b = got()
            for q in range(2):
                n = slice(q * QUADS, (q + 1) * QUADS)
                last = dve.tensor_scalar(qk_bias[:, n], b[:, n], qk_scale[:, q:q + 1], None, ALU.mult)
            last.then_inc(setup_ev, 1)
            b = got()
            dve.tensor_copy(v_bias[:], b[0:SPAN, 0:D]).then_inc(setup_ev, 1)
            b = got()
            dve.tensor_copy(r_mat[:].rearrange("p j n -> p (j n)"), b[0:DH, 0:512]).then_inc(setup_ev, 1)
            b = got()
            dve.tensor_copy(r_bias[:], b[:, 0:256]).then_inc(setup_ev, 1)
            dve.wait_ge(setup_ev, 18)
            for j in range(2):
                dve.tensor_scalar(w_qkT[:, j].rearrange("p a b c -> p (a b c)"),
                                  w_qkT[:, j].rearrange("p a b c -> p (a b c)"), g_col[:, j:j + 1], None, ALU.mult)
                dve.tensor_scalar(w_vT[:, j, :], w_vT[:, j, :], g_col[:, j:j + 1], None, ALU.mult)
            for m in range(G_IMG):
                dve.tensor_copy(vals[:, m, :, :, HD:VW],
                                head_mask[:, None, :, HD:VW].to_broadcast([VG * TOK, VGROUPS, VG, 1]))
            for b, v in ((bank[3], 1.0), (bank[4], 0.0), (bank[6], 0.0)):
                last = dve.memset(b[:], v)
            last.then_inc(setup_ev, 1)
            dve.wait_ge(cls_loaded, 32)
            dve.wait_ge(setup_ev, 19)

            def norm(g1):
                for f in range(2):
                    dve.wait_ge(patch_done, 2 * g1 + f + 1)
                    if f == 0:
                        dve.wait_ge(res_ready, g1)
                    dve.tensor_tensor(h[:, 2 * f:2 * f + 2, :],
                                      bank[2 + 3 * f][0:SPAN, 0:2 * D].rearrange("p (t d) -> p t d", t=2),
                                      tok_bias[:, None, :].to_broadcast([SPAN, 2, D]), ALU.add).then_inc(h_ready, 1)
                for j in range(TILES):
                    dve.wait_ge(h_ready, 2 * g1 + j // 2 + 1)
                    take(dve)
                    last = dve.bn_stats(st[:, j, :], h[:, j, :])
                last.then_inc(st_ready, 1)
                dve.wait_ge(st_ready, 4 * g1 + 1)
                take(dve)
                for j in range(TILES):
                    last = dve.bn_aggr(mv[:, j, :], st[:, j, :])
                last.then_inc(st_ready, 1)
                dve.wait_ge(st_ready, 4 * g1 + 2)
                dve.tensor_scalar(va[:], mv[:, :, 1], 1 + LN_EPS, LN_EPS * LN_EPS, ALU.mult, ALU.add).then_inc(st_ready, 1)
                dve.wait_ge(st_ready, 4 * g1 + 3)
                dve.tensor_scalar(rr[:].bitcast(I32), va[:].bitcast(I32), 1, -1, ALU.logical_shift_right,
                                  ALU.bitwise_xor).then_inc(st_ready, 1)
                dve.wait_ge(rr_ready, g1 + 1)
                for j in range(TILES):
                    if j == 0:
                        dve.wait_ge(xn_transposed, 2 * g1)
                    dve.tensor_scalar(xn[:, j, :], h[:, j, :], mv[:, j, 0:1], rr[:, j:j + 1],
                                      ALU.subtract, ALU.mult).then_inc(xn_ready, 1)

            def values(g):
                mask = head_mask[:, None, :, 0:HD].to_broadcast([VG * TOK, 2 * VGROUPS, VG, HD])
                for f in range(G_IMG // 2):
                    dve.wait_ge(v_filled, 4 * g + f + 1)
                    src = bank[2 + 3 * (f % 2)][0:VG * TOK, 0:2 * D]
                    dve.tensor_tensor(vals[:, 2 * f:2 * f + 2].rearrange("p m a b c -> p (m a) b c")[:, :, :, 0:HD],
                                      src.rearrange("p (a b c) -> p a b c", b=VG, c=HD), mask, ALU.mult)\
                       .then_inc(v_masked, 1)

            def cat(g):
                n = QUADS * G_IMG
                for q in range(2):
                    dve.wait_ge(sums_ready, 2 * g + q + 1)
                    dve.scalar_tensor_tensor(
                        qk[:, q * QUADS:(q + 1) * QUADS].rearrange("p a b c -> p (a b) c"),
                        qk_sum[:, q * n:(q + 1) * n, :], neigh[:, 0:1], qk_pad[:, q * n:(q + 1) * n, 1:1 + TOK],
                        ALU.mult, ALU.add).then_inc(cat_ready, 1)

            def softmax_in(g, j):
                b = bank[4 + 2 * (j % 2)]
                dve.wait_ge(scores_done, TILES * g + j + 1)
                s = b[0:SPAN, 0:HEADS * TOK].rearrange("p (a b) -> p a b", b=TOK)
                dve.tensor_reduce(smax[:, j % 2, :], s, axis=AX.X, op=ALU.max).then_inc(smax_ready, 1)
                dve.wait_ge(smax_ready, TILES * g + j + 1)
                if j == 0:
                    dve.wait_ge(p_transposed, TILES * g)
                elif j >= 2:
                    dve.wait_ge(p_transposed, TILES * g + j - 1)
                dve.tensor_tensor(probs[:, j % 2], s, smax[:, j % 2, :, None].to_broadcast([SPAN, HEADS, TOK]),
                                  ALU.subtract).then_inc(scores_read, 1)

            def finish(g, j):
                dve.wait_ge(pv_done, TILES * g + j + 1)
                o = bank[3][0:SPAN, 256:256 + HEADS * VW].rearrange("p (a b) -> p a b", b=VW)
                dve.reciprocal(rsum[:], o[:, :, HD]).then_inc(fin_step, 1)
                dve.wait_ge(fin_step, 2 * (TILES * g + j) + 1)
                dve.tensor_tensor(att[:], o[:, :, 0:HD], rsum[:, :, None].to_broadcast([SPAN, HEADS, HD]),
                                  ALU.mult).then_inc(o_read, 1)
                dve.wait_ge(o_read, TILES * g + j + 2)
                if j == 0:
                    dve.wait_ge(res_ready, g + 1)
                    dve.wait_ge(stored, 64 * g)
                dve.tensor_tensor(h2[:, j, :], att[:].rearrange("p a b -> p (a b)"), h_res[:, j, :], ALU.add)\
                   .then_inc(h2_ready, 1)
                dve.wait_ge(h2_ready, TILES * g + j + 1)
                dve.bn_stats(st2[:, j, :], h2[:, j, :]).then_inc(fin_step, 1)

            def norm2(g):
                dve.wait_ge(fin_step, 2 * TILES * (g + 1))
                take(dve)
                for j in range(TILES):
                    last = dve.bn_aggr(mv2[:, j, :], st2[:, j, :])
                last.then_inc(nrm_step, 1)
                dve.sem_inc(res_used, 1)
                dve.wait_ge(nrm_step, 2 * g + 1)
                dve.tensor_scalar(va2[:], mv2[:, :, 1], LN_EPS, None, ALU.add).then_inc(nrm_step, 1)
                dve.wait_ge(nrm_step, 2 * g + 2)
                dve.tensor_scalar(rs2[:].bitcast(I32), va2[:].bitcast(I32), 1, -1, ALU.logical_shift_right,
                                  ALU.bitwise_xor).then_inc(mv2_ready, 1)
                dve.wait_ge(rs2_ready, g + 1)
                for j in range(TILES):
                    dve.tensor_scalar(x2[:, j, :], h2[:, j, :], mv2[:, j, 0:1], rs2[:, j:j + 1],
                                      ALU.subtract, ALU.mult).then_inc(x2_ready, 1)

            def attention(g, more):
                values(g)
                cat(g)
                if more:
                    norm(g + 1)
                softmax_in(g, 0)
                softmax_in(g, 1)
                for j in range(TILES):
                    finish(g, j)
                    if j + 2 < TILES:
                        softmax_in(g, j + 2)
                norm2(g)

            norm(0)
            with dve.Fori(0, GROUPS - 1) as g:
                attention(g, True)
            attention(GROUPS - 1, False)

            def route_top(t, i):
                dve.wait_ge(logit_filled, t + 1)
                dve.wait_ge(exp_done, t + 1)
                dve.tensor_tensor(logit[i][:].rearrange("p r n -> p (r n)"), bank[2 + i][:, 0:256], r_bias[:],
                                  ALU.add).then_inc(logit_ready, 1)
                dve.wait_ge(logit_ready, t + 3)
                take(dve)
                for r in range(2):
                    last = dve.max(top8[i][:, r, :], logit[i][:, r, :])
                last.then_inc(top_ready, 1)
                dve.wait_ge(top_ready, 3 * t + 1)
                dve.tensor_scalar(nmax[i][:], top8[i][:, :, 0], -1.0, None, ALU.mult).then_inc(nmax_ready, 1)
                for r in range(2):
                    last = dve.max_index(idx8[i][:, r, :], top8[i][:, r, :], logit[i][:, r, :])
                last.then_inc(top_ready, 1)
                dve.wait_ge(top_ready, 3 * t + 2)
                dve.tensor_copy(idxf[:, bass.ds(t, 1)].rearrange("p t r k -> p (t r) k"), idx8[i][:, :, 0:TOPK])\
                   .then_inc(top_ready, 1)
                dve.wait_ge(top_ready, 3 * t + 3)
                dve.wait_ge(hot_used, t + 1)
                dve.tensor_tensor(
                    hot[i][:].rearrange("p r k n -> p (r k) n"),
                    iota_n[:, None, :].to_broadcast([ROWS, 2 * TOPK, EXPERTS]),
                    idxf[:, bass.ds(t, 1)].rearrange("p t r k -> p (t r k)")[:, :, None].to_broadcast([ROWS, 2 * TOPK, EXPERTS]),
                    ALU.is_equal).then_inc(hot_ready, 1)

            def route_weights(t, i):
                dve.wait_ge(exp_done, t + 3)
                dve.tensor_reduce(s4[i][:], etop[i][:], axis=AX.X, op=ALU.add).then_inc(wt_step, 1)
                dve.wait_ge(wt_step, 4 * t + 1)
                dve.scalar_tensor_tensor(den[i][:], zsum[i][:], 1e-8, s4[i][:], ALU.mult, ALU.add).then_inc(wt_step, 1)
                dve.wait_ge(wt_step, 4 * t + 2)
                dve.reciprocal(iden[i][:], den[i][:]).then_inc(wt_step, 1)
                dve.wait_ge(wt_step, 4 * t + 3)
                dve.tensor_tensor(wts[:, bass.ds(t, 1)].rearrange("p t r k -> p (t r) k"), etop[i][:],
                                  iden[i][:, :, None].to_broadcast([ROWS, 2, TOPK]), ALU.mult).then_inc(wt_step, 1)

            with dve.Fori(0, PAIRS) as p:
                for i in range(2):
                    route_top(2 * p + i, i)
                for i in range(2):
                    route_weights(2 * p + i, i)
            route_top(PAIRED, 0)
            route_weights(PAIRED, 0)

            dve.wait_ge(hot_used, TTILES + 2)
            cnt = bank[4][:, 0:256].rearrange("p (r n) -> p r n", r=2)
            link(dve.tensor_tensor(diag[:], cnt, ident[:, None, :].to_broadcast([128, 2, 128]), ALU.mult))
            link(dve.tensor_reduce(cum[:], diag[:], axis=AX.X, op=ALU.add))
            link(dve.tensor_scalar(cnt_i[:], cum[:], float(ROWS - 1), None, ALU.add))
            link(dve.tensor_scalar(nblk_i[:], cnt_i[:], 7, None, ALU.logical_shift_right))
            dve.tensor_copy(nblk[:], nblk_i[:]).then_inc(plan_ev, 1)
            dve.wait_ge(plan_ev, 1)
            dve.wait_ge(plan_ps, 1)
            link(dve.tensor_copy(cum[:], bank[5][:, 0:2]))
            link(dve.tensor_tensor(base_c[:], cum[:], nblk[:], ALU.subtract))
            link(dve.tensor_scalar(base_c[:], base_c[:], float(ROWS), None, ALU.mult))
            for r in range(2):
                last = dve.tensor_scalar(diag[:, r, :], ident[:], base_c[:, r:r + 1], None, ALU.mult)
            last.then_inc(plan_ev, 1)
            for r in range(2):
                last = dve.tensor_scalar(passed[:, r, :], iota_blk[:], cum[:, r:r + 1], None, ALU.is_ge)
            last.then_inc(plan_ev, 1)
            dve.wait_ge(plan_ps, 2)
            link(dve.tensor_copy(base_b[:], bank[6][:, 0:256]))
            dve.wait_ge(plan_ps, 3)
            dve.tensor_scalar(owner[:].rearrange("p r b -> p (r b)"), bank[7][0:1, 0:2 * BLOCKS],
                              float(EXPERTS - 1), None, ALU.min).then_inc(plan_ev, 1)

            def slot(t, i):
                dve.tensor_tensor(srank[i][:], rank[:, bass.ds(t, 1), :].rearrange("p a b -> p (a b)"), base_b[:],
                                  ALU.add).then_inc(slot_step, 1)
                dve.wait_ge(slot_step, 3 * t + 1)
                for e in range(2 * TOPK):
                    r = e // TOPK
                    last = dve.scalar_tensor_tensor(
                        pick[:, e, :], iota_n[:],
                        idxf[:, bass.ds(t, 1)].rearrange("p t r k -> p (t r k)")[:, e:e + 1],
                        srank[i][:, r * EXPERTS:(r + 1) * EXPERTS], ALU.is_equal, ALU.mult,
                        accum_out=slotf[i][:, e:e + 1])
                last.then_inc(slot_step, 1)
                dve.wait_ge(slot_step, 3 * t + 2)
                dve.tensor_copy(slots[:, bass.ds(t, 1), :].rearrange("p a b -> p (a b)"), slotf[i][:]).then_inc(slot_step, 1)
                dve.wait_ge(slot_step, 3 * t + 3)
                dve.wait_ge(scat_used, t + 1)
                dve.tensor_copy(slot_now[i][:], slotf[i][:]).then_inc(slot_ready, 1)

            with dve.Fori(0, PAIRS) as p:
                for i in range(2):
                    slot(2 * p + i, i)
            slot(PAIRED, 0)

            def experts(layer):
                width = (RANK, D)[layer]

                def copy_super(n, o, k):
                    for q in range(2):
                        dve.wait_ge(y_filled[layer], 2 * n + q + 1 + 2 * RING)
                        if q == 0:
                            dve.wait_ge(y_stored[layer][o], k)
                        b = bank[2 + q]
                        src = b[:].rearrange("p (k w) -> p k w", k=2)[:, :, 0:width]
                        last = dve.tensor_copy(os_[o][:, 2 * q:2 * q + 2, 0:width], src)
                        last.then_inc(y_copied[layer], 1)

                with dve.Fori(0, SUPERS // 2) as s:
                    for o in range(2):
                        copy_super(2 * s + o, o, 16 * s)
                if SUPERS % 2:
                    copy_super(SUPERS - 1, 0, 16 * (SUPERS // 2))

            def combine(layer, t, i, k):
                width = (RANK, D)[layer]
                dve.wait_ge(gathered[layer][i], 64 * k)
                w = wts[:, bass.ds(t, 1)].rearrange("p t r k -> p (t r k)")
                if layer == 1:
                    dve.wait_ge(h2t_loaded[i], 16 * k)
                for e in range(TOPK):
                    we = w[:, layer * TOPK + e:layer * TOPK + e + 1]
                    g = gat[i][:, e, 0:width]
                    if e == 0 and layer == 0:
                        ins = dve.tensor_scalar(acc[i][:, 0, 0:width], g, we, None, ALU.mult)
                    else:
                        prev = h2t[i][:, 0:width] if e == 0 else acc[i][:, (e - 1) % 2, 0:width]
                        dst = comb[i][:, 0:width] if e == TOPK - 1 else acc[i][:, e % 2, 0:width]
                        if e == TOPK - 1:
                            dve.wait_ge(comb_out[layer][i], (64 if layer == 0 else 16) * (k - 1))
                            if layer == 0:
                                dve.tensor_copy(slot_put[i][:], slots[:, bass.ds(t, 1), :].rearrange("p a b -> p (a b)"))
                        ins = dve.scalar_tensor_tensor(dst, g, we, prev, ALU.mult, ALU.add)
                    if e < TOPK - 1:
                        ins.then_inc(comb_step[layer], 1)
                        dve.wait_ge(comb_step[layer], (TOPK - 1) * t + e + 1)
                    else:
                        ins.then_inc(comb_ready[layer], 1)

            def indices(layer, t, i):
                dve.tensor_copy(slot_get[i][:], slots[:, bass.ds(t, 1), :].rearrange("p a b -> p (a b)"))\
                   .then_inc(idx_ready[layer], 1)

            def tiles(layer):
                for i in range(2):
                    indices(layer, i, i)
                with dve.Fori(0, PAIRS - 1) as p:
                    for i in range(2):
                        combine(layer, 2 * p + i, i, p + 1)
                        indices(layer, 2 * p + 2 + i, i)
                combine(layer, PAIRED - 2, 0, PAIRS)
                indices(layer, PAIRED, 0)
                combine(layer, PAIRED - 1, 1, PAIRS)
                combine(layer, PAIRED, 0, PAIRS + 1)

            experts(0)
            tiles(0)
            experts(1)
            tiles(1)


_INS = ['x', 'cls_tok', 'L0_tok_W', 'L0_tok_b', 'L0_attn_qkv_w', 'L0_attn_qkv_b', 'L0_attn_ln_g', 'L0_attn_ln_b',
        'L0_ffn_f_know', 'L0_ffn_r_know', 'L0_ffn_W_fk', 'L0_ffn_b_fk', 'L0_ffn_W_rk', 'L0_ffn_b_rk',
        'L0_ffn_emb_fk', 'L0_ffn_emb_rk']


def kernel(**inputs):
    import concourse.bacc as bacc
    from concourse.bass_utils import run_bass_kernel_spmd

    nc = bacc.Bacc("TRN2", target_bir_lowering=False, num_devices=1)
    arrays, args = {}, []
    for name in _INS:
        a = np.ascontiguousarray(inputs[name])
        arrays[f"in_{name}"] = a
        args.append(nc.dram_tensor(f"in_{name}", a.shape, mybir.dt.from_np(a.dtype), kind="ExternalInput").ap())
    res = nc.dram_tensor("out_0", (TOKENS, D), F32, kind="ExternalOutput").ap()
    tower(nc, *args, res)
    r = run_bass_kernel_spmd(nc, [arrays], core_ids=[0])
    return r.results[0]["out_0"].reshape(BATCH, TOK, D)
```

```python
import numpy as np
import concourse.bass as bass
from concourse import mybir
from contextlib import ExitStack

F32 = mybir.dt.float32
BF16 = mybir.dt.bfloat16
I32 = mybir.dt.int32
U32 = mybir.dt.uint32
ALU = mybir.AluOpType
ACT = mybir.ActivationFunctionType
AX = mybir.AxisListType

BATCH, CH, IMG, PATCH = 64, 3, 96, 16
HP = IMG // PATCH
TOK = HP * HP + 1
D = 192
DH = D // 2
HEADS, HD = 12, 16
HEADS_PER_QUAD = 4
QUADS = HEADS // HEADS_PER_QUAD
HALVES = 2
LN_EPS = 1e-5
BETA = 0.2
SCALE = HD ** -0.5

G_IMG = 8
GROUPS = BATCH // G_IMG
TILES = G_IMG // 2
SPAN = 64 + TOK
PAD = TOK + 2
SUB = G_IMG // 2 * CH * HP
LINE = PATCH * IMG
VG = 3
VGROUPS = HEADS // VG
VW = HD + 1

EXPERTS, RANK, DS, TOPK = 128, 128, 64, 4
TOKENS = BATCH * TOK
ROWS = 128
TTILES = -(-TOKENS // ROWS)
PTOK = TTILES * ROWS
LAST = TOKENS - (TTILES - 1) * ROWS
PAIRS = TTILES // 2
MAX_BLOCKS = (PTOK * TOPK + EXPERTS * (ROWS - 1)) // ROWS
SB = 4
RING = 3
BODY = SB * RING
STEPS = -(-MAX_BLOCKS // BODY)
BLOCKS = STEPS * BODY
SLOTS = BLOCKS * ROWS


def tower(nc, x, cls_tok, tok_w, tok_b, qkv_w, qkv_b, ln_g, ln_b,
          f_know, r_know, w_fk, b_fk, w_rk, b_rk, emb_fk, emb_rk, out):
    ctx = ExitStack()
    with ctx:
        phase = [ctx]

        def sb(name, shape, dt=F32):
            return phase[0].enter_context(nc.sbuf_tensor(name, shape, dt))

        def sem(name):
            return ctx.enter_context(nc.semaphore(name))

        bank = [ctx.enter_context(nc.psum_tensor(f"bank{i}", [128, 512], F32)) for i in range(8)]

        h2_dram = nc.dram_tensor("h2_dram", [PTOK, D], F32, kind="Internal").ap()
        wide_dram = nc.dram_tensor("wide_dram", [SLOTS, D], F32, kind="Internal").ap()
        mid_dram = nc.dram_tensor("mid_dram", [SLOTS, RANK], F32, kind="Internal").ap()

        ident = sb("ident", [128, 128])
        ones = sb("ones", [128, 128])
        before = sb("before", [128, 128], BF16)
        after = sb("after", [128, 128], BF16)
        upto = sb("upto", [128, 128], BF16)
        ones_bf = sb("ones_bf", [128, 1], BF16)
        zeros_bf = sb("zeros_bf", [128, 256], BF16)
        head_mask = sb("head_mask", [VG * TOK, VG, VW])
        iota_n = sb("iota_n", [128, EXPERTS])
        iota_blk = sb("iota_blk", [128, BLOCKS])
        ZW = 1632
        magic = sb("magic", [128, TTILES], I32)
        zeros = sb("zeros", [128, ZW])
        part_i = sb("part_i", [128, 1], I32)
        part_b = sb("part_b", [128, 1], I32)
        neigh = sb("neigh", [128, 1])
        qk_scale = sb("qk_scale", [128, 2])
        tmp_col = sb("tmp_col", [128, 1])

        tok_nat = sb("tok_nat", [DH, 2, CH * PATCH * PATCH])
        tok_wT = sb("tok_wT", [128, CH * HALVES, D])
        tok_bias = sb("tok_bias", [SPAN, D])
        qkv_nat = sb("qkv_nat", [DH, 6, D])
        w_qkT = sb("w_qkT", [DH, 2, 2 * HEADS, 2, HD])
        w_vT = sb("w_vT", [DH, 2, D])
        g_col = sb("g_col", [DH, 2])
        b_col = sb("b_col", [DH, 2])
        qk_brow = sb("qk_brow", [1, 2 * HEADS, 2, HD])
        v_brow = sb("v_brow", [1, D])
        qk_bias = sb("qk_bias", [128, 2 * QUADS])
        v_bias = sb("v_bias", [SPAN, D])
        emb = sb("emb", [128, 2, DS])
        emb_sq = sb("emb_sq", [128, 2, DS])
        emb_n2 = sb("emb_n2", [128, 2])
        emb_a = sb("emb_a", [128, 2])
        emb_y = sb("emb_y", [128, 2])
        emb_t = sb("emb_t", [128, 2])
        emb_n1 = sb("emb_n1", [128, 2])
        emb_inv = sb("emb_inv", [128, 2])
        emb_nrm = sb("emb_nrm", [128, 2, DS])
        embT = sb("embT", [DS, 2, EXPERTS])
        wr_nat = sb("wr_nat", [DH, 2, 2, DS])
        wrT = sb("wrT", [DS, 2, D])
        br_col = sb("br_col", [DS, 2])
        r_mat = sb("r_mat", [DH, 2, 2 * EXPERTS])
        r_bias = sb("r_bias", [128, 2 * EXPERTS])

        h2r = sb("h2r", [ROWS, TTILES, D])
        mv2 = sb("mv2", [ROWS, TTILES, 2])
        rs2 = sb("rs2", [ROWS, TTILES])
        x2t = [sb(f"x2t{i}", [ROWS, D]) for i in range(2)]
        idxf = sb("idxf", [ROWS, TTILES, 2, TOPK])
        wts = sb("wts", [ROWS, TTILES, 2, TOPK])
        owner = sb("owner", [1, 2, BLOCKS], I32)
        step_has = sb("step_has", [1, 2, STEPS])
        steps_f = sb("steps_f", [1, 2])
        steps_used = sb("steps_used", [1, 2], I32)
        slotf = [sb(f"slotf{i}", [ROWS, 2 * TOPK]) for i in range(2)]
        slot_now = [sb(f"slot_now{i}", [ROWS, 2 * TOPK], I32) for i in range(2)]
        slot_get = [sb(f"slot_get{i}", [ROWS, 2 * TOPK], I32) for i in range(2)]
        slot_put = [sb(f"slot_put{i}", [ROWS, 2 * TOPK], I32) for i in range(2)]
        acc = [sb(f"acc{i}", [ROWS, 2, D]) for i in range(2)]
        slots = sb("slots", [ROWS, TTILES, 2 * TOPK], I32)

        phase[0] = ExitStack()
        lines = [sb(f"lines{s}", [SUB, LINE]) for s in range(2)]
        patches = [sb(f"patches{s}", [SUB, HALVES, HP, 128]) for s in range(2)]
        pixT = sb("pixT", [128, HALVES, CH, G_IMG, 64])
        h = sb("h", [SPAN, TILES, D])
        h_res = sb("h_res", [SPAN, TILES, D])
        st = sb("st", [SPAN, TILES, 6])
        mv = sb("mv", [SPAN, TILES, 2])
        va = sb("va", [SPAN, TILES])
        rr = sb("rr", [SPAN, TILES])
        rt = sb("rt", [SPAN, TILES])
        xn = sb("xn", [SPAN, TILES, D])
        xnT = sb("xnT", [DH, 2, G_IMG, TOK])
        xnT_rep = sb("xnT_rep", [DH, 2 * G_IMG, VG, TOK])
        qk_pad = sb("qk_pad", [128, 2 * QUADS * G_IMG, PAD])
        qk_sum = sb("qk_sum", [128, 2 * QUADS * G_IMG, TOK])
        qk = sb("qk", [128, 2 * QUADS, G_IMG, TOK])
        k_quad = sb("k_quad", [128, QUADS * G_IMG, HEADS_PER_QUAD, TOK])
        vals = sb("vals", [VG * TOK, G_IMG, VGROUPS, VG, VW])
        smax = sb("smax", [SPAN, 2, HEADS])
        probs = sb("probs", [SPAN, 2, HEADS, TOK])
        probsT = sb("probsT", [VG * TOK, 2, VGROUPS, SPAN])
        rsum = sb("rsum", [SPAN, HEADS])
        att = sb("att", [SPAN, HEADS, HD])
        h2 = sb("h2", [SPAN, TILES, D])
        phase[0].close()

        phase[0] = ExitStack()
        st2 = sb("st2", [ROWS, TTILES, 6])
        va2 = sb("va2", [ROWS, TTILES])
        rt2 = sb("rt2", [ROWS, TTILES])
        x2T = [sb(f"x2T{i}", [DH, 2, ROWS]) for i in range(2)]
        logit = [sb(f"logit{i}", [ROWS, 2, EXPERTS]) for i in range(2)]
        escr = [sb(f"escr{i}", [ROWS, 2, EXPERTS]) for i in range(2)]
        top8 = [sb(f"top8_{i}", [ROWS, 2, 8]) for i in range(2)]
        idx8 = [sb(f"idx8_{i}", [ROWS, 2, 8], U32) for i in range(2)]
        nmax = [sb(f"nmax{i}", [ROWS, 2]) for i in range(2)]
        etop = [sb(f"etop{i}", [ROWS, 2, TOPK]) for i in range(2)]
        zsum = [sb(f"zsum{i}", [ROWS, 2]) for i in range(2)]
        s4 = [sb(f"s4_{i}", [ROWS, 2]) for i in range(2)]
        den = [sb(f"den{i}", [ROWS, 2]) for i in range(2)]
        iden = [sb(f"iden{i}", [ROWS, 2]) for i in range(2)]
        hot = [sb(f"hot{i}", [ROWS, 2, TOPK, EXPERTS], BF16) for i in range(2)]
        rank = sb("rank", [ROWS, TTILES, 2 * EXPERTS])
        cnt_i = sb("cnt_i", [128, 2], I32)
        nblk_i = sb("nblk_i", [128, 2], I32)
        nblk = sb("nblk", [128, 2], BF16)
        cum = sb("cum", [128, 2])
        base_c = sb("base_c", [128, 2])
        diag = sb("diag", [128, 2, 128])
        base_b = sb("base_b", [128, 2 * EXPERTS])
        passed = sb("passed", [128, 2, BLOCKS], BF16)
        srank = [sb(f"srank{i}", [ROWS, 2 * EXPERTS]) for i in range(2)]
        pick = sb("pick", [ROWS, 2 * TOPK, EXPERTS])
        phase[0].close()

        phase[0] = ExitStack()
        xs = [sb(f"xs{r}", [ROWS, SB, D]) for r in range(RING)]
        fw = [sb(f"fw{r}", [128, SB, 256]) for r in range(RING)]
        xsT = [sb(f"xsT{i}", [128, 256]) for i in range(2)]
        os_ = [sb(f"os{r}", [ROWS, SB, D]) for r in range(RING)]
        gat = [sb(f"gat{i}", [ROWS, TOPK, D]) for i in range(2)]
        comb = [sb(f"comb{i}", [ROWS, D]) for i in range(2)]

        phase[0].close()
        phase[0] = ctx
        w_loaded = sem("w_loaded")
        cls_loaded = sem("cls_loaded")
        pool_step = sem("pool_step")
        consts = sem("consts")
        zeroed = sem("zeroed")
        setup_ps = sem("setup_ps")
        setup_ev = sem("setup_ev")
        dve_step = sem("dve_step")
        embn_ready = sem("embn_ready")
        raw_used = sem("raw_used")
        lines_loaded = [sem(f"lines_loaded{s}") for s in range(2)]
        ring_filled = sem("ring_filled")
        ring_emptied = sem("ring_emptied")
        patch_done = sem("patch_done")
        patches_ready = sem("patches_ready")
        rep_ready = sem("rep_ready")
        st_ready = sem("st_ready")
        rr_step = sem("rr_step")
        rr_ready = sem("rr_ready")
        rs2_ready = sem("rs2_ready")
        emb_a_ready = sem("emb_a_ready")
        emb_y_step = sem("emb_y_step")
        emb_y_ready = sem("emb_y_ready")
        rs2_step = sem("rs2_step")
        taken = sem("taken")
        smax_ready = sem("smax_ready")
        fin_step = sem("fin_step")
        top_ready = sem("top_ready")
        wt_step = sem("wt_step")
        slot_step = sem("slot_step")
        comb_step = [sem(f"comb_step{p}") for p in range(2)]
        h_ready = sem("h_ready")
        res_ready = sem("res_ready")
        res_used = sem("res_used")
        xn_ready = sem("xn_ready")
        xn_transposed = sem("xn_transposed")
        xnT_copied = sem("xnT_copied")
        sums_ready = sem("sums_ready")
        cat_ready = sem("cat_ready")
        quad_ready = sem("quad_ready")
        v_filled = sem("v_filled")
        v_masked = sem("v_masked")
        scores_done = sem("scores_done")
        scores_read = sem("scores_read")
        probs_ready = sem("probs_ready")
        p_transposed = sem("p_transposed")
        pT_copied = sem("pT_copied")
        pv_done = sem("pv_done")
        o_read = sem("o_read")
        h2_ready = sem("h2_ready")
        stored = sem("stored")

        h2r_loaded = sem("h2r_loaded")
        st2_ready = sem("st2_ready")
        x2t_ready = sem("x2t_ready")
        idx_done = sem("idx_done")
        x2T_filled = sem("x2T_filled")
        x2T_copied = sem("x2T_copied")
        logit_filled = sem("logit_filled")
        logit_ready = sem("logit_ready")
        nmax_ready = sem("nmax_ready")
        exp_done = sem("exp_done")
        hot_ready = sem("hot_ready")
        rank_filled = sem("rank_filled")
        rank_copied = sem("rank_copied")
        hot_used = sem("hot_used")
        plan_ps = sem("plan_ps")
        plan_ev = sem("plan_ev")
        slot_ready = sem("slot_ready")
        scattered = [sem(f"scattered{i}") for i in range(2)]

        xs_loaded = [[sem(f"xs_loaded{p}_{r}") for r in range(RING)] for p in range(2)]
        fw_loaded = [[sem(f"fw_loaded{p}_{r}") for r in range(RING)] for p in range(2)]
        t_filled = [sem(f"t_filled{p}") for p in range(2)]
        t_copied = [sem(f"t_copied{p}") for p in range(2)]
        y_filled = [sem(f"y_filled{p}") for p in range(2)]
        y_copied = [sem(f"y_copied{p}") for p in range(2)]
        y_stored = [[sem(f"y_stored{p}_{i}") for i in range(RING)] for p in range(2)]

        idx_ready = [sem(f"idx_ready{p}") for p in range(2)]
        gathered = [[sem(f"gathered{p}_{i}") for i in range(2)] for p in range(2)]
        comb_ready = [sem(f"comb_ready{p}") for p in range(2)]
        comb_out = [[sem(f"comb_out{p}_{i}") for i in range(2)] for p in range(2)]

        def take(engine):
            engine.sem_inc(taken, 1)

        block = ctx.enter_context(nc.Block())

        lines_view = x.rearrange("b c (hp r) w -> (b c hp) (r w)", r=PATCH)
        f_view = f_know.rearrange("n (p j) r -> (n p) (j r)", j=2)
        r_view = r_know.rearrange("n r d -> (n r) d")
        SUPERS = STEPS * RING
        W_LOADS = 16
        PAIRED = 2 * PAIRS

        @block.sync
        def _(sp):
            sp.dma_start(lines[0][:], lines_view[0:SUB, :]).then_inc(lines_loaded[0], 16)
            sp.dma_start(lines[1][:], lines_view[SUB:2 * SUB, :]).then_inc(lines_loaded[1], 16)
            n = 0
            for dst, src in (
                    (tok_nat[:], tok_w.rearrange("(c p) k -> p c k", p=DH)),
                    (qkv_nat[:], qkv_w.rearrange("(c p) k -> p c k", p=DH)),
                    (tok_bias[:], tok_b.partition_broadcast(SPAN)),
                    (g_col[:], ln_g.rearrange("(j p) -> p j", p=DH)),
                    (b_col[:], ln_b.rearrange("(j p) -> p j", p=DH)),
                    (qk_brow[:, :, 0, :], qkv_b[0:2 * D].rearrange("(o n j) -> o n j", o=1, j=HD)),
                    (qk_brow[:, :, 1, :], qkv_b[0:2 * D].rearrange("(o n j) -> o n j", o=1, j=HD)),
                    (v_brow[:], qkv_b[2 * D:3 * D].rearrange("(o n) -> o n", o=1)),
                    (emb[:, 0, :], emb_fk), (emb[:, 1, :], emb_rk),
                    (wr_nat[:, 0], w_fk.rearrange("(j p) k -> p j k", p=DH)),
                    (wr_nat[:, 1], w_rk.rearrange("(j p) k -> p j k", p=DH)),
                    (br_col[:, 0:1], b_fk.rearrange("(p o) -> p o", o=1)),
                    (br_col[:, 1:2], b_rk.rearrange("(p o) -> p o", o=1))):
                sp.dma_start(dst, src, allow_slow_non_contiguous=True).then_inc(w_loaded, 16)
                n += 1
            sp.wait_ge(w_loaded, 16 * n)
            for a in range(2):
                sp.dma_start(tok_bias[64 * a:64 * a + 1, :], cls_tok[0]).then_inc(cls_loaded, 16)
            sp.wait_ge(consts, 1)
            sp.dma_start(h2_dram[TOKENS:PTOK, :], zeros[0:PTOK - TOKENS, 0:D]).then_inc(zeroed, 16)

            def zero_slots(g):
                for dram, width in ((wide_dram, D), (mid_dram, RANK)):
                    k = SLOTS * width // 128 // ZW // GROUPS
                    view = dram.rearrange("(p r) d -> p (r d)", p=128).rearrange("p (k z) -> p k z", z=ZW)
                    sp.dma_start(view[:, bass.ds(g * k, k), :], zeros[:, None, :].to_broadcast([128, k, ZW]))\
                      .then_inc(zeroed, 16)

            def store_group(g):
                sp.wait_ge(h2_ready, TILES * (g + 1))
                for a in range(2):
                    rows = h2_dram[bass.ds(g * G_IMG * TOK, G_IMG * TOK), :]
                    view = rows.rearrange("(t a n) d -> n t a d", a=2, n=TOK)
                    sp.dma_start(view[:, :, a, :], h2[64 * a:64 * a + TOK]).then_inc(stored, 16)

            def load_lines(g1):
                for s in range(2):
                    sp.wait_ge(patches_ready, 2 * (g1 - 1) + s + 1)
                    row = g1 * (2 * SUB) + s * SUB
                    sp.dma_start(lines[s][:], lines_view[bass.ds(row, SUB), :]).then_inc(lines_loaded[s], 16)

            load_lines(1)
            with sp.Fori(0, GROUPS - 2) as g:
                load_lines(g + 2)
                zero_slots(g)
                store_group(g)
            for g in (GROUPS - 2, GROUPS - 1):
                zero_slots(g)
                store_group(g)

            sp.wait_ge(stored, 16 * 2 * GROUPS)
            sp.wait_ge(zeroed, 16 * (1 + 2 * GROUPS))
            sp.dma_start(h2r[:], h2_dram.rearrange("(t p) d -> p t d", p=ROWS)).then_inc(h2r_loaded, 16)

            def expert_loads(layer):
                src = (wide_dram, mid_dram)[layer]
                width = (D, RANK)[layer]
                used = sp.value_load(steps_used[0:1, layer:layer + 1], min_val=1, max_val=STEPS)
                with sp.Fori(0, STEPS) as s, sp.If(s < used):
                    _, experts = nc.values_load_multi_w_load_instructions(
                        owner[0:1, layer, bass.ds(s * BODY, BODY)], engines=[mybir.EngineType.SP],
                        min_val=0, max_val=EXPERTS - 1,
                        skip_runtime_bounds_check_because="owner is clamped to the experts where it is computed")
                    for r in range(RING):
                        sp.wait_ge(y_filled[layer], 2 * (s * RING + r) + 2)
                        rows = src[bass.ds((s * RING + r) * (SB * ROWS), SB * ROWS), :]
                        sp.dma_start(xs[r][:, :, 0:width], rows.rearrange("(k p) d -> p k d", p=ROWS))\
                          .then_inc(xs_loaded[layer][r], 16)
                        for k in range(SB):
                            e = experts[r * SB + k]
                            if layer == 0:
                                sp.dma_start(fw[r][0:DH, k, :], f_view[bass.ds(e * DH, DH), :])\
                                  .then_inc(fw_loaded[0][r], 16)
                            else:
                                sp.dma_start(fw[r][:, k, 0:D], r_view[bass.ds(e * RANK, RANK), :])\
                                  .then_inc(fw_loaded[1][r], 16)

            sp.wait_ge(plan_ev, 4)
            for i in range(2):
                sp.wait_ge(scattered[i], 64 * (PAIRS + (1 - i)))
            expert_loads(0)
            for i in range(2):
                sp.wait_ge(comb_out[0][i], 64 * (PAIRS + (1 - i)))
            expert_loads(1)

            def store_out(t, i, n):
                sp.wait_ge(comb_ready[1], t + 1)
                sp.dma_start(out[bass.ds(t * ROWS, n), :], comb[i][0:n, :]).then_inc(comb_out[1][i], 16)

            with sp.Fori(0, PAIRS) as p:
                for i in range(2):
                    store_out(2 * p + i, i, ROWS)
            store_out(PAIRED, 0, LAST)
            for i in range(2):
                sp.wait_ge(comb_out[1][i], 16 * (PAIRS + (1 - i)))

        @block.gpsimd
        def _(pool):
            step = [0]

            def link(ins):
                step[0] += 1
                ins.then_inc(pool_step, 1)
                pool.wait_ge(pool_step, step[0])

            pool.memset(zeros[:], 0.0).then_inc(consts, 1)
            link(pool.memset(ident[:], 0.0))
            link(pool.affine_select(out=ident[:], in_=ident[:], compare_op=ALU.not_equal, fill=1.0,
                                    base=0, pattern=[[-1, 128]], channel_multiplier=1))
            link(pool.memset(before[:], 1.0))
            link(pool.affine_select(out=before[:], in_=before[:], compare_op=ALU.is_gt, fill=0.0,
                                    base=0, pattern=[[1, 128]], channel_multiplier=-1))
            link(pool.memset(after[:], 1.0))
            link(pool.affine_select(out=after[:], in_=after[:], compare_op=ALU.is_ge, fill=0.0,
                                    base=0, pattern=[[-1, 128]], channel_multiplier=1))
            link(pool.memset(upto[:], 1.0))
            link(pool.affine_select(out=upto[:], in_=upto[:], compare_op=ALU.is_ge, fill=0.0,
                                    base=0, pattern=[[1, 128]], channel_multiplier=-1))
            link(pool.memset(head_mask[:], 1.0))
            link(pool.affine_select(out=head_mask[:], in_=head_mask[:], compare_op=ALU.is_ge, fill=0.0,
                                    base=0, pattern=[[-TOK, VG], [0, VW]], channel_multiplier=1))
            link(pool.affine_select(out=head_mask[:], in_=head_mask[:], compare_op=ALU.is_ge, fill=0.0,
                                    base=TOK - 1, pattern=[[TOK, VG], [0, VW]], channel_multiplier=-1))
            link(pool.iota(iota_n[:], pattern=[[1, EXPERTS]], base=0, channel_multiplier=0,
                           allow_small_or_imprecise_dtypes=True))
            link(pool.iota(iota_blk[:], pattern=[[1, BLOCKS]], base=0, channel_multiplier=0,
                           allow_small_or_imprecise_dtypes=True))
            link(pool.iota(part_i[:], pattern=[[0, 1]], base=0, channel_multiplier=1))
            link(pool.memset(pixT[:], 0.0))
            link(pool.memset(qk_pad[:], 0.0))
            link(pool.memset(k_quad[:], 0.0))
            link(pool.memset(magic[:], 0x5f3759df + 1))
            link(pool.memset(ones_bf[:], 1.0))
            link(pool.memset(zeros_bf[:], 0.0))
            pool.memset(ones[:], 1.0).then_inc(consts, 1)

            def regroup(g1, s):
                pool.wait_ge(lines_loaded[s], 16 * (g1 + 1))
                take(pool)
                if not (isinstance(g1, int) and g1 == 0):
                    pool.wait_ge(ring_filled, 10 * (g1 - 1) + 2 * s + 2)
                    take(pool)
                for half in range(HALVES):
                    w = LINE // HALVES
                    src = lines[s][:, half * w:(half + 1) * w].rearrange("q (r w c) -> q w r c", r=8, c=PATCH)
                    dst = patches[s][:, half].rearrange("q w (r c) -> q w r c", c=PATCH)
                    last = pool.tensor_copy(dst, src)
                last.then_inc(patches_ready, 1)

            STEPS_OF_ROOT = 12

            def inverse_root(y, a, t, steps, n, ready):
                pool.tensor_tensor(y.bitcast(I32), y.bitcast(I32), magic[0:y.shape[0], 0:y.shape[1]], ALU.add)\
                    .then_inc(steps, 1)
                for i in range(3):
                    pool.wait_ge(steps, n + 4 * i + 1)
                    pool.tensor_tensor(t, y, y, ALU.mult).then_inc(steps, 1)
                    pool.wait_ge(steps, n + 4 * i + 2)
                    pool.tensor_tensor(t, t, a, ALU.mult).then_inc(steps, 1)
                    pool.wait_ge(steps, n + 4 * i + 3)
                    take(pool)
                    pool.tensor_scalar(t, t, -0.5, 1.5, ALU.mult, ALU.add).then_inc(steps, 1)
                    pool.wait_ge(steps, n + 4 * i + 4)
                    pool.tensor_tensor(y, y, t, ALU.mult).then_inc(ready if i == 2 else steps, 1)

            def norm_factors(g1):
                pool.wait_ge(st_ready, 4 * (g1 + 1))
                inverse_root(rr[:], va[:], rt[:], rr_step, STEPS_OF_ROOT * g1, rr_ready)

            def group(g, more):
                pool.wait_ge(h_ready, 2 * (g + 1))
                pool.wait_ge(res_used, g + 1)
                pool.tensor_tensor(h_res[:], h[:], v_bias[:, None, :].to_broadcast([SPAN, TILES, D]),
                                   ALU.add).then_inc(res_ready, 1)
                for q in range(2):
                    pool.wait_ge(ring_emptied, 2 + 4 + 10 * g + QUADS * (q + 1))
                    pool.wait_ge(cat_ready, 2 * g + q + 1)
                    n = QUADS * G_IMG
                    v = qk_pad[:, q * n:(q + 1) * n, :]
                    pool.tensor_tensor(qk_sum[:, q * n:(q + 1) * n, :], v[:, :, 0:TOK], v[:, :, 2:PAD],
                                       ALU.add).then_inc(sums_ready, 1)
                if more > 1:
                    regroup(g + 2, 0)
                if more > 0:
                    norm_factors(g + 1)
                if more > 1:
                    regroup(g + 2, 1)

            regroup(0, 0)
            regroup(0, 1)
            pool.wait_ge(emb_a_ready, 1)
            inverse_root(emb_y[:], emb_a[:], emb_t[:], emb_y_step, 0, emb_y_ready)
            regroup(1, 0)
            norm_factors(0)
            regroup(1, 1)
            with pool.Fori(0, GROUPS - 2) as g:
                group(g, 2)
            group(GROUPS - 2, 1)
            group(GROUPS - 1, 0)

            pool.wait_ge(st2_ready, 4)
            inverse_root(rs2[:], va2[:], rt2[:], rs2_step, 0, rs2_ready)

            pool.wait_ge(zeroed, 16 * (1 + 2 * GROUPS))

            def scatter_x2(t, i):
                pool.wait_ge(slot_ready, t + 1)
                take(pool)
                for e in range(TOPK):
                    pool.indirect_dma_start(wide_dram, bass.IndirectOffsetOnAxis(ap=slot_now[i][:, e:e + 1], axis=0),
                                            x2t[i][:], None).then_inc(scattered[i], 16)

            with pool.Fori(0, PAIRS) as p:
                for i in range(2):
                    scatter_x2(2 * p + i, i)
            scatter_x2(PAIRED, 0)

            def expert_rows(layer):
                used = pool.value_load(steps_used[0:1, layer:layer + 1], min_val=1, max_val=STEPS)
                for i in range(RING):
                    pool.wait_ge(y_stored[layer][i], used * 16)
                    take(pool)

            pool.wait_ge(plan_ev, 4)
            expert_rows(0)

            def gather(layer, t, i):
                pool.wait_ge(idx_ready[layer], t + 1)
                take(pool)
                for e in range(TOPK):
                    pool.indirect_dma_start(
                        gat[i][:, e, :], None, wide_dram,
                        bass.IndirectOffsetOnAxis(ap=slot_get[i][:, layer * TOPK + e:layer * TOPK + e + 1], axis=0))\
                        .then_inc(gathered[layer][i], 16)

            def scatter_mid(t, i, k):
                pool.wait_ge(comb_ready[0], t + 1)
                take(pool)
                for e in range(TOPK):
                    pool.indirect_dma_start(
                        mid_dram, bass.IndirectOffsetOnAxis(ap=slot_put[i][:, TOPK + e:TOPK + e + 1], axis=0),
                        comb[i][:, 0:RANK], None).then_inc(comb_out[0][i], 16)

            with pool.Fori(0, PAIRS) as p:
                for i in range(2):
                    gather(0, 2 * p + i, i)
                for i in range(2):
                    scatter_mid(2 * p + i, i, p + 1)
            gather(0, PAIRED, 0)
            scatter_mid(PAIRED, 0, PAIRS + 1)

            expert_rows(1)

            with pool.Fori(0, PAIRS) as p:
                for i in range(2):
                    gather(1, 2 * p + i, i)
            gather(1, PAIRED, 0)
            for i in range(2):
                pool.wait_ge(gathered[1][i], 64 * (PAIRS + (1 - i)))

        @block.tensor
        def _(pe):
            pe.sem_inc(x2T_filled, 2)
            pe.sem_inc(hot_used, 2)
            for layer in range(2):
                pe.sem_inc(y_filled[layer], 2 * RING)

            fills = [0]

            def filled(ins):
                fills[0] += 1
                ins.then_inc(setup_ps, 1)

            def room():
                if fills[0] >= 4:
                    pe.wait_ge(setup_ev, fills[0] - 3)
                return bank[fills[0] % 4]

            pe.wait_ge(consts, 2)
            pe.wait_ge(w_loaded, 16 * 14)
            for kt in range(CH * HALVES):
                b = room()
                for c in range(2):
                    last = pe.transpose(b[:, c * DH:(c + 1) * DH], tok_nat[:, c, kt * 128:(kt + 1) * 128],
                                        ident[0:DH, 0:DH])
                filled(last)
            for c in range(6):
                b = room()
                for j in range(2):
                    last = pe.transpose(b[0:DH, j * DH:(j + 1) * DH], qkv_nat[:, c, j * DH:(j + 1) * DH],
                                        ident[0:DH, 0:DH])
                filled(last)
            b = room()
            for r in range(2):
                for j in range(2):
                    last = pe.transpose(b[0:DS, (2 * r + j) * DH:(2 * r + j + 1) * DH], wr_nat[:, r, j, :],
                                        ident[0:DH, 0:DH])
            filled(last)
            b = room()
            pe.wait_ge(embn_ready, 1)
            for r in range(2):
                last = pe.transpose(b[0:DS, r * 128:(r + 1) * 128], emb_nrm[:, r, :], ident[:])
            filled(last)
            b = room()
            pe.wait_ge(setup_ev, 14)
            for n in range(2 * QUADS):
                q, i = divmod(n, QUADS)
                heads = slice(q * HEADS + i * 4, q * HEADS + i * 4 + 4)
                for j in range(2):
                    pe.matmul(b[:, n:n + 1], w_qkT[:, j, heads].rearrange("p a b c -> p (a b c)"),
                              b_col[:, j:j + 1], start=j == 0, stop=False)
                last = pe.matmul(b[:, n:n + 1], qk_brow[0:1, heads].rearrange("p a b c -> p (a b c)"),
                                 ones[0:1, 0:1], start=False, stop=True)
            filled(last)
            b = room()
            for j in range(2):
                pe.matmul(b[0:SPAN, 0:D], b_col[:, j:j + 1].to_broadcast([DH, SPAN]), w_vT[:, j, :],
                          start=j == 0, stop=False)
            filled(pe.matmul(b[0:SPAN, 0:D], ones[0:1, 0:SPAN], v_brow[:], start=False, stop=True))
            b = room()
            for r in range(2):
                for j in range(2):
                    last = pe.matmul(b[0:DH, j * 256 + r * 128:j * 256 + (r + 1) * 128],
                                     wrT[:, r, j * DH:(j + 1) * DH], embT[:, r, :], start=True, stop=True)
            filled(last)
            b = room()
            for r in range(2):
                last = pe.matmul(b[:, r * 128:(r + 1) * 128], br_col[:, r:r + 1].to_broadcast([DS, 128]),
                                 embT[:, r, :], start=True, stop=True)
            filled(last)
            pe.wait_ge(setup_ev, 19)

            def to_pixels(g1, u0):
                for s in range(2):
                    pe.wait_ge(patches_ready, 2 * g1 + s + 1)
                    for half in range(HALVES):
                        u = 2 * s + half
                        pe.wait_ge(ring_emptied, u0 + u + 1)
                        cols = bank[u % 2][:, 0:HP * SUB].rearrange("p (k b c y v) -> p k v b c y", k=CH, b=4, c=CH, y=HP)
                        for w in range(HP):
                            last = pe.transpose(cols[:, w % CH, w // CH], patches[s][:, half, w, :], ident[0:SUB, 0:SUB])
                        last.then_inc(ring_filled, 1)

            def embed(g1, j, first):
                f, t = divmod(j, 2)
                if j == 0:
                    pe.wait_ge(ring_emptied, 10 * g1 + 4 + 2)
                if t == 0 and not first:
                    pe.wait_ge(v_masked, 4 * g1 - 1 + f)
                for kt in range(CH * HALVES):
                    c, half = divmod(kt, HALVES)
                    last = pe.matmul(bank[2 + 3 * f][:, t * D:(t + 1) * D],
                                     pixT[:, half, c, 2 * j:2 * j + 2, :].rearrange("p a n -> p (a n)"),
                                     tok_wT[:, kt, :], start=kt == 0, stop=kt == CH * HALVES - 1)
                if t == 1:
                    last.then_inc(patch_done, 1)

            def project(g):
                for j in range(TILES):
                    f, t = divmod(j, 2)
                    pe.wait_ge(xn_ready, TILES * g + j + 1)
                    for k in range(2):
                        last = pe.transpose(bank[2 + 3 * f][0:DH, k * 256 + t * 128:k * 256 + t * 128 + SPAN],
                                            xn[:, j, k * DH:(k + 1) * DH], ident[0:SPAN, 0:SPAN])
                    if t == 1:
                        last.then_inc(xn_transposed, 1)
                pe.wait_ge(xnT_copied, 2 * (g + 1))
                for n in range(2 * QUADS):
                    q, i = divmod(n, QUADS)
                    heads = slice(q * HEADS + i * 4, q * HEADS + i * 4 + 4)
                    pe.wait_ge(ring_emptied, 4 + 10 * g + n + 1)
                    for j in range(2):
                        last = pe.matmul(bank[n % 2][:, 0:G_IMG * TOK],
                                         w_qkT[:, j, heads].rearrange("p a b c -> p (a b c)"),
                                         xnT[:, j].rearrange("p i n -> p (i n)"), start=j == 0, stop=j == 1)
                    last.then_inc(ring_filled, 1)
                pe.wait_ge(rep_ready, g + 1)
                for m in range(G_IMG):
                    f, t = divmod(m, 2)
                    if t == 0 and f >= 2:
                        pe.wait_ge(v_masked, 4 * g + f - 1)
                    for j in range(2):
                        last = pe.matmul(bank[2 + 3 * (f % 2)][0:VG * TOK, t * D:(t + 1) * D],
                                         xnT_rep[:, j * G_IMG + m].rearrange("p r n -> p (r n)"),
                                         w_vT[:, j, :], start=j == 0, stop=j == 1)
                    if t == 1:
                        last.then_inc(v_filled, 1)

            def scores(g, j):
                if j == 0:
                    pe.wait_ge(quad_ready, g + 1)
                pe.wait_ge(scores_read, TILES * g + j + 1)
                b = bank[4 + 2 * (j % 2)]
                for a in range(2):
                    for i in range(QUADS):
                        w = HEADS_PER_QUAD * TOK
                        last = pe.matmul(b[64 * a:64 * a + TOK, i * w:(i + 1) * w], qk[:, i, 2 * j + a, :],
                                         k_quad[:, i * G_IMG + 2 * j + a].rearrange("p a b -> p (a b)"),
                                         start=True, stop=True)
                last.then_inc(scores_done, 1)

            def turn(g, j):
                pe.wait_ge(probs_ready, TILES * g + j + 1)
                pe.wait_ge(pT_copied, TILES * g + j + 1)
                for v in range(VGROUPS):
                    last = pe.transpose(bank[7][0:VG * TOK, v * SPAN:(v + 1) * SPAN],
                                        probs[:, j % 2, VG * v:VG * (v + 1), :].rearrange("p a b -> p (a b)"),
                                        ident[0:SPAN, 0:SPAN])
                last.then_inc(p_transposed, 1)

            def attend(g, j):
                pe.wait_ge(pT_copied, TILES * g + j + 2)
                pe.wait_ge(o_read, TILES * g + j + 1)
                if j == 0:
                    pe.wait_ge(v_masked, 4 * (g + 1))
                for a in range(2):
                    for v in range(VGROUPS):
                        last = pe.matmul(bank[3][64 * a:64 * a + TOK, 256 + v * VG * VW:256 + (v + 1) * VG * VW],
                                         probsT[:, j % 2, v, 64 * a:64 * a + TOK],
                                         vals[:, 2 * j + a, v].rearrange("p a b -> p (a b)"),
                                         start=True, stop=True)
                last.then_inc(pv_done, 1)

            def attention(g, more):
                project(g)
                if more:
                    to_pixels(g + 1, 4 + 10 * g + 6)
                scores(g, 0)
                scores(g, 1)
                if more:
                    embed(g + 1, 0, False)
                    embed(g + 1, 1, False)
                turn(g, 0)
                scores(g, 2)
                if more:
                    embed(g + 1, 2, False)
                attend(g, 0)
                turn(g, 1)
                scores(g, 3)
                if more:
                    embed(g + 1, 3, False)
                attend(g, 1)
                turn(g, 2)
                attend(g, 2)
                turn(g, 3)
                attend(g, 3)

            to_pixels(0, 0)
            for j in range(TILES):
                embed(0, j, True)
            with pe.Fori(0, GROUPS - 1) as g:
                attention(g, True)
            attention(GROUPS - 1, False)

            pe.wait_ge(o_read, TILES * GROUPS + 1)
            pe.wait_ge(scores_read, TILES * GROUPS + 2)
            pe.matmul(bank[4][:, 0:256], zeros_bf[:, 0:128], zeros_bf[:], start=True, stop=False,
                      skip_group_check=True)

            def route_transpose(t, i):
                pe.wait_ge(x2t_ready, t + 1)
                pe.wait_ge(x2T_copied, t + 1)
                for j in range(2):
                    last = pe.transpose(bank[i][0:DH, j * ROWS:(j + 1) * ROWS], x2t[i][:, j * DH:(j + 1) * DH],
                                        ident[:])
                last.then_inc(x2T_filled, 1)

            def route_logits(t, i):
                pe.wait_ge(x2T_copied, t + 3)
                pe.wait_ge(logit_ready, t + 1)
                for j in range(2):
                    last = pe.matmul(bank[2 + i][:, 0:256], x2T[i][:, j, :], r_mat[:, j, :],
                                     start=j == 0, stop=j == 1)
                last.then_inc(logit_filled, 1)

            def route_rank(t, i):
                pe.wait_ge(hot_ready, t + 1)
                for e in range(TOPK):
                    last = pe.matmul(bank[4][:, 0:256], before[:], hot[i][:, :, e, :], start=False, stop=False,
                                     skip_group_check=True)
                last.then_inc(rank_filled, 1)
                pe.wait_ge(rank_copied, t + 1)
                for e in range(TOPK):
                    last = pe.matmul(bank[4][:, 0:256], after[:], hot[i][:, :, e, :], start=False, stop=False,
                                     skip_group_check=True)
                last.then_inc(hot_used, 1)

            def route(t, i):
                route_transpose(t, i)
                route_logits(t, i)

            for i in range(2):
                route(i, i)
            with pe.Fori(0, PAIRS - 1) as p:
                for i in range(2):
                    route_rank(2 * p + i, i)
                    route(2 * p + 2 + i, i)
            route_rank(PAIRED - 2, 0)
            route(PAIRED, 0)
            route_rank(PAIRED - 1, 1)
            route_rank(PAIRED, 0)

            pe.wait_ge(plan_ev, 1)
            for r in range(2):
                last = pe.matmul(bank[5][:, r:r + 1], upto[:], nblk[:, r:r + 1], start=True, stop=True)
            last.then_inc(plan_ps, 1)
            pe.wait_ge(plan_ev, 2)
            for r in range(2):
                last = pe.matmul(bank[6][:, r * 128:(r + 1) * 128], ones[:], diag[:, r, :], start=True, stop=True)
            last.then_inc(plan_ps, 1)
            pe.wait_ge(plan_ev, 3)
            for r in range(2):
                last = pe.matmul(bank[7][0:1, r * BLOCKS:(r + 1) * BLOCKS], ones_bf[:], passed[:, r, :],
                                 start=True, stop=True)
            last.then_inc(plan_ps, 1)
            pe.wait_ge(plan_ev, 4)

            def experts(layer):
                parts = (2, 1)[layer]
                kp = (DH, RANK)[layer]
                width = (RANK, D)[layer]
                filled_ = t_filled[layer]
                used = pe.value_load(steps_used[0:1, layer:layer + 1], min_val=1, max_val=STEPS)
                with pe.Fori(0, STEPS) as s, pe.If(s < used):
                    def transposed(n):
                        r, k = divmod(n, SB)
                        if k == 0:
                            pe.wait_ge(xs_loaded[layer][r], 16 * (s + 1))
                        pe.wait_ge(t_copied[layer], s * BODY + n + 1)
                        for j in range(parts):
                            src = xs[r][:, k, j:D:2] if layer == 0 else xs[r][:, k, 0:RANK]
                            last = pe.transpose(bank[n % 2][0:kp, j * ROWS:(j + 1) * ROWS], src, ident[:])
                        last.then_inc(filled_, 1)

                    transposed(0)
                    for n in range(BODY):
                        r, k = divmod(n, SB)
                        if n + 1 < BODY:
                            transposed(n + 1)
                        if k == 0:
                            pe.wait_ge(fw_loaded[layer][r], 16 * SB * (s + 1))
                        if k % 2 == 0:
                            pe.wait_ge(y_copied[layer], s * (BODY // 2) + n // 2 + 1)
                        pe.wait_ge(t_copied[layer], s * BODY + n + 3)
                        dst = bank[2 + (n // 2) % 2][:, (k % 2) * 256:(k % 2) * 256 + width]
                        for j in range(parts):
                            w = fw[r][0:kp, k, j * 128:(j + 1) * 128] if layer == 0 else fw[r][:, k, 0:D]
                            last = pe.matmul(dst, xsT[n % 2][0:kp, j * ROWS:(j + 1) * ROWS], w,
                                             start=j == 0, stop=j == parts - 1)
                        if k % 2 == 1:
                            last.then_inc(y_filled[layer], 1)

            experts(0)
            experts(1)

        @block.scalar
        def _(act):
            act.sem_inc(ring_emptied, 2)
            act.sem_inc(pT_copied, 1)
            act.sem_inc(x2T_copied, 2)
            act.sem_inc(exp_done, 2)
            for layer in range(2):
                act.sem_inc(t_copied[layer], 2)
                act.sem_inc(y_copied[layer], 2)
            act.wait_ge(consts, 2)

            def pixels(g1, u0):
                for u in range(4):
                    s, half = divmod(u, 2)
                    act.wait_ge(ring_filled, u0 + u + 1)
                    if u == 0:
                        act.wait_ge(patch_done, 2 * g1)
                    src = bank[u % 2][:, 0:HP * SUB].rearrange("p (k b n) -> p k b n", k=CH, b=4)
                    dst = pixT[:, half, :, s * 4:(s + 1) * 4, 1:TOK]
                    act.activation(dst, src, ACT.Copy).then_inc(ring_emptied, 1)

            def projections(g):
                for f in range(2):
                    act.wait_ge(xn_transposed, 2 * g + f + 1)
                    src = bank[2 + 3 * f][0:DH, :].rearrange("p (k a n) -> p k a n", k=2, a=4)[:, :, :, 0:TOK]
                    act.activation(xnT[:, :, 4 * f:4 * f + 4, :], src, ACT.Copy).then_inc(xnT_copied, 1)
                act.wait_ge(xnT_copied, 2 * (g + 1))
                act.activation(xnT_rep[:], xnT[:].rearrange("p k (i o) n -> p (k i) o n", o=1)
                               .to_broadcast([DH, 2 * G_IMG, VG, TOK]), ACT.Copy).then_inc(rep_ready, 1)
                for n in range(2 * QUADS):
                    q = n // QUADS
                    act.wait_ge(ring_filled, 4 + 10 * g + n + 1)
                    if n % QUADS == 0:
                        act.wait_ge(cat_ready, 2 * g + q + 1)
                    act.activation(qk_pad[:, n * G_IMG:(n + 1) * G_IMG, 1:1 + TOK],
                                   bank[n % 2][:, 0:G_IMG * TOK].rearrange("p (i n) -> p i n", n=TOK),
                                   ACT.Identity, bias=qk_bias[:, n:n + 1], scale=qk_scale[:, q:q + 1])\
                       .then_inc(ring_emptied, 1)

            def quads(g):
                act.wait_ge(cat_ready, 2 * g + 4)
                for hh in range(HEADS_PER_QUAD):
                    rows = slice(32 * hh, 32 * hh + 32)
                    last = act.activation(k_quad[rows, :, hh, :],
                                          qk[rows, QUADS:].rearrange("p i m n -> p (i m) n"), ACT.Copy)
                last.then_inc(quad_ready, 1)

            def exps(g, j):
                act.wait_ge(scores_read, TILES * g + j + 3)
                p = probs[:, j % 2].rearrange("p a b -> p (a b)")
                act.activation(p, p, ACT.Exp).then_inc(probs_ready, 1)

            def copy_pT(g, j):
                act.wait_ge(p_transposed, TILES * g + j + 1)
                act.activation(probsT[:, j % 2].rearrange("p a b -> p (a b)"), bank[7][0:VG * TOK, 0:VGROUPS * SPAN],
                               ACT.Copy).then_inc(pT_copied, 1)

            def attention(g, more):
                projections(g)
                if more:
                    pixels(g + 1, 4 + 10 * g + 6)
                quads(g)
                exps(g, 0)
                exps(g, 1)
                copy_pT(g, 0)
                exps(g, 2)
                copy_pT(g, 1)
                exps(g, 3)
                copy_pT(g, 2)
                copy_pT(g, 3)

            act.wait_ge(setup_ev, 19)
            pixels(0, 0)
            with act.Fori(0, GROUPS - 1) as g:
                attention(g, True)
            attention(GROUPS - 1, False)

            def route_T(t, i):
                act.wait_ge(x2T_filled, t + 3)
                act.activation(x2T[i][:].rearrange("p j n -> p (j n)"), bank[i][0:DH, 0:2 * ROWS], ACT.Copy)\
                   .then_inc(x2T_copied, 1)

            def route_exp(t, i):
                act.wait_ge(nmax_ready, t + 1)
                for r in range(2):
                    act.activation(escr[i][:, r, :], logit[i][:, r, :], ACT.Exp, bias=nmax[i][:, r:r + 1],
                                   accum_out=zsum[i][:, r:r + 1])
                    last = act.activation(etop[i][:, r, :], top8[i][:, r, 0:TOPK], ACT.Exp,
                                          bias=nmax[i][:, r:r + 1])
                last.then_inc(exp_done, 1)

            def route_rank(t, i):
                act.wait_ge(rank_filled, t + 1)
                act.activation(rank[:, bass.ds(t, 1), :].rearrange("p a b -> p (a b)"), bank[4][:, 0:256],
                               ACT.Copy).then_inc(rank_copied, 1)

            for i in range(2):
                route_T(i, i)
            with act.Fori(0, PAIRS - 1) as p:
                for i in range(2):
                    route_exp(2 * p + i, i)
                    route_rank(2 * p + i, i)
                    route_T(2 * p + 2 + i, i)
            route_exp(PAIRED - 2, 0)
            route_rank(PAIRED - 2, 0)
            route_T(PAIRED, 0)
            route_exp(PAIRED - 1, 1)
            route_rank(PAIRED - 1, 1)
            route_exp(PAIRED, 0)
            route_rank(PAIRED, 0)

            def experts(layer):
                cols = (256, 128)[layer]
                kp = (DH, RANK)[layer]
                width = (RANK, D)[layer]
                used = act.value_load(steps_used[0:1, layer:layer + 1], min_val=1, max_val=STEPS)
                with act.Fori(0, STEPS) as s, act.If(s < used):
                    for n in range(BODY + 1):
                        if n < BODY:
                            act.wait_ge(t_filled[layer], s * BODY + n + 1)
                            act.activation(xsT[n % 2][0:kp, 0:cols], bank[n % 2][0:kp, 0:cols], ACT.Copy)\
                               .then_inc(t_copied[layer], 1)
                        if n % 2 == 0 and n > 0:
                            q = n // 2 - 1
                            r = q // 2
                            act.wait_ge(y_filled[layer], s * (BODY // 2) + q + 1 + 2 * RING)
                            if q % 2 == 0:
                                act.wait_ge(y_stored[layer][r], 16 * s)
                            src = bank[2 + q % 2][:].rearrange("p (k w) -> p k w", k=2)[:, :, 0:width]
                            act.activation(os_[r][:, 2 * (q % 2):2 * (q % 2) + 2, 0:width], src, ACT.Copy)\
                               .then_inc(y_copied[layer], 1)
                            if q % 2 == 1:
                                act.wait_ge(y_copied[layer], s * (BODY // 2) + q + 3)
                                rows = wide_dram[bass.ds((s * RING + r) * (SB * ROWS), SB * ROWS), 0:width]
                                act.dma_start(rows.rearrange("(k p) d -> p k d", p=ROWS), os_[r][:, :, 0:width])\
                                   .then_inc(y_stored[layer][r], 16)

            act.wait_ge(plan_ev, 4)
            experts(0)
            experts(1)

        @block.vector
        def _(dve):
            step = [0]

            def link(ins):
                step[0] += 1
                ins.then_inc(dve_step, 1)
                dve.wait_ge(dve_step, step[0])

            dve.sem_inc(cat_ready, 2)
            dve.sem_inc(scores_read, 2)
            dve.sem_inc(o_read, 1)
            dve.sem_inc(res_used, 1)
            dve.sem_inc(logit_ready, 2)

            dve.wait_ge(consts, 2)
            dve.wait_ge(w_loaded, 16 * 14)
            link(dve.tensor_tensor(emb_sq[:], emb[:], emb[:], ALU.mult))
            link(dve.tensor_reduce(emb_n2[:], emb_sq[:], axis=AX.X, op=ALU.add))
            link(dve.tensor_scalar(emb_a[:], emb_n2[:], 1e-30, None, ALU.max))
            dve.tensor_scalar(emb_y[:].bitcast(I32), emb_a[:].bitcast(I32), 1, -1, ALU.logical_shift_right,
                              ALU.bitwise_xor).then_inc(emb_a_ready, 1)
            dve.wait_ge(emb_y_ready, 1)
            link(dve.tensor_tensor(emb_n1[:], emb_n2[:], emb_y[:], ALU.mult))
            link(dve.tensor_scalar(emb_n1[:], emb_n1[:], 1e-8, None, ALU.add))
            link(dve.reciprocal(emb_inv[:], emb_n1[:]))
            dve.tensor_tensor(emb_nrm[:], emb[:], emb_inv[:, :, None].to_broadcast([128, 2, DS]), ALU.mult)\
               .then_inc(embn_ready, 1)
            link(dve.tensor_scalar(part_b[:], part_i[:], 4, 1, ALU.logical_shift_right, ALU.bitwise_and))
            link(dve.tensor_copy(neigh[:], part_b[:]))
            link(dve.tensor_scalar(tmp_col[:], neigh[:], 0.0, SCALE * (1 + BETA), ALU.is_equal, ALU.mult))
            link(dve.scalar_tensor_tensor(qk_scale[:, 0:1], neigh[:], -SCALE * BETA, tmp_col[:], ALU.mult, ALU.add))
            link(dve.memset(qk_scale[:, 1:2], 1.0))

            fills = [0]

            def got():
                fills[0] += 1
                dve.wait_ge(setup_ps, fills[0])
                return bank[(fills[0] - 1) % 4]

            for kt in range(CH * HALVES):
                b = got()
                dve.tensor_copy(tok_wT[:, kt, :], b[:, 0:D]).then_inc(setup_ev, 1)
            for c in range(6):
                b = got()
                for j in range(2):
                    if c < 4:
                        src = b[0:DH, j * DH:(j + 1) * DH].rearrange("p (n o k) -> p n o k", o=1, k=HD)
                        last = dve.tensor_copy(w_qkT[:, j, c * 6:(c + 1) * 6], src.to_broadcast([DH, 6, 2, HD]))
                    else:
                        last = dve.tensor_copy(w_vT[:, j, (c - 4) * DH:(c - 3) * DH], b[0:DH, j * DH:(j + 1) * DH])
                last.then_inc(setup_ev, 1)
            b = got()
            dve.tensor_copy(wrT[:].rearrange("p r d -> p (r d)"), b[0:DS, 0:2 * D]).then_inc(setup_ev, 1)
            b = got()
            dve.tensor_copy(embT[:].rearrange("p r d -> p (r d)"), b[0:DS, 0:256]).then_inc(setup_ev, 1)
            b = got()
            for q in range(2):
                n = slice(q * QUADS, (q + 1) * QUADS)
                last = dve.tensor_scalar(qk_bias[:, n], b[:, n], qk_scale[:, q:q + 1], None, ALU.mult)
            last.then_inc(setup_ev, 1)
            b = got()
            dve.tensor_copy(v_bias[:], b[0:SPAN, 0:D]).then_inc(setup_ev, 1)
            b = got()
            dve.tensor_copy(r_mat[:].rearrange("p j n -> p (j n)"), b[0:DH, 0:512]).then_inc(setup_ev, 1)
            b = got()
            dve.tensor_copy(r_bias[:], b[:, 0:256]).then_inc(setup_ev, 1)
            dve.wait_ge(setup_ev, 18)
            for j in range(2):
                dve.tensor_scalar(w_qkT[:, j].rearrange("p a b c -> p (a b c)"),
                                  w_qkT[:, j].rearrange("p a b c -> p (a b c)"), g_col[:, j:j + 1], None, ALU.mult)
                dve.tensor_scalar(w_vT[:, j, :], w_vT[:, j, :], g_col[:, j:j + 1], None, ALU.mult)
            for m in range(G_IMG):
                dve.tensor_copy(vals[:, m, :, :, HD:VW],
                                head_mask[:, None, :, HD:VW].to_broadcast([VG * TOK, VGROUPS, VG, 1]))
            for b, v in ((bank[3], 1.0), (bank[4], 0.0), (bank[6], 0.0)):
                last = dve.memset(b[:], v)
            last.then_inc(setup_ev, 1)
            dve.wait_ge(cls_loaded, 32)
            dve.wait_ge(setup_ev, 19)

            def embedded(g1, f):
                dve.wait_ge(patch_done, 2 * g1 + f + 1)
                if f == 0:
                    dve.wait_ge(res_ready, g1)
                dve.tensor_tensor(h[:, 2 * f:2 * f + 2, :],
                                  bank[2 + 3 * f][0:SPAN, 0:2 * D].rearrange("p (t d) -> p t d", t=2),
                                  tok_bias[:, None, :].to_broadcast([SPAN, 2, D]), ALU.add).then_inc(h_ready, 1)
                dve.wait_ge(h_ready, 2 * g1 + f + 1)
                take(dve)
                for j in range(2 * f, 2 * f + 2):
                    last = dve.bn_stats(st[:, j, :], h[:, j, :])
                if f == 1:
                    last.then_inc(st_ready, 1)

            def variance(g1):
                dve.wait_ge(st_ready, 4 * g1 + 1)
                take(dve)
                for j in range(TILES):
                    last = dve.bn_aggr(mv[:, j, :], st[:, j, :])
                last.then_inc(st_ready, 1)
                dve.wait_ge(st_ready, 4 * g1 + 2)
                dve.tensor_scalar(va[:], mv[:, :, 1], 1 + LN_EPS, LN_EPS * LN_EPS, ALU.mult, ALU.add).then_inc(st_ready, 1)
                dve.wait_ge(st_ready, 4 * g1 + 3)
                dve.tensor_scalar(rr[:].bitcast(I32), va[:].bitcast(I32), 1, -1, ALU.logical_shift_right,
                                  ALU.bitwise_xor).then_inc(st_ready, 1)

            def normalise(g1):
                dve.wait_ge(rr_ready, g1 + 1)
                for j in range(TILES):
                    if j == 0:
                        dve.wait_ge(xn_transposed, 2 * g1)
                    dve.tensor_scalar(xn[:, j, :], h[:, j, :], mv[:, j, 0:1], rr[:, j:j + 1],
                                      ALU.subtract, ALU.mult).then_inc(xn_ready, 1)

            def values(g):
                mask = head_mask[:, None, :, 0:HD].to_broadcast([VG * TOK, 2 * VGROUPS, VG, HD])
                for f in range(G_IMG // 2):
                    dve.wait_ge(v_filled, 4 * g + f + 1)
                    src = bank[2 + 3 * (f % 2)][0:VG * TOK, 0:2 * D]
                    dve.tensor_tensor(vals[:, 2 * f:2 * f + 2].rearrange("p m a b c -> p (m a) b c")[:, :, :, 0:HD],
                                      src.rearrange("p (a b c) -> p a b c", b=VG, c=HD), mask, ALU.mult)\
                       .then_inc(v_masked, 1)

            def cat(g):
                n = QUADS * G_IMG
                for q in range(2):
                    dve.wait_ge(sums_ready, 2 * g + q + 1)
                    dve.scalar_tensor_tensor(
                        qk[:, q * QUADS:(q + 1) * QUADS].rearrange("p a b c -> p (a b) c"),
                        qk_sum[:, q * n:(q + 1) * n, :], neigh[:, 0:1], qk_pad[:, q * n:(q + 1) * n, 1:1 + TOK],
                        ALU.mult, ALU.add).then_inc(cat_ready, 1)

            def softmax_in(g, j):
                b = bank[4 + 2 * (j % 2)]
                dve.wait_ge(scores_done, TILES * g + j + 1)
                s = b[0:SPAN, 0:HEADS * TOK].rearrange("p (a b) -> p a b", b=TOK)
                dve.tensor_reduce(smax[:, j % 2, :], s, axis=AX.X, op=ALU.max).then_inc(smax_ready, 1)
                dve.wait_ge(smax_ready, TILES * g + j + 1)
                if j == 0:
                    dve.wait_ge(p_transposed, TILES * g)
                elif j >= 2:
                    dve.wait_ge(p_transposed, TILES * g + j - 1)
                dve.tensor_tensor(probs[:, j % 2], s, smax[:, j % 2, :, None].to_broadcast([SPAN, HEADS, TOK]),
                                  ALU.subtract).then_inc(scores_read, 1)

            def finish(g, j):
                dve.wait_ge(pv_done, TILES * g + j + 1)
                o = bank[3][0:SPAN, 256:256 + HEADS * VW].rearrange("p (a b) -> p a b", b=VW)
                dve.reciprocal(rsum[:], o[:, :, HD]).then_inc(fin_step, 1)
                dve.wait_ge(fin_step, TILES * g + j + 1)
                dve.tensor_tensor(att[:], o[:, :, 0:HD], rsum[:, :, None].to_broadcast([SPAN, HEADS, HD]),
                                  ALU.mult).then_inc(o_read, 1)
                dve.wait_ge(o_read, TILES * g + j + 2)
                if j == 0:
                    dve.wait_ge(res_ready, g + 1)
                    dve.wait_ge(stored, 32 * g)
                dve.tensor_tensor(h2[:, j, :], att[:].rearrange("p a b -> p (a b)"), h_res[:, j, :], ALU.add)\
                   .then_inc(h2_ready, 1)
                if j == TILES - 1:
                    dve.wait_ge(h2_ready, TILES * (g + 1))
                    dve.sem_inc(res_used, 1)

            def attention(g, more):
                values(g)
                cat(g)
                softmax_in(g, 0)
                softmax_in(g, 1)
                if more:
                    embedded(g + 1, 0)
                softmax_in(g, 2)
                finish(g, 0)
                if more:
                    embedded(g + 1, 1)
                    variance(g + 1)
                softmax_in(g, 3)
                finish(g, 1)
                finish(g, 2)
                if more:
                    normalise(g + 1)
                finish(g, 3)

            embedded(0, 0)
            embedded(0, 1)
            variance(0)
            normalise(0)
            with dve.Fori(0, GROUPS - 1) as g:
                attention(g, True)
            attention(GROUPS - 1, False)

            dve.wait_ge(h2r_loaded, 16)
            for t in range(TTILES):
                last = dve.bn_stats(st2[:, t, :], h2r[:, t, :])
            last.then_inc(st2_ready, 1)
            dve.wait_ge(st2_ready, 1)
            for t in range(TTILES):
                last = dve.bn_aggr(mv2[:, t, :], st2[:, t, :])
            last.then_inc(st2_ready, 1)
            dve.wait_ge(st2_ready, 2)
            dve.tensor_scalar(va2[:], mv2[:, :, 1], LN_EPS, None, ALU.add).then_inc(st2_ready, 1)
            dve.wait_ge(st2_ready, 3)
            dve.tensor_scalar(rs2[:].bitcast(I32), va2[:].bitcast(I32), 1, -1, ALU.logical_shift_right,
                              ALU.bitwise_xor).then_inc(st2_ready, 1)
            dve.wait_ge(rs2_ready, 1)

            def normalised(t, i):
                return dve.tensor_scalar(x2t[i][:], h2r[:, bass.ds(t, 1), :].rearrange("p t d -> p (t d)"),
                                         mv2[:, bass.ds(t, 1), 0:1].rearrange("p t o -> p (t o)"),
                                         rs2[:, bass.ds(t, 1)], ALU.subtract, ALU.mult)

            def route_x2(t, i):
                dve.wait_ge(x2T_filled, t + 1)
                normalised(t, i).then_inc(x2t_ready, 1)

            def route_top(t, i):
                dve.wait_ge(logit_filled, t + 1)
                dve.wait_ge(exp_done, t + 1)
                dve.tensor_tensor(logit[i][:].rearrange("p r n -> p (r n)"), bank[2 + i][:, 0:256], r_bias[:],
                                  ALU.add).then_inc(logit_ready, 1)
                dve.wait_ge(logit_ready, t + 3)
                take(dve)
                for r in range(2):
                    last = dve.max(top8[i][:, r, :], logit[i][:, r, :])
                last.then_inc(top_ready, 1)
                dve.wait_ge(top_ready, 2 * t + 1)
                dve.tensor_scalar(nmax[i][:], top8[i][:, :, 0], -1.0, None, ALU.mult).then_inc(nmax_ready, 1)
                for r in range(2):
                    last = dve.max_index(idx8[i][:, r, :], top8[i][:, r, :], logit[i][:, r, :])
                last.then_inc(top_ready, 1)
                dve.wait_ge(top_ready, 2 * t + 2)
                dve.tensor_copy(idxf[:, bass.ds(t, 1)].rearrange("p t r k -> p (t r) k"), idx8[i][:, :, 0:TOPK])\
                   .then_inc(idx_done, 1)
                dve.wait_ge(idx_done, t + 1)
                dve.wait_ge(hot_used, t + 1)
                dve.tensor_tensor(
                    hot[i][:].rearrange("p r k n -> p (r k) n"),
                    iota_n[:, None, :].to_broadcast([ROWS, 2 * TOPK, EXPERTS]),
                    idxf[:, bass.ds(t, 1)].rearrange("p t r k -> p (t r k)")[:, :, None].to_broadcast([ROWS, 2 * TOPK, EXPERTS]),
                    ALU.is_equal).then_inc(hot_ready, 1)

            def route_weights(t, i):
                dve.wait_ge(exp_done, t + 3)
                dve.tensor_reduce(s4[i][:], etop[i][:], axis=AX.X, op=ALU.add).then_inc(wt_step, 1)
                dve.wait_ge(wt_step, 4 * t + 1)
                dve.scalar_tensor_tensor(den[i][:], zsum[i][:], 1e-8, s4[i][:], ALU.mult, ALU.add).then_inc(wt_step, 1)
                dve.wait_ge(wt_step, 4 * t + 2)
                dve.reciprocal(iden[i][:], den[i][:]).then_inc(wt_step, 1)
                dve.wait_ge(wt_step, 4 * t + 3)
                dve.tensor_tensor(wts[:, bass.ds(t, 1)].rearrange("p t r k -> p (t r) k"), etop[i][:],
                                  iden[i][:, :, None].to_broadcast([ROWS, 2, TOPK]), ALU.mult).then_inc(wt_step, 1)

            for i in range(2):
                route_x2(i, i)
            with dve.Fori(0, PAIRS - 1) as p:
                for i in range(2):
                    route_top(2 * p + i, i)
                    route_x2(2 * p + 2 + i, i)
                    route_weights(2 * p + i, i)
            route_top(PAIRED - 2, 0)
            route_x2(PAIRED, 0)
            route_weights(PAIRED - 2, 0)
            route_top(PAIRED - 1, 1)
            route_weights(PAIRED - 1, 1)
            route_top(PAIRED, 0)
            route_weights(PAIRED, 0)

            dve.wait_ge(hot_used, TTILES + 2)
            cnt = bank[4][:, 0:256].rearrange("p (r n) -> p r n", r=2)
            link(dve.tensor_tensor(diag[:], cnt, ident[:, None, :].to_broadcast([128, 2, 128]), ALU.mult))
            link(dve.tensor_reduce(cum[:], diag[:], axis=AX.X, op=ALU.add))
            link(dve.tensor_scalar(cnt_i[:], cum[:], float(ROWS - 1), None, ALU.add))
            link(dve.tensor_scalar(nblk_i[:], cnt_i[:], 7, None, ALU.logical_shift_right))
            dve.tensor_copy(nblk[:], nblk_i[:]).then_inc(plan_ev, 1)
            dve.wait_ge(plan_ev, 1)
            dve.wait_ge(plan_ps, 1)
            link(dve.tensor_copy(cum[:], bank[5][:, 0:2]))
            link(dve.tensor_tensor(base_c[:], cum[:], nblk[:], ALU.subtract))
            link(dve.tensor_scalar(base_c[:], base_c[:], float(ROWS), None, ALU.mult))
            for r in range(2):
                last = dve.tensor_scalar(diag[:, r, :], ident[:], base_c[:, r:r + 1], None, ALU.mult)
            last.then_inc(plan_ev, 1)
            for r in range(2):
                last = dve.tensor_scalar(passed[:, r, :], iota_blk[:], cum[:, r:r + 1], None, ALU.is_ge)
            last.then_inc(plan_ev, 1)
            dve.wait_ge(plan_ps, 2)
            link(dve.tensor_copy(base_b[:], bank[6][:, 0:256]))
            dve.wait_ge(plan_ps, 3)
            link(dve.tensor_scalar(owner[:].rearrange("p r b -> p (r b)"), bank[7][0:1, 0:2 * BLOCKS],
                                   float(EXPERTS - 1), None, ALU.min))
            link(dve.tensor_scalar(step_has[:], bank[7][0:1, 0:2 * BLOCKS].rearrange("p (r s n) -> p r s n", r=2, n=BODY)[:, :, :, 0],
                                   float(EXPERTS), None, ALU.is_lt))
            link(dve.tensor_reduce(steps_f[:], step_has[:], axis=AX.X, op=ALU.add))
            dve.tensor_copy(steps_used[:], steps_f[:]).then_inc(plan_ev, 1)

            def slot(t, i, k):
                dve.tensor_tensor(srank[i][:], rank[:, bass.ds(t, 1), :].rearrange("p a b -> p (a b)"), base_b[:],
                                  ALU.add).then_inc(slot_step, 1)
                dve.wait_ge(slot_step, 3 * t + 1)
                for e in range(2 * TOPK):
                    r = e // TOPK
                    last = dve.scalar_tensor_tensor(
                        pick[:, e, :], iota_n[:],
                        idxf[:, bass.ds(t, 1)].rearrange("p t r k -> p (t r k)")[:, e:e + 1],
                        srank[i][:, r * EXPERTS:(r + 1) * EXPERTS], ALU.is_equal, ALU.mult,
                        accum_out=slotf[i][:, e:e + 1])
                last.then_inc(slot_step, 1)
                dve.wait_ge(slot_step, 3 * t + 2)
                dve.tensor_copy(slots[:, bass.ds(t, 1), :].rearrange("p a b -> p (a b)"), slotf[i][:]).then_inc(slot_step, 1)
                dve.wait_ge(scattered[i], 64 * k)
                normalised(t, i)
                dve.tensor_copy(slot_now[i][:], slotf[i][:]).then_inc(slot_ready, 1)

            with dve.Fori(0, PAIRS) as p:
                for i in range(2):
                    slot(2 * p + i, i, p)
            slot(PAIRED, 0, PAIRS)

            def combine(layer, t, i, k):
                width = (RANK, D)[layer]
                dve.wait_ge(gathered[layer][i], 64 * k)
                w = wts[:, bass.ds(t, 1)].rearrange("p t r k -> p (t r k)")
                for e in range(TOPK):
                    we = w[:, layer * TOPK + e:layer * TOPK + e + 1]
                    g = gat[i][:, e, 0:width]
                    if e == 0 and layer == 0:
                        ins = dve.tensor_scalar(acc[i][:, 0, 0:width], g, we, None, ALU.mult)
                    else:
                        prev = h2r[:, bass.ds(t, 1), :].rearrange("p t d -> p (t d)") if e == 0 else acc[i][:, (e - 1) % 2, 0:width]
                        dst = comb[i][:, 0:width] if e == TOPK - 1 else acc[i][:, e % 2, 0:width]
                        if e == TOPK - 1:
                            dve.wait_ge(comb_out[layer][i], (64 if layer == 0 else 16) * (k - 1))
                            if layer == 0:
                                dve.tensor_copy(slot_put[i][:], slots[:, bass.ds(t, 1), :].rearrange("p a b -> p (a b)"))
                        ins = dve.scalar_tensor_tensor(dst, g, we, prev, ALU.mult, ALU.add)
                    if e < TOPK - 1:
                        ins.then_inc(comb_step[layer], 1)
                        dve.wait_ge(comb_step[layer], (TOPK - 1) * t + e + 1)
                    else:
                        ins.then_inc(comb_ready[layer], 1)

            def indices(layer, t, i):
                dve.tensor_copy(slot_get[i][:], slots[:, bass.ds(t, 1), :].rearrange("p a b -> p (a b)"))\
                   .then_inc(idx_ready[layer], 1)

            def tiles(layer):
                for i in range(2):
                    indices(layer, i, i)
                with dve.Fori(0, PAIRS - 1) as p:
                    for i in range(2):
                        combine(layer, 2 * p + i, i, p + 1)
                        indices(layer, 2 * p + 2 + i, i)
                combine(layer, PAIRED - 2, 0, PAIRS)
                indices(layer, PAIRED, 0)
                combine(layer, PAIRED - 1, 1, PAIRS)
                combine(layer, PAIRED, 0, PAIRS + 1)

            for layer in range(2):
                tiles(layer)


_INS = ['x', 'cls_tok', 'L0_tok_W', 'L0_tok_b', 'L0_attn_qkv_w', 'L0_attn_qkv_b', 'L0_attn_ln_g', 'L0_attn_ln_b',
        'L0_ffn_f_know', 'L0_ffn_r_know', 'L0_ffn_W_fk', 'L0_ffn_b_fk', 'L0_ffn_W_rk', 'L0_ffn_b_rk',
        'L0_ffn_emb_fk', 'L0_ffn_emb_rk']


def kernel(**inputs):
    import concourse.bacc as bacc
    from concourse.bass_utils import run_bass_kernel_spmd

    nc = bacc.Bacc("TRN2", target_bir_lowering=False, num_devices=1)
    arrays, args = {}, []
    for name in _INS:
        a = np.ascontiguousarray(inputs[name])
        arrays[f"in_{name}"] = a
        args.append(nc.dram_tensor(f"in_{name}", a.shape, mybir.dt.from_np(a.dtype), kind="ExternalInput").ap())
    res = nc.dram_tensor("out_0", (TOKENS, D), F32, kind="ExternalOutput").ap()
    tower(nc, *args, res)
    r = run_bass_kernel_spmd(nc, [arrays], core_ids=[0])
    return r.results[0]["out_0"].reshape(BATCH, TOK, D)
```

```python
import numpy as np
import concourse.bass as bass
from concourse import mybir
from contextlib import ExitStack

F32 = mybir.dt.float32
BF16 = mybir.dt.bfloat16
I32 = mybir.dt.int32
U32 = mybir.dt.uint32
ALU = mybir.AluOpType
ACT = mybir.ActivationFunctionType
AX = mybir.AxisListType

BATCH, CH, IMG, PATCH = 64, 3, 96, 16
HP = IMG // PATCH
TOK = HP * HP + 1
D = 192
DH = D // 2
HEADS, HD = 12, 16
HEADS_PER_QUAD = 4
QUADS = HEADS // HEADS_PER_QUAD
HALVES = 2
LN_EPS = 1e-5
BETA = 0.2
SCALE = HD ** -0.5

G_IMG = 8
GROUPS = BATCH // G_IMG
RING_USES = 6
TILES = G_IMG // 2
SPAN = 64 + TOK
PAD = TOK + 2
SUB = G_IMG // 2 * CH * HP
LINE = PATCH * IMG
VG = 3
VGROUPS = HEADS // VG
VW = HD + 1

EXPERTS, RANK, DS, TOPK = 128, 128, 64, 4
TOKENS = BATCH * TOK
ROWS = 128
TTILES = -(-TOKENS // ROWS)
PTOK = TTILES * ROWS
LAST = TOKENS - (TTILES - 1) * ROWS
PAIRS = TTILES // 2
EARLY = (GROUPS - 1) * G_IMG * TOK // ROWS
MAX_BLOCKS = (PTOK * TOPK + EXPERTS * (ROWS - 1)) // ROWS
SB = 4
RING = 3
BODY = SB * RING
PAIRS_OF_STEP = BODY // 2
STEPS = -(-MAX_BLOCKS // BODY)
BLOCKS = STEPS * BODY
SLOTS = BLOCKS * ROWS


def tower(nc, x, cls_tok, tok_w, tok_b, qkv_w, qkv_b, ln_g, ln_b,
          f_know, r_know, w_fk, b_fk, w_rk, b_rk, emb_fk, emb_rk, out):
    ctx = ExitStack()
    with ctx:
        phase = [ctx]

        def sb(name, shape, dt=F32):
            return phase[0].enter_context(nc.sbuf_tensor(name, shape, dt))

        def sem(name):
            return ctx.enter_context(nc.semaphore(name))

        bank = [ctx.enter_context(nc.psum_tensor(f"bank{i}", [128, 512], F32)) for i in range(8)]

        h2_dram = nc.dram_tensor("h2_dram", [PTOK, D], F32, kind="Internal").ap()
        wide_dram = nc.dram_tensor("wide_dram", [SLOTS, D], F32, kind="Internal").ap()
        mid_dram = nc.dram_tensor("mid_dram", [SLOTS, RANK], F32, kind="Internal").ap()

        ident = sb("ident", [128, 128])
        ones = sb("ones", [128, 128])
        before = sb("before", [128, 128], BF16)
        after = sb("after", [128, 128], BF16)
        upto = sb("upto", [128, 128], BF16)
        ones_bf = sb("ones_bf", [128, 1], BF16)
        zeros_bf = sb("zeros_bf", [128, 256], BF16)
        head_mask = sb("head_mask", [VG * TOK, VG, VW])
        iota_n = sb("iota_n", [128, EXPERTS])
        iota_blk = sb("iota_blk", [128, BLOCKS])
        ZW = 1632
        zeros = sb("zeros", [128, ZW])
        part_i = sb("part_i", [128, 1], I32)
        part_b = sb("part_b", [128, 2], I32)
        part_head = sb("part_head", [128, 1])
        head_rows = sb("head_rows", [128, HEADS_PER_QUAD])
        neigh = sb("neigh", [128, 1])
        qk_scale = sb("qk_scale", [128, 2])
        tmp_col = sb("tmp_col", [128, 1])

        tok_nat = sb("tok_nat", [DH, 2, CH * PATCH * PATCH])
        tok_wT = sb("tok_wT", [128, CH * HALVES, D])
        tok_bias = sb("tok_bias", [SPAN, D])
        qkv_nat = sb("qkv_nat", [DH, 6, D])
        w_qkT = sb("w_qkT", [DH, 2, 2 * D])
        w_vT = sb("w_vT", [DH, 2, D])
        g_col = sb("g_col", [DH, 2])
        b_col = sb("b_col", [DH, 2])
        qk_brow = sb("qk_brow", [1, 2 * D])
        v_brow = sb("v_brow", [1, D])
        qk_bias = sb("qk_bias", [128, 2 * QUADS])
        v_bias = sb("v_bias", [SPAN, D])
        emb = sb("emb", [128, 2, DS])
        emb_sq = sb("emb_sq", [128, 2, DS])
        emb_n2 = sb("emb_n2", [128, 2])
        emb_a = sb("emb_a", [128, 2])
        emb_y = sb("emb_y", [128, 2])
        emb_t = sb("emb_t", [128, 2])
        emb_n1 = sb("emb_n1", [128, 2])
        emb_inv = sb("emb_inv", [128, 2])
        emb_nrm = sb("emb_nrm", [128, 2, DS])
        embT = sb("embT", [DS, 2, EXPERTS])
        wr_nat = sb("wr_nat", [DH, 2, 2, DS])
        wrT = sb("wrT", [DS, 2, D])
        br_col = sb("br_col", [DS, 2])
        r_mat = sb("r_mat", [DH, 2, 2 * EXPERTS])
        r_bias = sb("r_bias", [128, 2 * EXPERTS])

        h2r = sb("h2r", [ROWS, TTILES, D])
        mv2 = sb("mv2", [ROWS, TTILES, 2])
        rs2 = sb("rs2", [ROWS, TTILES])
        st2 = sb("st2", [ROWS, TTILES, 6])
        va2 = sb("va2", [ROWS, TTILES])
        rt2 = sb("rt2", [ROWS, TTILES])
        nb2 = sb("nb2", [ROWS, TTILES])
        x2t = [sb(f"x2t{i}", [ROWS, D]) for i in range(2)]
        idxf = sb("idxf", [ROWS, TTILES, 2, TOPK])
        wts = sb("wts", [ROWS, TTILES, 2, TOPK])
        owner = sb("owner", [1, 2, BLOCKS], I32)
        step_has = sb("step_has", [1, 2, STEPS])
        steps_f = sb("steps_f", [1, 2])
        steps_used = sb("steps_used", [1, 2], I32)
        slotf = [sb(f"slotf{i}", [ROWS, 2 * TOPK]) for i in range(2)]
        slot_now = [sb(f"slot_now{i}", [ROWS, 2 * TOPK], I32) for i in range(2)]
        slot_get = [sb(f"slot_get{i}", [ROWS, 2 * TOPK], I32) for i in range(2)]
        slot_put = [sb(f"slot_put{i}", [ROWS, 2 * TOPK], I32) for i in range(2)]
        acc = [sb(f"acc{i}", [ROWS, 2, D]) for i in range(2)]
        slots = sb("slots", [ROWS, TTILES, 2 * TOPK], I32)

        phase[0] = ExitStack()
        lines = [sb(f"lines{s}", [SUB, LINE]) for s in range(2)]
        patches = [sb(f"patches{s}", [SUB, HALVES, HP, 128]) for s in range(2)]
        pixT = sb("pixT", [128, HALVES, CH, G_IMG, 64])
        h = sb("h", [SPAN, TILES, D])
        h_res = sb("h_res", [SPAN, TILES, D])
        st = sb("st", [SPAN, TILES, 6])
        mv = sb("mv", [SPAN, TILES, 2])
        va = sb("va", [SPAN, TILES])
        rr = sb("rr", [SPAN, TILES])
        rt = sb("rt", [SPAN, TILES])
        xn = sb("xn", [SPAN, TILES, D])
        xnT = sb("xnT", [DH, 2, G_IMG, TOK])
        xnT_rep = sb("xnT_rep", [DH, 2 * G_IMG, VG, TOK])
        qk_pad = sb("qk_pad", [128, 2 * QUADS * G_IMG, PAD])
        qk_sum = sb("qk_sum", [128, 2 * QUADS * G_IMG, TOK])
        qk = sb("qk", [128, 2 * QUADS, G_IMG, TOK])
        k_quad = sb("k_quad", [128, QUADS * G_IMG, HEADS_PER_QUAD, TOK])
        vals = sb("vals", [VG * TOK, G_IMG, VGROUPS, VG, VW])
        smax = sb("smax", [SPAN, 2, HEADS])
        probs = sb("probs", [SPAN, 2, HEADS, TOK])
        probsT = sb("probsT", [VG * TOK, 2, VGROUPS, SPAN])
        rsum = sb("rsum", [SPAN, HEADS])
        att = sb("att", [SPAN, HEADS, HD])
        h2 = sb("h2", [SPAN, TILES, D])
        phase[0].close()

        phase[0] = ExitStack()
        x2T = [sb(f"x2T{i}", [DH, 2, ROWS]) for i in range(2)]
        logit = [sb(f"logit{i}", [ROWS, 2, EXPERTS]) for i in range(2)]
        escr = [sb(f"escr{i}", [ROWS, 2, EXPERTS]) for i in range(2)]
        top8 = [sb(f"top8_{i}", [ROWS, 2, 8]) for i in range(2)]
        idx8 = [sb(f"idx8_{i}", [ROWS, 2, 8], U32) for i in range(2)]
        nmax = [sb(f"nmax{i}", [ROWS, 2]) for i in range(2)]
        etop = [sb(f"etop{i}", [ROWS, 2, TOPK]) for i in range(2)]
        zsum = [sb(f"zsum{i}", [ROWS, 2]) for i in range(2)]
        s4 = [sb(f"s4_{i}", [ROWS, 2]) for i in range(2)]
        den = [sb(f"den{i}", [ROWS, 2]) for i in range(2)]
        iden = [sb(f"iden{i}", [ROWS, 2]) for i in range(2)]
        hot = [sb(f"hot{i}", [ROWS, 2, TOPK, EXPERTS], BF16) for i in range(2)]
        rank = sb("rank", [ROWS, TTILES, 2 * EXPERTS])
        cnt_i = sb("cnt_i", [128, 2], I32)
        nblk_i = sb("nblk_i", [128, 2], I32)
        nblk = sb("nblk", [128, 2], BF16)
        cum = sb("cum", [128, 2])
        base_c = sb("base_c", [128, 2])
        diag = sb("diag", [128, 2, 128])
        base_b = sb("base_b", [128, 2 * EXPERTS])
        passed = sb("passed", [128, 2, BLOCKS], BF16)
        srank = [sb(f"srank{i}", [ROWS, 2 * EXPERTS]) for i in range(2)]
        pick = sb("pick", [ROWS, 2 * TOPK, EXPERTS])

        xs = [sb(f"xs{r}", [ROWS, SB, D]) for r in range(RING)]
        fw = [sb(f"fw{r}", [128, SB, 256]) for r in range(RING)]
        xsT = [sb(f"xsT{i}", [128, 256]) for i in range(2)]
        os_ = [sb(f"os{r}", [ROWS, SB, D]) for r in range(RING)]
        gat = [sb(f"gat{i}", [ROWS, TOPK, D]) for i in range(2)]
        comb = [sb(f"comb{i}", [ROWS, D]) for i in range(2)]

        phase[0].close()
        phase[0] = ctx
        w_loaded = sem("w_loaded")
        tok_loaded = sem("tok_loaded")
        weights_ready = sem("weights_ready")
        cleared = sem("cleared")
        cls_loaded = sem("cls_loaded")
        pool_step = sem("pool_step")
        consts = sem("consts")
        zeroed = sem("zeroed")
        tail_zeroed = sem("tail_zeroed")
        setup_ps = sem("setup_ps")
        setup_ev = sem("setup_ev")
        dve_step = sem("dve_step")
        embn_ready = sem("embn_ready")
        lines_loaded = [sem(f"lines_loaded{s}") for s in range(2)]
        ring_filled = sem("ring_filled")
        ring_emptied = sem("ring_emptied")
        queries_filled = sem("queries_filled")
        queries_padded = sem("queries_padded")
        keys_padded = sem("keys_padded")
        patch_done = sem("patch_done")
        patches_ready = sem("patches_ready")
        rep_ready = sem("rep_ready")
        st_ready = sem("st_ready")
        rr_step = sem("rr_step")
        emb_y_step = sem("emb_y_step")
        rs2_step = sem("rs2_step")
        nb2_ready = sem("nb2_ready")
        taken = sem("taken")
        smax_ready = sem("smax_ready")
        fin_step = sem("fin_step")
        top_ready = sem("top_ready")
        wt_step = sem("wt_step")
        slot_step = sem("slot_step")
        comb_step = [sem(f"comb_step{p}") for p in range(2)]
        h_ready = sem("h_ready")
        res_ready = sem("res_ready")
        res_used = sem("res_used")
        xn_ready = sem("xn_ready")
        xn_transposed = sem("xn_transposed")
        xnT_copied = sem("xnT_copied")
        sums_ready = sem("sums_ready")
        cat_ready = sem("cat_ready")
        quad_ready = sem("quad_ready")
        v_filled = sem("v_filled")
        v_masked = sem("v_masked")
        scores_done = sem("scores_done")
        scores_read = sem("scores_read")
        probs_ready = sem("probs_ready")
        p_transposed = sem("p_transposed")
        pT_copied = sem("pT_copied")
        pv_done = sem("pv_done")
        o_read = sem("o_read")
        h2_ready = sem("h2_ready")
        stored = sem("stored")

        h2r_loaded = sem("h2r_loaded")
        st2_ready = sem("st2_ready")
        va2_step = sem("va2_step")
        x2t_ready = sem("x2t_ready")
        idx_done = sem("idx_done")
        x2T_filled = sem("x2T_filled")
        x2T_copied = sem("x2T_copied")
        logit_filled = sem("logit_filled")
        logit_ready = sem("logit_ready")
        nmax_ready = sem("nmax_ready")
        exp_done = sem("exp_done")
        hot_ready = sem("hot_ready")
        rank_filled = sem("rank_filled")
        rank_copied = sem("rank_copied")
        hot_used = sem("hot_used")
        plan_ps = sem("plan_ps")
        plan_ev = sem("plan_ev")
        slot_ready = sem("slot_ready")
        scattered = [sem(f"scattered{i}") for i in range(2)]

        xs_loaded = [[sem(f"xs_loaded{p}_{r}") for r in range(RING)] for p in range(2)]
        fw_loaded = [[sem(f"fw_loaded{p}_{r}") for r in range(RING)] for p in range(2)]
        last_loaded = [[sem(f"last_loaded{p}_{r}") for r in range(RING)] for p in range(2)]
        t_filled = [sem(f"t_filled{p}") for p in range(2)]
        t_copied = [sem(f"t_copied{p}") for p in range(2)]
        y_filled = [sem(f"y_filled{p}") for p in range(2)]
        y_copied = [sem(f"y_copied{p}") for p in range(2)]
        y_stored = [[sem(f"y_stored{p}_{i}") for i in range(RING)] for p in range(2)]

        idx_ready = [sem(f"idx_ready{p}") for p in range(2)]
        gathered = [[sem(f"gathered{p}_{i}") for i in range(2)] for p in range(2)]
        comb_ready = [sem(f"comb_ready{p}") for p in range(2)]
        comb_out = [[sem(f"comb_out{p}_{i}") for i in range(2)] for p in range(2)]

        def take(engine):
            engine.sem_inc(taken, 1)

        block = ctx.enter_context(nc.Block())

        lines_view = x.rearrange("b c (hp r) w -> (b c hp) (r w)", r=PATCH)
        f_view = f_know.rearrange("n (p j) r -> (n p) (j r)", j=2)
        r_view = r_know.rearrange("n r d -> (n r) d")
        PAIRED = 2 * PAIRS

        @block.sync
        def _(sp):
            sp.sem_inc(stored, 1)
            for i in range(2):
                sp.sem_inc(comb_out[1][i], 1)
            sp.dma_start(lines[0][:], lines_view[0:SUB, :]).then_inc(lines_loaded[0], 16)
            sp.dma_start(lines[1][:], lines_view[SUB:2 * SUB, :]).then_inc(lines_loaded[1], 16)
            n = 0
            sp.dma_start(tok_nat[:], tok_w.rearrange("(c p) k -> p c k", p=DH)).then_inc(tok_loaded, 16)
            for dst, src in (
                    (qkv_nat[:], qkv_w.rearrange("(c p) k -> p c k", p=DH)),
                    (tok_bias[:], tok_b.partition_broadcast(SPAN)),
                    (g_col[:], ln_g.rearrange("(j p) -> p j", p=DH)),
                    (b_col[:], ln_b.rearrange("(j p) -> p j", p=DH)),
                    (qk_brow[:], qkv_b[0:2 * D].rearrange("(o n) -> o n", o=1)),
                    (v_brow[:], qkv_b[2 * D:3 * D].rearrange("(o n) -> o n", o=1)),
                    (emb[:, 0, :], emb_fk), (emb[:, 1, :], emb_rk),
                    (wr_nat[:, 0], w_fk.rearrange("(j p) k -> p j k", p=DH)),
                    (wr_nat[:, 1], w_rk.rearrange("(j p) k -> p j k", p=DH)),
                    (br_col[:, 0:1], b_fk.rearrange("(p o) -> p o", o=1)),
                    (br_col[:, 1:2], b_rk.rearrange("(p o) -> p o", o=1))):
                sp.dma_start(dst, src, allow_slow_non_contiguous=True).then_inc(w_loaded, 16)
                n += 1
            sp.wait_ge(w_loaded, 16 * n)
            for a in range(2):
                sp.dma_start(tok_bias[64 * a:64 * a + 1, :], cls_tok[0]).then_inc(cls_loaded, 16)
            sp.wait_ge(consts, 1)
            sp.dma_start(h2_dram[TOKENS:PTOK, :], zeros[0:PTOK - TOKENS, 0:D]).then_inc(tail_zeroed, 16)

            def zero_slots(g):
                for dram, width in ((wide_dram, D), (mid_dram, RANK)):
                    k = SLOTS * width // 128 // ZW // GROUPS
                    view = dram.rearrange("(p r) d -> p (r d)", p=128).rearrange("p (k z) -> p k z", z=ZW)
                    sp.dma_start(view[:, bass.ds(g * k, k), :], zeros[:, None, :].to_broadcast([128, k, ZW]))\
                      .then_inc(zeroed, 16)

            def store_group(g):
                sp.wait_ge(h2_ready, TILES * (g + 1))
                for a in range(2):
                    rows = h2_dram[bass.ds(g * G_IMG * TOK, G_IMG * TOK), :]
                    view = rows.rearrange("(t a n) d -> n t a d", a=2, n=TOK)
                    sp.dma_start(view[:, :, a, :], h2[64 * a:64 * a + TOK]).then_inc(stored, 16)

            def load_lines(g1):
                for s in range(2):
                    sp.wait_ge(patches_ready, 2 * (g1 - 1) + s + 1)
                    row = g1 * (2 * SUB) + s * SUB
                    sp.dma_start(lines[s][:], lines_view[bass.ds(row, SUB), :]).then_inc(lines_loaded[s], 16)

            load_lines(1)
            load_lines(2)
            with sp.Fori(0, GROUPS - 3) as g:
                load_lines(g + 3)
                zero_slots(g)
                store_group(g)
            for g in (GROUPS - 3, GROUPS - 2):
                zero_slots(g)
                store_group(g)
            h2_tiles = h2_dram.rearrange("(t p) d -> p t d", p=ROWS)
            sp.wait_ge(stored, 32 * (GROUPS - 1) + 1)
            sp.dma_start(h2r[:, 0:EARLY, :], h2_tiles[:, 0:EARLY, :]).then_inc(h2r_loaded, 16)
            store_group(GROUPS - 1)
            sp.wait_ge(h2r_loaded, 16)

            sp.wait_ge(stored, 32 * GROUPS + 1)
            sp.wait_ge(tail_zeroed, 16)
            sp.dma_start(h2r[:, EARLY:, :], h2_tiles[:, EARLY:, :]).then_inc(h2r_loaded, 16)
            zero_slots(GROUPS - 1)

            def expert_loads(layer, filled):
                src = (wide_dram, mid_dram)[layer]
                width = (D, RANK)[layer]
                used = sp.value_load(steps_used[0:1, layer:layer + 1], min_val=1, max_val=STEPS)

                def owners(s):
                    _, experts = nc.values_load_multi_w_load_instructions(
                        owner[0:1, layer, bass.ds(s * BODY, BODY)], engines=[mybir.EngineType.SP],
                        min_val=0, max_val=EXPERTS - 1,
                        skip_runtime_bounds_check_because="owner is clamped to the experts where it is computed")
                    return experts

                def load_rows(s, r):
                    rows = src[bass.ds((s * RING + r) * (SB * ROWS), SB * ROWS), :]
                    sp.dma_start(xs[r][:, :, 0:width], rows.rearrange("(k p) d -> p k d", p=ROWS))\
                      .then_inc(xs_loaded[layer][r], 16)

                def load_weights(experts, r):
                    for k in range(SB - 1):
                        e = experts[r * SB + k]
                        if layer == 0:
                            sp.dma_start(fw[r][0:DH, k, :], f_view[bass.ds(e * DH, DH), :])\
                              .then_inc(fw_loaded[0][r], 16)
                        else:
                            sp.dma_start(fw[r][:, k, 0:D], r_view[bass.ds(e * RANK, RANK), :])\
                              .then_inc(fw_loaded[1][r], 16)

                experts = owners(0)
                for r in range(RING):
                    load_weights(experts, r)
                for i in range(2):
                    sp.wait_ge(filled[i], 64 * (PAIRS + (1 - i)))
                for r in range(RING):
                    load_rows(0, r)
                with sp.Fori(0, STEPS - 1) as s, sp.If(s + 1 < used):
                    experts = owners(s + 1)
                    for r in range(RING):
                        sp.wait_ge(y_filled[layer], 2 * (s * RING + r) + 2 + 2 * RING)
                        load_rows(s + 1, r)
                        load_weights(experts, r)

            sp.wait_ge(plan_ev, 4)
            expert_loads(0, scattered)
            sp.wait_ge(comb_ready[0], 1)
            expert_loads(1, comb_out[0])

            def store_out(t, i, n):
                sp.wait_ge(comb_ready[1], t + 1)
                sp.dma_start(out[bass.ds(t * ROWS, n), :], comb[i][0:n, :]).then_inc(comb_out[1][i], 16)

            with sp.Fori(0, PAIRS) as p:
                for i in range(2):
                    store_out(2 * p + i, i, ROWS)
            store_out(PAIRED, 0, LAST)
            for i in range(2):
                sp.wait_ge(comb_out[1][i], 16 * (PAIRS + (1 - i)) + 1)

        @block.gpsimd
        def _(pool):
            step = [0]

            def link(ins):
                step[0] += 1
                ins.then_inc(pool_step, 1)
                pool.wait_ge(pool_step, step[0])

            pool.memset(zeros[:], 0.0).then_inc(consts, 1)
            link(pool.memset(ident[:], 0.0))
            link(pool.affine_select(out=ident[:], in_=ident[:], compare_op=ALU.not_equal, fill=1.0,
                                    base=0, pattern=[[-1, 128]], channel_multiplier=1))
            link(pool.iota(part_i[:], pattern=[[0, 1]], base=0, channel_multiplier=1))
            pool.memset(ones[:], 1.0).then_inc(consts, 1)

            def head_masks():
                link(pool.memset(head_mask[:], 1.0))
                link(pool.affine_select(out=head_mask[:], in_=head_mask[:], compare_op=ALU.is_ge, fill=0.0,
                                        base=0, pattern=[[-TOK, VG], [0, VW]], channel_multiplier=1))
                pool.affine_select(out=head_mask[:], in_=head_mask[:], compare_op=ALU.is_ge, fill=0.0,
                                   base=TOK - 1, pattern=[[TOK, VG], [0, VW]], channel_multiplier=-1)\
                    .then_inc(consts, 1)

            def routing_constants():
                link(pool.memset(before[:], 1.0))
                link(pool.affine_select(out=before[:], in_=before[:], compare_op=ALU.is_gt, fill=0.0,
                                        base=0, pattern=[[1, 128]], channel_multiplier=-1))
                link(pool.memset(after[:], 1.0))
                link(pool.affine_select(out=after[:], in_=after[:], compare_op=ALU.is_ge, fill=0.0,
                                        base=0, pattern=[[-1, 128]], channel_multiplier=1))
                link(pool.memset(upto[:], 1.0))
                link(pool.affine_select(out=upto[:], in_=upto[:], compare_op=ALU.is_ge, fill=0.0,
                                        base=0, pattern=[[1, 128]], channel_multiplier=-1))
                link(pool.iota(iota_n[:], pattern=[[1, EXPERTS]], base=0, channel_multiplier=0,
                               allow_small_or_imprecise_dtypes=True))
                link(pool.iota(iota_blk[:], pattern=[[1, BLOCKS]], base=0, channel_multiplier=0,
                               allow_small_or_imprecise_dtypes=True))
                link(pool.memset(ones_bf[:], 1.0))
                pool.memset(zeros_bf[:], 0.0).then_inc(consts, 1)

            def regroup(g1, s):
                pool.wait_ge(lines_loaded[s], 16 * (g1 + 1))
                take(pool)
                if not (isinstance(g1, int) and g1 == 0):
                    pool.wait_ge(ring_filled, RING_USES * (g1 - 1) + 2 * s + 2)
                    take(pool)
                for half in range(HALVES):
                    w = LINE // HALVES
                    src = lines[s][:, half * w:(half + 1) * w].rearrange("q (r w c) -> q w r c", r=8, c=PATCH)
                    dst = patches[s][:, half].rearrange("q w (r c) -> q w r c", c=PATCH)
                    last = pool.tensor_copy(dst, src)
                last.then_inc(patches_ready, 1)

            def sums(g, k):
                n = QUADS * G_IMG
                q = 1 - k
                if k == 0:
                    pool.wait_ge(keys_padded, g + 1)
                else:
                    pool.wait_ge(ring_emptied, 2 + 4 + RING_USES * g + 2)
                    pool.wait_ge(queries_padded, g + 1)
                pool.wait_ge(cat_ready, 2 * g + k + 1)
                v = qk_pad[:, q * n:(q + 1) * n, :]
                pool.tensor_tensor(qk_sum[:, q * n:(q + 1) * n, :], v[:, :, 0:TOK], v[:, :, 2:PAD],
                                   ALU.add).then_inc(sums_ready, 1)

            def residual(g):
                pool.wait_ge(h_ready, 2 * (g + 1))
                pool.wait_ge(res_used, g + 1)
                pool.tensor_tensor(h_res[:], h[:], v_bias[:, None, :].to_broadcast([SPAN, TILES, D]),
                                   ALU.add).then_inc(res_ready, 1)

            def group(g, more):
                if more > 0:
                    sums(g + 1, 0)
                    sums(g + 1, 1)
                    residual(g + 1)
                if more > 2:
                    for s in range(2):
                        regroup(g + 3, s)

            for s in range(2):
                regroup(0, s)
            head_masks()
            for s in range(2):
                regroup(1, s)
            routing_constants()
            residual(0)
            sums(0, 0)
            sums(0, 1)
            for s in range(2):
                regroup(2, s)
            with pool.Fori(0, GROUPS - 3) as g:
                group(g, 3)
            group(GROUPS - 3, 2)
            group(GROUPS - 2, 1)

            pool.wait_ge(zeroed, 16 * 2 * GROUPS)

            def scatter_x2(t, i):
                pool.wait_ge(slot_ready, t + 1)
                take(pool)
                for e in range(TOPK):
                    pool.indirect_dma_start(wide_dram, bass.IndirectOffsetOnAxis(ap=slot_now[i][:, e:e + 1], axis=0),
                                            x2t[i][:], None).then_inc(scattered[i], 16)

            with pool.Fori(0, PAIRS) as p:
                for i in range(2):
                    scatter_x2(2 * p + i, i)
            scatter_x2(PAIRED, 0)

            def expert_rows(layer):
                width = (RANK, D)[layer]
                used = pool.value_load(steps_used[0:1, layer:layer + 1], min_val=1, max_val=STEPS)

                def last_owners(s):
                    _, experts = nc.values_load_multi_w_load_instructions(
                        owner[0:1, layer, bass.ds(s * BODY, BODY)].rearrange("p (r k) -> p r k", k=SB)[:, :, SB - 1],
                        engines=[mybir.EngineType.Pool], min_val=0, max_val=EXPERTS - 1,
                        skip_runtime_bounds_check_because="owner is clamped to the experts where it is computed")
                    return experts

                def load_matrix(r, e):
                    if layer == 0:
                        pool.dma_start(fw[r][0:DH, SB - 1, :], f_view[bass.ds(e * DH, DH), :])\
                            .then_inc(last_loaded[0][r], 16)
                    else:
                        pool.dma_start(fw[r][:, SB - 1, 0:D], r_view[bass.ds(e * RANK, RANK), :])\
                            .then_inc(last_loaded[1][r], 16)

                def store(s, r, pairs):
                    pool.wait_ge(y_copied[layer], pairs + 2 * r + 4)
                    rows = wide_dram[bass.ds((s * RING + r) * (SB * ROWS), SB * ROWS), 0:width]
                    pool.dma_start(rows.rearrange("(k p) d -> p k d", p=ROWS), os_[r][:, :, 0:width])\
                        .then_inc(y_stored[layer][r], 16)

                experts = last_owners(0)
                for r in range(RING):
                    load_matrix(r, experts[r])
                with pool.Fori(0, STEPS - 1) as s, pool.If(s + 1 < used):
                    experts = last_owners(s + 1)
                    for r in range(RING):
                        store(s, r, (s + 1) * PAIRS_OF_STEP)
                        load_matrix(r, experts[r])
                for r in range(RING):
                    store(used - 1, r, used * PAIRS_OF_STEP)
                for r in range(RING):
                    pool.wait_ge(y_stored[layer][r], used * 16)
                    take(pool)

            pool.wait_ge(plan_ev, 4)
            expert_rows(0)

            def gather(layer, t, i):
                pool.wait_ge(idx_ready[layer], t + 1)
                take(pool)
                for e in range(TOPK):
                    pool.indirect_dma_start(
                        gat[i][:, e, :], None, wide_dram,
                        bass.IndirectOffsetOnAxis(ap=slot_get[i][:, layer * TOPK + e:layer * TOPK + e + 1], axis=0))\
                        .then_inc(gathered[layer][i], 16)

            def scatter_mid(t, i):
                pool.wait_ge(comb_ready[0], t + 1)
                take(pool)
                for e in range(TOPK):
                    pool.indirect_dma_start(
                        mid_dram, bass.IndirectOffsetOnAxis(ap=slot_put[i][:, TOPK + e:TOPK + e + 1], axis=0),
                        comb[i][:, 0:RANK], None).then_inc(comb_out[0][i], 16)

            with pool.Fori(0, PAIRS) as p:
                for i in range(2):
                    gather(0, 2 * p + i, i)
                for i in range(2):
                    scatter_mid(2 * p + i, i)
            gather(0, PAIRED, 0)
            scatter_mid(PAIRED, 0)

            expert_rows(1)

            with pool.Fori(0, PAIRS) as p:
                for i in range(2):
                    gather(1, 2 * p + i, i)
            gather(1, PAIRED, 0)
            for i in range(2):
                pool.wait_ge(gathered[1][i], 64 * (PAIRS + (1 - i)))

        @block.tensor
        def _(pe):
            pe.sem_inc(x2T_filled, 2)
            pe.sem_inc(p_transposed, 2)
            pe.sem_inc(hot_used, 2)
            for layer in range(2):
                pe.sem_inc(y_filled[layer], 2 * RING)

            fills = [0]
            fill_banks = [bank[(3, 4, 6, 7)[n % 4]] for n in range(15)] + [bank[7], bank[0], bank[1]]

            def filled(ins):
                fills[0] += 1
                ins.then_inc(setup_ps, 1)

            def room():
                if fills[0] >= 4:
                    pe.wait_ge(setup_ev, fills[0] - 3)
                return fill_banks[fills[0]]

            def token_weights():
                for kt in range(CH * HALVES):
                    b = room()
                    for c in range(2):
                        last = pe.transpose(b[:, c * DH:(c + 1) * DH], tok_nat[:, c, kt * 128:(kt + 1) * 128],
                                            ident[0:DH, 0:DH])
                    filled(last)

            def projection_weights():
                for c in range(6):
                    b = room()
                    for j in range(2):
                        last = pe.transpose(b[0:DH, j * DH:(j + 1) * DH], qkv_nat[:, c, j * DH:(j + 1) * DH],
                                            ident[0:DH, 0:DH])
                    filled(last)
                b = room()
                for r in range(2):
                    for j in range(2):
                        last = pe.transpose(b[0:DS, (2 * r + j) * DH:(2 * r + j + 1) * DH], wr_nat[:, r, j, :],
                                            ident[0:DH, 0:DH])
                filled(last)

            def projection_biases():
                b = room()
                pe.wait_ge(setup_ev, 13)
                for n in range(QUADS):
                    cols = slice(n * 128, (n + 1) * 128)
                    for j in range(2):
                        pe.matmul(b[:, n:n + 1], w_qkT[:, j, cols], b_col[:, j:j + 1], start=j == 0, stop=False)
                    last = pe.matmul(b[:, n:n + 1], qk_brow[0:1, cols], ones[0:1, 0:1], start=False, stop=True)
                filled(last)
                b = room()
                for j in range(2):
                    pe.matmul(b[0:SPAN, 0:D], b_col[:, j:j + 1].to_broadcast([DH, SPAN]), w_vT[:, j, :],
                              start=j == 0, stop=False)
                filled(pe.matmul(b[0:SPAN, 0:D], ones[0:1, 0:SPAN], v_brow[:], start=False, stop=True))

            def router():
                b = room()
                pe.wait_ge(embn_ready, 1)
                for r in range(2):
                    last = pe.transpose(b[0:DS, r * 128:(r + 1) * 128], emb_nrm[:, r, :], ident[:])
                filled(last)
                pe.wait_ge(ring_emptied, 2 + 4)
                b = room()
                pe.wait_ge(setup_ev, 16)
                for r in range(2):
                    for j in range(2):
                        last = pe.matmul(b[0:DH, j * 256 + r * 128:j * 256 + (r + 1) * 128],
                                         wrT[:, r, j * DH:(j + 1) * DH], embT[:, r, :], start=True, stop=True)
                filled(last)
                b = room()
                for r in range(2):
                    last = pe.matmul(b[:, r * 128:(r + 1) * 128], br_col[:, r:r + 1].to_broadcast([DS, 128]),
                                     embT[:, r, :], start=True, stop=True)
                filled(last)

            def to_pixels(g1, u0, s):
                pe.wait_ge(patches_ready, 2 * g1 + s + 1)
                for half in range(HALVES):
                    u = 2 * s + half
                    pe.wait_ge(ring_emptied, u0 + u + 1)
                    cols = bank[u % 2][:, 0:HP * SUB].rearrange("p (k b c y v) -> p k v b c y", k=CH, b=4, c=CH, y=HP)
                    for w in range(HP):
                        last = pe.transpose(cols[:, w % CH, w // CH], patches[s][:, half, w, :], ident[0:SUB, 0:SUB])
                    last.then_inc(ring_filled, 1)

            def embed(g1, j, first):
                f, t = divmod(j, 2)
                if j == 0:
                    pe.wait_ge(ring_emptied, RING_USES * g1 + 4 + 2)
                if t == 0 and not first:
                    pe.wait_ge(xnT_copied, 2 * (g1 - 1) + f + 1)
                for kt in range(CH * HALVES):
                    c, half = divmod(kt, HALVES)
                    last = pe.matmul(bank[2 + 3 * f][:, t * D:(t + 1) * D],
                                     pixT[:, half, c, 2 * j:2 * j + 2, :].rearrange("p a n -> p (a n)"),
                                     tok_wT[:, kt, :], start=kt == 0, stop=kt == CH * HALVES - 1)
                if t == 1:
                    last.then_inc(patch_done, 1)

            def turn_xn(g):
                for j in range(TILES):
                    f, t = divmod(j, 2)
                    pe.wait_ge(xn_ready, TILES * g + j + 1)
                    if t == 0 and not (isinstance(g, int) and g == 0):
                        pe.wait_ge(v_masked, 4 * g - 1 + f)
                    for k in range(2):
                        last = pe.transpose(bank[2 + 3 * f][0:DH, k * 256 + t * 128:k * 256 + t * 128 + SPAN],
                                            xn[:, j, k * DH:(k + 1) * DH], ident[0:SPAN, 0:SPAN])
                    if t == 1:
                        last.then_inc(xn_transposed, 1)

            def project(g, n):
                cols = slice((QUADS - 1 - n) * 128, (QUADS - n) * 128)
                if n == 0:
                    pe.wait_ge(xnT_copied, 2 * (g + 1))
                if n < 2:
                    pe.wait_ge(ring_emptied, 4 + RING_USES * g + n + 1)
                else:
                    pe.wait_ge(pT_copied, TILES * g + 1)
                dst = (bank[0], bank[1], bank[7])[n]
                for j in range(2):
                    last = pe.matmul(dst[:, 0:G_IMG * TOK], w_qkT[:, j, cols],
                                     xnT[:, j].rearrange("p i n -> p (i n)"), start=j == 0, stop=j == 1)
                last.then_inc(ring_filled if n < 2 else queries_filled, 1)

            def project_values(g, embedding):
                pe.wait_ge(rep_ready, g + 1)
                for m in range(G_IMG):
                    f, t = divmod(m, 2)
                    if t == 0 and f >= 2:
                        pe.wait_ge(v_masked, 4 * g + f - 1)
                    elif t == 0 and embedding:
                        pe.wait_ge(h_ready, 2 * (g + 1) + f + 1)
                    for j in range(2):
                        last = pe.matmul(bank[2 + 3 * (f % 2)][0:VG * TOK, t * D:(t + 1) * D],
                                         xnT_rep[:, j * G_IMG + m].rearrange("p r n -> p (r n)"),
                                         w_vT[:, j, :], start=j == 0, stop=j == 1)
                    if t == 1:
                        last.then_inc(v_filled, 1)

            def scores(g, j):
                if j == 0:
                    pe.wait_ge(quad_ready, g + 1)
                    pe.wait_ge(cat_ready, 2 * g + 4)
                pe.wait_ge(scores_read, TILES * g + j + 1)
                b = bank[4 + 2 * (j % 2)]
                for a in range(2):
                    for i in range(QUADS):
                        w = HEADS_PER_QUAD * TOK
                        last = pe.matmul(b[64 * a:64 * a + TOK, i * w:(i + 1) * w], qk[:, i, 2 * j + a, :],
                                         k_quad[:, i * G_IMG + 2 * j + a].rearrange("p a b -> p (a b)"),
                                         start=True, stop=True)
                last.then_inc(scores_done, 1)

            def turn(g, j):
                pe.wait_ge(probs_ready, TILES * g + j + 1)
                pe.wait_ge(pT_copied, TILES * g + j + 1)
                for v in range(VGROUPS):
                    last = pe.transpose(bank[7][0:VG * TOK, v * SPAN:(v + 1) * SPAN],
                                        probs[:, j % 2, VG * v:VG * (v + 1), :].rearrange("p a b -> p (a b)"),
                                        ident[0:SPAN, 0:SPAN])
                last.then_inc(p_transposed, 1)

            def attend(g, j):
                pe.wait_ge(pT_copied, TILES * g + j + 2)
                pe.wait_ge(o_read, TILES * g + j + 1)
                if j == 0:
                    pe.wait_ge(v_masked, 4 * (g + 1))
                for a in range(2):
                    for v in range(VGROUPS):
                        last = pe.matmul(bank[3][64 * a:64 * a + TOK, 256 + v * VG * VW:256 + (v + 1) * VG * VW],
                                         probsT[:, j % 2, v, 64 * a:64 * a + TOK],
                                         vals[:, 2 * j + a, v].rearrange("p a b -> p (a b)"),
                                         start=True, stop=True)
                last.then_inc(pv_done, 1)

            def attention(g, more):
                ring = 4 + RING_USES * (g + 1) + 2
                scores(g, 0)
                scores(g, 1)
                if more > 0:
                    turn_xn(g + 1)
                turn(g, 0)
                scores(g, 2)
                if more > 0:
                    project(g + 1, 0)
                turn(g, 1)
                scores(g, 3)
                if more > 0:
                    project(g + 1, 1)
                attend(g, 0)
                turn(g, 2)
                attend(g, 1)
                turn(g, 3)
                attend(g, 2)
                if more > 0:
                    project(g + 1, 2)
                attend(g, 3)
                if more > 1:
                    for s in range(2):
                        to_pixels(g + 2, ring, s)
                    for j in range(TILES):
                        embed(g + 2, j, False)
                if more > 0:
                    project_values(g + 1, more > 1)

            pe.wait_ge(consts, 2)
            pe.wait_ge(tok_loaded, 16)
            token_weights()
            pe.wait_ge(w_loaded, 16 * 12)
            projection_weights()
            for s in range(2):
                to_pixels(0, 0, s)
            projection_biases()
            for j in range(TILES):
                embed(0, j, True)
            router()
            pe.wait_ge(weights_ready, 1)
            pe.wait_ge(setup_ev, 18)
            turn_xn(0)
            for n in range(QUADS):
                project(0, n)
            for s in range(2):
                to_pixels(1, 4 + 2, s)
            for j in range(TILES):
                embed(1, j, False)
            project_values(0, True)
            with pe.Fori(0, GROUPS - 2) as g:
                attention(g, 2)
            attention(GROUPS - 2, 1)
            attention(GROUPS - 1, 0)

            pe.wait_ge(consts, 4)
            pe.wait_ge(o_read, TILES * GROUPS + 1)
            pe.wait_ge(scores_read, TILES * GROUPS + 2)
            pe.matmul(bank[4][:, 0:256], zeros_bf[:, 0:128], zeros_bf[:], start=True, stop=False,
                      skip_group_check=True)

            def route_transpose(t, i):
                pe.wait_ge(x2t_ready, t + 1)
                pe.wait_ge(x2T_copied, t + 1)
                for j in range(2):
                    last = pe.transpose(bank[i][0:DH, j * ROWS:(j + 1) * ROWS], x2t[i][:, j * DH:(j + 1) * DH],
                                        ident[:])
                last.then_inc(x2T_filled, 1)

            def route_logits(t, i):
                pe.wait_ge(x2T_copied, t + 3)
                pe.wait_ge(logit_ready, t + 1)
                for j in range(2):
                    last = pe.matmul(bank[2 + i][:, 0:256], x2T[i][:, j, :], r_mat[:, j, :],
                                     start=j == 0, stop=j == 1)
                last.then_inc(logit_filled, 1)

            def route(t, i, then):
                pe.wait_ge(hot_ready, t + 1)
                for e in range(TOPK):
                    last = pe.matmul(bank[4][:, 0:256], before[:], hot[i][:, :, e, :], start=False, stop=False,
                                     skip_group_check=True)
                last.then_inc(rank_filled, 1)
                if then is not None:
                    route_transpose(then, i)
                pe.wait_ge(rank_copied, t + 1)
                for e in range(TOPK):
                    last = pe.matmul(bank[4][:, 0:256], after[:], hot[i][:, :, e, :], start=False, stop=False,
                                     skip_group_check=True)
                last.then_inc(hot_used, 1)
                if then is not None:
                    route_logits(then, i)

            for i in range(2):
                route_transpose(i, i)
                route_logits(i, i)
            with pe.Fori(0, PAIRS - 1) as p:
                for i in range(2):
                    route(2 * p + i, i, 2 * p + 2 + i)
            route(PAIRED - 2, 0, PAIRED)
            route(PAIRED - 1, 1, None)
            route(PAIRED, 0, None)

            pe.wait_ge(plan_ev, 1)
            for r in range(2):
                last = pe.matmul(bank[5][:, r:r + 1], upto[:], nblk[:, r:r + 1], start=True, stop=True)
            last.then_inc(plan_ps, 1)
            pe.wait_ge(plan_ev, 2)
            for r in range(2):
                last = pe.matmul(bank[6][:, r * 128:(r + 1) * 128], ones[:], diag[:, r, :], start=True, stop=True)
            last.then_inc(plan_ps, 1)
            pe.wait_ge(plan_ev, 3)
            for r in range(2):
                last = pe.matmul(bank[7][0:1, r * BLOCKS:(r + 1) * BLOCKS], ones_bf[:], passed[:, r, :],
                                 start=True, stop=True)
            last.then_inc(plan_ps, 1)
            pe.wait_ge(plan_ev, 4)

            def experts(layer):
                parts = (2, 1)[layer]
                kp = (DH, RANK)[layer]
                width = (RANK, D)[layer]
                filled_ = t_filled[layer]
                used = pe.value_load(steps_used[0:1, layer:layer + 1], min_val=1, max_val=STEPS)

                def transposed(s, n):
                    r, k = divmod(n, SB)
                    if k == 0:
                        pe.wait_ge(xs_loaded[layer][r], 16 * (s + 1))
                    pe.wait_ge(t_copied[layer], s * BODY + n + 1)
                    for j in range(parts):
                        src = xs[r][:, k, j:D:2] if layer == 0 else xs[r][:, k, 0:RANK]
                        last = pe.transpose(bank[n % 2][0:kp, j * ROWS:(j + 1) * ROWS], src, ident[:])
                    last.then_inc(filled_, 1)

                transposed(0, 0)
                with pe.Fori(0, STEPS) as s, pe.If(s < used):
                    for n in range(BODY):
                        r, k = divmod(n, SB)
                        if n + 1 < BODY:
                            transposed(s, n + 1)
                        else:
                            with pe.If(s + 1 < used):
                                transposed(s + 1, 0)
                        if k == 0:
                            pe.wait_ge(fw_loaded[layer][r], 16 * (SB - 1) * (s + 1))
                        if k == SB - 1:
                            pe.wait_ge(last_loaded[layer][r], 16 * (s + 1))
                        if k % 2 == 0:
                            pe.wait_ge(y_copied[layer], (s + 1) * PAIRS_OF_STEP + n // 2 + 1)
                        pe.wait_ge(t_copied[layer], s * BODY + n + 3)
                        dst = bank[2 + (n // 2) % 2][:, (k % 2) * 256:(k % 2) * 256 + width]
                        for j in range(parts):
                            w = fw[r][0:kp, k, j * 128:(j + 1) * 128] if layer == 0 else fw[r][:, k, 0:D]
                            last = pe.matmul(dst, xsT[n % 2][0:kp, j * ROWS:(j + 1) * ROWS], w,
                                             start=j == 0, stop=j == parts - 1)
                        if k % 2 == 1:
                            last.then_inc(y_filled[layer], 1)

            experts(0)
            experts(1)

        @block.scalar
        def _(act):
            act.sem_inc(ring_emptied, 2)
            act.sem_inc(pT_copied, 1)
            act.sem_inc(x2T_copied, 2)
            act.sem_inc(exp_done, 2)
            for layer in range(2):
                act.sem_inc(t_copied[layer], 2)
            act.wait_ge(consts, 1)
            for a, n, w in ((pixT[:].rearrange("p a b c d -> p (a b c) d"), HALVES * CH * G_IMG, 64),
                            (qk_pad[:], 2 * QUADS * G_IMG, PAD)):
                act.activation(a, zeros[:, None, 0:w].to_broadcast([128, n, w]), ACT.Copy)\
                   .then_inc(cleared, 1)
            act.wait_ge(cleared, 2)

            def pixels(g1, u0):
                for u in range(4):
                    s, half = divmod(u, 2)
                    act.wait_ge(ring_filled, u0 + u + 1)
                    if u == 0 and not (isinstance(g1, int) and g1 == 0):
                        act.wait_ge(patch_done, 2 * g1)
                    src = bank[u % 2][:, 0:HP * SUB].rearrange("p (k b n) -> p k b n", k=CH, b=4)
                    dst = pixT[:, half, :, s * 4:(s + 1) * 4, 1:TOK]
                    act.activation(dst, src, ACT.Copy).then_inc(ring_emptied, 1)

            def copy_xnT(g):
                for f in range(2):
                    act.wait_ge(xn_transposed, 2 * g + f + 1)
                    src = bank[2 + 3 * f][0:DH, :].rearrange("p (k a n) -> p k a n", k=2, a=4)[:, :, :, 0:TOK]
                    act.activation(xnT[:, :, 4 * f:4 * f + 4, :], src, ACT.Copy).then_inc(xnT_copied, 1)

            def replicate(g):
                act.wait_ge(xnT_copied, 2 * (g + 1))
                act.activation(xnT_rep[:], xnT[:].rearrange("p k (i o) n -> p (k i) o n", o=1)
                               .to_broadcast([DH, 2 * G_IMG, VG, TOK]), ACT.Copy).then_inc(rep_ready, 1)

            def pad(g, m):
                n = (5 - m) // 2
                q = m // QUADS
                if m == 5:
                    act.wait_ge(cat_ready, 2 * g + 1)
                if m == 2:
                    act.wait_ge(cat_ready, 2 * g + 2)
                if m % 2 == 1:
                    act.wait_ge(ring_filled, 4 + RING_USES * g + n + 1)
                src = bank[n][64 * (m % 2):64 * (m % 2) + 64, 0:G_IMG * TOK].rearrange("p (i n) -> p i n", n=TOK)
                for c in range(2):
                    half = slice(64 * c, 64 * c + 64)
                    ins = act.activation(qk_pad[half, m * G_IMG:(m + 1) * G_IMG, 1:1 + TOK], src, ACT.Identity,
                                         bias=qk_bias[half, m:m + 1], scale=qk_scale[half, q:q + 1])
                if m == 3:
                    ins.then_inc(keys_padded, 1)
                elif m % 2 == 0:
                    ins.then_inc(ring_emptied, 1)

            def quads(g):
                act.wait_ge(cat_ready, 2 * g + 3)
                for hh in range(HEADS_PER_QUAD):
                    last = act.activation(k_quad[:, :, hh, :], qk[:, QUADS:].rearrange("p i m n -> p (i m) n"),
                                          ACT.Copy, scale=head_rows[:, hh:hh + 1])
                last.then_inc(quad_ready, 1)

            def exps(g, j):
                act.wait_ge(scores_read, TILES * g + j + 3)
                p = probs[:, j % 2].rearrange("p a b -> p (a b)")
                act.activation(p, p, ACT.Exp).then_inc(probs_ready, 1)

            def copy_pT(g, j):
                act.wait_ge(p_transposed, TILES * g + j + 3)
                act.activation(probsT[:, j % 2].rearrange("p a b -> p (a b)"), bank[7][0:VG * TOK, 0:VGROUPS * SPAN],
                               ACT.Copy).then_inc(pT_copied, 1)

            def attention(g, more):
                exps(g, 0)
                if more > 0:
                    copy_xnT(g + 1)
                exps(g, 1)
                copy_pT(g, 0)
                if more > 0:
                    pad(g + 1, 5)
                copy_pT(g, 1)
                exps(g, 2)
                if more > 0:
                    pad(g + 1, 4)
                exps(g, 3)
                copy_pT(g, 2)
                if more > 0:
                    pad(g + 1, 3)
                copy_pT(g, 3)
                if more > 0:
                    pad(g + 1, 2)
                if more > 1:
                    pixels(g + 2, 4 + RING_USES * (g + 1) + 2)
                if more > 0:
                    replicate(g + 1)
                    quads(g + 1)

            pixels(0, 0)
            act.wait_ge(weights_ready, 1)
            copy_xnT(0)
            for m in (5, 4, 3, 2):
                pad(0, m)
            pixels(1, 4 + 2)
            replicate(0)
            quads(0)
            with act.Fori(0, GROUPS - 2) as g:
                attention(g, 2)
            attention(GROUPS - 2, 1)
            attention(GROUPS - 1, 0)

            def route_T(t, i):
                act.wait_ge(x2T_filled, t + 3)
                act.activation(x2T[i][:].rearrange("p j n -> p (j n)"), bank[i][0:DH, 0:2 * ROWS], ACT.Copy)\
                   .then_inc(x2T_copied, 1)

            def route_exp(t, i):
                act.wait_ge(nmax_ready, t + 1)
                for r in range(2):
                    act.activation(escr[i][:, r, :], logit[i][:, r, :], ACT.Exp, bias=nmax[i][:, r:r + 1],
                                   accum_out=zsum[i][:, r:r + 1])
                    last = act.activation(etop[i][:, r, :], top8[i][:, r, 0:TOPK], ACT.Exp,
                                          bias=nmax[i][:, r:r + 1])
                last.then_inc(exp_done, 1)

            def route_rank(t, i):
                act.wait_ge(rank_filled, t + 1)
                act.activation(rank[:, bass.ds(t, 1), :].rearrange("p a b -> p (a b)"), bank[4][:, 0:256],
                               ACT.Copy).then_inc(rank_copied, 1)

            def route_x2(t, i):
                act.wait_ge(x2T_filled, t + 1)
                act.activation(x2t[i][:], h2r[:, bass.ds(t, 1), :].rearrange("p t d -> p (t d)"), ACT.Identity,
                               bias=nb2[:, bass.ds(t, 1)], scale=rs2[:, bass.ds(t, 1)]).then_inc(x2t_ready, 1)

            def route(t, i, transposed, normalised):
                route_exp(t, i)
                route_rank(t, i)
                if transposed is not None:
                    route_T(transposed, i)
                if normalised is not None:
                    route_x2(normalised, i)

            act.wait_ge(nb2_ready, 1)
            for i in range(2):
                route_x2(i, i)
            for i in range(2):
                route_T(i, i)
                route_x2(2 + i, i)
            act.wait_ge(nb2_ready, 2)
            with act.Fori(0, PAIRS - 2) as p:
                for i in range(2):
                    route(2 * p + i, i, 2 * p + 2 + i, 2 * p + 4 + i)
            route(PAIRED - 4, 0, PAIRED - 2, PAIRED)
            route(PAIRED - 3, 1, PAIRED - 1, None)
            route(PAIRED - 2, 0, PAIRED, None)
            route(PAIRED - 1, 1, None, None)
            route(PAIRED, 0, None, None)

            def experts(layer):
                cols = (256, 128)[layer]
                kp = (DH, RANK)[layer]
                used = act.value_load(steps_used[0:1, layer:layer + 1], min_val=1, max_val=STEPS)
                with act.Fori(0, STEPS) as s, act.If(s < used):
                    for n in range(BODY):
                        act.wait_ge(t_filled[layer], s * BODY + n + 1)
                        act.activation(xsT[n % 2][0:kp, 0:cols], bank[n % 2][0:kp, 0:cols], ACT.Copy)\
                           .then_inc(t_copied[layer], 1)

            act.wait_ge(plan_ev, 4)
            experts(0)
            experts(1)

        @block.vector
        def _(dve):
            step = [0]

            def link(ins):
                step[0] += 1
                ins.then_inc(dve_step, 1)
                dve.wait_ge(dve_step, step[0])

            dve.sem_inc(cat_ready, 2)
            dve.sem_inc(scores_read, 2)
            dve.sem_inc(o_read, 1)
            dve.sem_inc(res_used, 1)
            dve.sem_inc(logit_ready, 2)
            for layer in range(2):
                dve.sem_inc(y_copied[layer], 2 + PAIRS_OF_STEP)

            def root_guess(y, a, steps):
                dve.tensor_scalar(y.bitcast(I32), a.bitcast(I32), -0.5, float(0x5f3759df), ALU.mult, ALU.add)\
                   .then_inc(steps, 1)

            def root_newton(y, a, t, steps, n, i):
                dve.wait_ge(steps, n + 3 * i + 1)
                dve.tensor_tensor(t, y, y, ALU.mult).then_inc(steps, 1)
                dve.wait_ge(steps, n + 3 * i + 2)
                dve.scalar_tensor_tensor(t, t, -0.5, a, ALU.mult, ALU.mult).then_inc(steps, 1)
                dve.wait_ge(steps, n + 3 * i + 3)
                dve.scalar_tensor_tensor(y, t, 1.5, y, ALU.add, ALU.mult).then_inc(steps, 1)

            ROOT = 10

            def inverse_root(y, a, t, steps, n):
                root_guess(y, a, steps)
                for i in range(3):
                    root_newton(y, a, t, steps, n, i)
                dve.wait_ge(steps, n + ROOT)

            dve.wait_ge(consts, 2)
            dve.tensor_scalar(part_b[:, 0:1], part_i[:], 6, 1, ALU.logical_shift_right, ALU.bitwise_and)
            link(dve.tensor_scalar(part_b[:, 1:2], part_i[:], 4, 3, ALU.logical_shift_right, ALU.bitwise_and))
            dve.tensor_copy(part_head[:], part_b[:, 1:2])
            link(dve.tensor_copy(neigh[:], part_b[:, 0:1]))
            for hh in range(HEADS_PER_QUAD):
                dve.tensor_scalar(head_rows[:, hh:hh + 1], part_head[:], float(hh), None, ALU.is_equal)
            link(dve.tensor_scalar(tmp_col[:], neigh[:], 0.0, SCALE * (1 + BETA), ALU.is_equal, ALU.mult))
            link(dve.scalar_tensor_tensor(qk_scale[:, 0:1], neigh[:], -SCALE * BETA, tmp_col[:], ALU.mult, ALU.add))
            link(dve.memset(qk_scale[:, 1:2], 1.0))

            fills = [0]
            fill_banks = [bank[(3, 4, 6, 7)[n % 4]] for n in range(15)] + [bank[7], bank[0], bank[1]]

            def got():
                fills[0] += 1
                dve.wait_ge(setup_ps, fills[0])
                return fill_banks[fills[0] - 1]

            for kt in range(CH * HALVES):
                b = got()
                dve.tensor_copy(tok_wT[:, kt, :], b[:, 0:D]).then_inc(setup_ev, 1)
            for c in range(6):
                b = got()
                for j in range(2):
                    dst = w_qkT[:, j, c * DH:(c + 1) * DH] if c < 4 else w_vT[:, j, (c - 4) * DH:(c - 3) * DH]
                    last = dve.tensor_copy(dst, b[0:DH, j * DH:(j + 1) * DH])
                last.then_inc(setup_ev, 1)
            b = got()
            dve.tensor_copy(wrT[:].rearrange("p r d -> p (r d)"), b[0:DS, 0:2 * D]).then_inc(setup_ev, 1)
            dve.wait_ge(w_loaded, 16 * 12)
            link(dve.tensor_tensor(emb_sq[:], emb[:], emb[:], ALU.mult))
            link(dve.tensor_reduce(emb_n2[:], emb_sq[:], axis=AX.X, op=ALU.add))
            link(dve.tensor_scalar(emb_a[:], emb_n2[:], 1e-30, None, ALU.max))
            inverse_root(emb_y[:], emb_a[:], emb_t[:], emb_y_step, 0)
            link(dve.tensor_tensor(emb_n1[:], emb_n2[:], emb_y[:], ALU.mult))
            link(dve.tensor_scalar(emb_n1[:], emb_n1[:], 1e-8, None, ALU.add))
            link(dve.reciprocal(emb_inv[:], emb_n1[:]))
            dve.tensor_tensor(emb_nrm[:], emb[:], emb_inv[:, :, None].to_broadcast([128, 2, DS]), ALU.mult)\
               .then_inc(embn_ready, 1)
            b = got()
            for c in range(2):
                for parity in range(2):
                    last = dve.tensor_copy(qk_bias[64 * c:64 * c + 64, parity:2 * QUADS:2],
                                           b[64 * parity:64 * parity + 64, 0:QUADS])
            link(last)
            for q in range(2):
                n = slice(q * QUADS, (q + 1) * QUADS)
                last = dve.tensor_scalar(qk_bias[:, n], qk_bias[:, n], qk_scale[:, q:q + 1], None, ALU.mult)
            last.then_inc(setup_ev, 1)
            b = got()
            dve.tensor_copy(v_bias[:], b[0:SPAN, 0:D]).then_inc(setup_ev, 1)
            for j in range(2):
                dve.tensor_scalar(w_qkT[:, j, :], w_qkT[:, j, :], g_col[:, j:j + 1], None, ALU.mult)
                dve.tensor_scalar(w_vT[:, j, :], w_vT[:, j, :], g_col[:, j:j + 1], None, ALU.mult)
            dve.wait_ge(consts, 3)
            for m in range(G_IMG):
                dve.tensor_copy(vals[:, m, :, :, HD:VW],
                                head_mask[:, None, :, HD:VW].to_broadcast([VG * TOK, VGROUPS, VG, 1]))
            dve.wait_ge(setup_ev, 15)
            for b, v in ((bank[3], 1.0), (bank[4], 0.0), (bank[6], 0.0)):
                last = dve.memset(b[:], v)
            last.then_inc(weights_ready, 1)
            dve.wait_ge(cls_loaded, 32)
            dve.wait_ge(weights_ready, 1)

            def embedded(g1, f):
                dve.wait_ge(patch_done, 2 * g1 + f + 1)
                if f == 0 and not (isinstance(g1, int) and g1 == 0):
                    dve.wait_ge(res_ready, g1)
                dve.tensor_tensor(h[:, 2 * f:2 * f + 2, :],
                                  bank[2 + 3 * f][0:SPAN, 0:2 * D].rearrange("p (t d) -> p t d", t=2),
                                  tok_bias[:, None, :].to_broadcast([SPAN, 2, D]), ALU.add).then_inc(h_ready, 1)
                dve.wait_ge(h_ready, 2 * g1 + f + 1)
                take(dve)
                for j in range(2 * f, 2 * f + 2):
                    last = dve.bn_stats(st[:, j, :], h[:, j, :])
                if f == 1:
                    last.then_inc(st_ready, 1)

            def variance(g1):
                dve.wait_ge(st_ready, 3 * g1 + 1)
                take(dve)
                for j in range(TILES):
                    last = dve.bn_aggr(mv[:, j, :], st[:, j, :])
                last.then_inc(st_ready, 1)
                dve.wait_ge(st_ready, 3 * g1 + 2)
                dve.tensor_scalar(va[:], mv[:, :, 1], 1 + LN_EPS, LN_EPS * LN_EPS, ALU.mult, ALU.add).then_inc(st_ready, 1)
                dve.wait_ge(st_ready, 3 * (g1 + 1))
                root_guess(rr[:], va[:], rr_step)

            def newton(g1, i):
                root_newton(rr[:], va[:], rt[:], rr_step, ROOT * g1, i)

            def normalise(g1):
                dve.wait_ge(rr_step, ROOT * (g1 + 1))
                for j in range(TILES):
                    if j == 0 and not (isinstance(g1, int) and g1 == 0):
                        dve.wait_ge(xn_transposed, 2 * g1)
                    dve.tensor_scalar(xn[:, j, :], h[:, j, :], mv[:, j, 0:1], rr[:, j:j + 1],
                                      ALU.subtract, ALU.mult).then_inc(xn_ready, 1)

            def values(g, f):
                mask = head_mask[:, None, :, 0:HD].to_broadcast([VG * TOK, 2 * VGROUPS, VG, HD])
                dve.wait_ge(v_filled, 4 * g + f + 1)
                src = bank[2 + 3 * (f % 2)][0:VG * TOK, 0:2 * D]
                dve.tensor_tensor(vals[:, 2 * f:2 * f + 2].rearrange("p m a b c -> p (m a) b c")[:, :, :, 0:HD],
                                  src.rearrange("p (a b c) -> p a b c", b=VG, c=HD), mask, ALU.mult)\
                   .then_inc(v_masked, 1)

            def cat(g, k):
                n = QUADS * G_IMG
                q = 1 - k
                dve.wait_ge(sums_ready, 2 * g + k + 1)
                dve.scalar_tensor_tensor(
                    qk[:, q * QUADS:(q + 1) * QUADS].rearrange("p a b c -> p (a b) c"),
                    qk_sum[:, q * n:(q + 1) * n, :], neigh[:, 0:1], qk_pad[:, q * n:(q + 1) * n, 1:1 + TOK],
                    ALU.mult, ALU.add).then_inc(cat_ready, 1)

            def softmax_in(g, j):
                b = bank[4 + 2 * (j % 2)]
                dve.wait_ge(scores_done, TILES * g + j + 1)
                s = b[0:SPAN, 0:HEADS * TOK].rearrange("p (a b) -> p a b", b=TOK)
                dve.tensor_reduce(smax[:, j % 2, :], s, axis=AX.X, op=ALU.max).then_inc(smax_ready, 1)
                dve.wait_ge(smax_ready, TILES * g + j + 1)
                dve.wait_ge(p_transposed, TILES * g + j + 1)
                dve.tensor_tensor(probs[:, j % 2], s, smax[:, j % 2, :, None].to_broadcast([SPAN, HEADS, TOK]),
                                  ALU.subtract).then_inc(scores_read, 1)

            def finish(g, j):
                dve.wait_ge(pv_done, TILES * g + j + 1)
                o = bank[3][0:SPAN, 256:256 + HEADS * VW].rearrange("p (a b) -> p a b", b=VW)
                dve.reciprocal(rsum[:], o[:, :, HD]).then_inc(fin_step, 1)
                dve.wait_ge(fin_step, TILES * g + j + 1)
                dve.tensor_tensor(att[:], o[:, :, 0:HD], rsum[:, :, None].to_broadcast([SPAN, HEADS, HD]),
                                  ALU.mult).then_inc(o_read, 1)
                dve.wait_ge(o_read, TILES * g + j + 2)
                if j == 0:
                    dve.wait_ge(res_ready, g + 1)
                    dve.wait_ge(stored, 32 * g + 1)
                dve.tensor_tensor(h2[:, j, :], att[:].rearrange("p a b -> p (a b)"), h_res[:, j, :], ALU.add)\
                   .then_inc(h2_ready, 1)
                if j == TILES - 1:
                    dve.wait_ge(h2_ready, TILES * (g + 1))
                    dve.sem_inc(res_used, 1)

            def queries(g):
                dve.wait_ge(queries_filled, g + 1)
                for m in range(2):
                    src = bank[7][64 * m:64 * m + 64, 0:G_IMG * TOK].rearrange("p (i n) -> p i n", n=TOK)
                    for c in range(2):
                        half = slice(64 * c, 64 * c + 64)
                        last = dve.tensor_scalar(qk_pad[half, m * G_IMG:(m + 1) * G_IMG, 1:1 + TOK], src,
                                                 qk_scale[half, 0:1], qk_bias[half, m:m + 1], ALU.mult, ALU.add)
                last.then_inc(queries_padded, 1)

            def prepare(g, embedding):
                if embedding:
                    embedded(g + 1, 0)
                    embedded(g + 1, 1)
                    variance(g + 1)
                for f in range(3):
                    values(g, f)
                    if embedding:
                        newton(g + 1, f)
                    elif f == 1:
                        cat(g, 1)
                if embedding:
                    normalise(g + 1)
                values(g, 3)

            def attention(g, more):
                softmax_in(g, 0)
                softmax_in(g, 1)
                softmax_in(g, 2)
                if more == 0:
                    dve.wait_ge(h2r_loaded, 16)
                    token_stats(0, EARLY // 2)
                softmax_in(g, 3)
                finish(g, 0)
                if more == 0:
                    token_stats(EARLY // 2, EARLY)
                finish(g, 1)
                finish(g, 2)
                if more == 0:
                    token_factors(0, EARLY, 0)
                finish(g, 3)
                if more > 0:
                    cat(g + 1, 0)
                    queries(g + 1)
                    if more > 1:
                        cat(g + 1, 1)
                    prepare(g + 1, more > 1)

            def token_stats(lo, hi):
                for t in range(lo, hi):
                    dve.bn_stats(st2[:, t, :], h2r[:, t, :]).then_inc(st2_ready, 1)

            def token_factors(lo, hi, part):
                dve.wait_ge(st2_ready, hi)
                for t in range(lo, hi):
                    last = dve.bn_aggr(mv2[:, t, :], st2[:, t, :])
                last.then_inc(va2_step, 1)
                dve.wait_ge(va2_step, 2 * part + 1)
                dve.tensor_scalar(va2[:, lo:hi], mv2[:, lo:hi, 1], LN_EPS, None, ALU.add).then_inc(va2_step, 1)
                dve.wait_ge(va2_step, 2 * part + 2)
                inverse_root(rs2[:, lo:hi], va2[:, lo:hi], rt2[:, lo:hi], rs2_step, ROOT * part)
                dve.scalar_tensor_tensor(nb2[:, lo:hi], mv2[:, lo:hi, 0], -1.0, rs2[:, lo:hi], ALU.mult, ALU.mult)\
                   .then_inc(nb2_ready, 1)

            embedded(0, 0)
            embedded(0, 1)
            b = got()
            dve.tensor_copy(embT[:].rearrange("p r d -> p (r d)"), b[0:DS, 0:256]).then_inc(setup_ev, 1)
            variance(0)
            for i in range(3):
                newton(0, i)
            normalise(0)
            b = got()
            dve.tensor_copy(r_mat[:].rearrange("p j n -> p (j n)"), b[0:DH, 0:512]).then_inc(setup_ev, 1)
            b = got()
            dve.tensor_copy(r_bias[:], b[:, 0:256]).then_inc(setup_ev, 1)
            queries(0)
            cat(0, 0)
            cat(0, 1)
            prepare(0, True)
            with dve.Fori(0, GROUPS - 2) as g:
                attention(g, 2)
            attention(GROUPS - 2, 1)
            attention(GROUPS - 1, 0)

            def normalised(t, i):
                return dve.tensor_scalar(x2t[i][:], h2r[:, bass.ds(t, 1), :].rearrange("p t d -> p (t d)"),
                                         mv2[:, bass.ds(t, 1), 0:1].rearrange("p t o -> p (t o)"),
                                         rs2[:, bass.ds(t, 1)], ALU.subtract, ALU.mult)

            def route_top(t, i, weigh):
                dve.wait_ge(logit_filled, t + 1)
                dve.wait_ge(exp_done, t + 1)
                dve.tensor_tensor(logit[i][:].rearrange("p r n -> p (r n)"), bank[2 + i][:, 0:256], r_bias[:],
                                  ALU.add).then_inc(logit_ready, 1)
                if weigh:
                    weight_sum(t - 1, 1 - i)
                dve.wait_ge(logit_ready, t + 3)
                take(dve)
                for r in range(2):
                    last = dve.max(top8[i][:, r, :], logit[i][:, r, :])
                last.then_inc(top_ready, 1)
                if weigh:
                    weight_den(t - 1, 1 - i)
                dve.wait_ge(top_ready, 2 * t + 1)
                dve.tensor_scalar(nmax[i][:], top8[i][:, :, 0], -1.0, None, ALU.mult).then_inc(nmax_ready, 1)
                for r in range(2):
                    last = dve.max_index(idx8[i][:, r, :], top8[i][:, r, :], logit[i][:, r, :])
                last.then_inc(top_ready, 1)
                if weigh:
                    weight_inv(t - 1, 1 - i)
                dve.wait_ge(top_ready, 2 * t + 2)
                dve.tensor_copy(idxf[:, bass.ds(t, 1)].rearrange("p t r k -> p (t r) k"), idx8[i][:, :, 0:TOPK])\
                   .then_inc(idx_done, 1)
                if weigh:
                    weight(t - 1, 1 - i)
                dve.wait_ge(idx_done, t + 1)
                dve.wait_ge(hot_used, t + 1)
                dve.tensor_tensor(
                    hot[i][:].rearrange("p r k n -> p (r k) n"),
                    iota_n[:, None, :].to_broadcast([ROWS, 2 * TOPK, EXPERTS]),
                    idxf[:, bass.ds(t, 1)].rearrange("p t r k -> p (t r k)")[:, :, None].to_broadcast([ROWS, 2 * TOPK, EXPERTS]),
                    ALU.is_equal).then_inc(hot_ready, 1)

            def weight_sum(t, i):
                dve.wait_ge(exp_done, t + 3)
                dve.tensor_reduce(s4[i][:], etop[i][:], axis=AX.X, op=ALU.add).then_inc(wt_step, 1)

            def weight_den(t, i):
                dve.wait_ge(wt_step, 4 * t + 1)
                dve.scalar_tensor_tensor(den[i][:], zsum[i][:], 1e-8, s4[i][:], ALU.mult, ALU.add).then_inc(wt_step, 1)

            def weight_inv(t, i):
                dve.wait_ge(wt_step, 4 * t + 2)
                dve.reciprocal(iden[i][:], den[i][:]).then_inc(wt_step, 1)

            def weight(t, i):
                dve.wait_ge(wt_step, 4 * t + 3)
                dve.tensor_tensor(wts[:, bass.ds(t, 1)].rearrange("p t r k -> p (t r) k"), etop[i][:],
                                  iden[i][:, :, None].to_broadcast([ROWS, 2, TOPK]), ALU.mult).then_inc(wt_step, 1)

            dve.wait_ge(consts, 4)
            route_top(0, 0, False)
            dve.wait_ge(h2r_loaded, 32)
            token_stats(EARLY, TTILES)
            token_factors(EARLY, TTILES, 1)
            with dve.Fori(0, PAIRS - 1) as p:
                for i in range(2):
                    route_top(2 * p + 1 + i, 1 - i, True)
            route_top(PAIRED - 1, 1, True)
            route_top(PAIRED, 0, True)
            for part in (weight_sum, weight_den, weight_inv, weight):
                part(PAIRED, 0)

            dve.wait_ge(hot_used, TTILES + 2)
            cnt = bank[4][:, 0:256].rearrange("p (r n) -> p r n", r=2)
            link(dve.tensor_tensor(diag[:], cnt, ident[:, None, :].to_broadcast([128, 2, 128]), ALU.mult))
            link(dve.tensor_reduce(cum[:], diag[:], axis=AX.X, op=ALU.add))
            link(dve.tensor_scalar(cnt_i[:], cum[:], float(ROWS - 1), None, ALU.add))
            link(dve.tensor_scalar(nblk_i[:], cnt_i[:], 7, None, ALU.logical_shift_right))
            dve.tensor_copy(nblk[:], nblk_i[:]).then_inc(plan_ev, 1)
            dve.wait_ge(plan_ev, 1)
            dve.wait_ge(plan_ps, 1)
            link(dve.tensor_copy(cum[:], bank[5][:, 0:2]))
            link(dve.tensor_tensor(base_c[:], cum[:], nblk[:], ALU.subtract))
            link(dve.tensor_scalar(base_c[:], base_c[:], float(ROWS), None, ALU.mult))
            for r in range(2):
                last = dve.tensor_scalar(diag[:, r, :], ident[:], base_c[:, r:r + 1], None, ALU.mult)
            last.then_inc(plan_ev, 1)
            for r in range(2):
                last = dve.tensor_scalar(passed[:, r, :], iota_blk[:], cum[:, r:r + 1], None, ALU.is_ge)
            last.then_inc(plan_ev, 1)
            dve.wait_ge(plan_ps, 2)
            link(dve.tensor_copy(base_b[:], bank[6][:, 0:256]))
            dve.wait_ge(plan_ps, 3)
            link(dve.tensor_scalar(owner[:].rearrange("p r b -> p (r b)"), bank[7][0:1, 0:2 * BLOCKS],
                                   float(EXPERTS - 1), None, ALU.min))
            link(dve.tensor_scalar(step_has[:], bank[7][0:1, 0:2 * BLOCKS].rearrange("p (r s n) -> p r s n", r=2, n=BODY)[:, :, :, 0],
                                   float(EXPERTS), None, ALU.is_lt))
            link(dve.tensor_reduce(steps_f[:], step_has[:], axis=AX.X, op=ALU.add))
            dve.tensor_copy(steps_used[:], steps_f[:]).then_inc(plan_ev, 1)

            def slot(t, i, k):
                dve.tensor_tensor(srank[i][:], rank[:, bass.ds(t, 1), :].rearrange("p a b -> p (a b)"), base_b[:],
                                  ALU.add).then_inc(slot_step, 1)
                dve.wait_ge(slot_step, 3 * t + 1)
                for e in range(2 * TOPK):
                    r = e // TOPK
                    last = dve.scalar_tensor_tensor(
                        pick[:, e, :], iota_n[:],
                        idxf[:, bass.ds(t, 1)].rearrange("p t r k -> p (t r k)")[:, e:e + 1],
                        srank[i][:, r * EXPERTS:(r + 1) * EXPERTS], ALU.is_equal, ALU.mult,
                        accum_out=slotf[i][:, e:e + 1])
                last.then_inc(slot_step, 1)
                dve.wait_ge(slot_step, 3 * t + 2)
                dve.tensor_copy(slots[:, bass.ds(t, 1), :].rearrange("p a b -> p (a b)"), slotf[i][:]).then_inc(slot_step, 1)
                if not (isinstance(k, int) and k == 0):
                    dve.wait_ge(scattered[i], 64 * k)
                normalised(t, i)
                dve.tensor_copy(slot_now[i][:], slotf[i][:]).then_inc(slot_ready, 1)

            for i in range(2):
                slot(i, i, 0)
            with dve.Fori(0, PAIRS - 1) as p:
                for i in range(2):
                    slot(2 * p + 2 + i, i, p + 1)
            slot(PAIRED, 0, PAIRS)

            def combine(layer, t, i, k):
                width = (RANK, D)[layer]
                dve.wait_ge(gathered[layer][i], 64 * k)
                w = wts[:, bass.ds(t, 1)].rearrange("p t r k -> p (t r k)")
                for e in range(TOPK):
                    we = w[:, layer * TOPK + e:layer * TOPK + e + 1]
                    g = gat[i][:, e, 0:width]
                    if e == 0 and layer == 0:
                        ins = dve.tensor_scalar(acc[i][:, 0, 0:width], g, we, None, ALU.mult)
                    else:
                        prev = h2r[:, bass.ds(t, 1), :].rearrange("p t d -> p (t d)") if e == 0 else acc[i][:, (e - 1) % 2, 0:width]
                        dst = comb[i][:, 0:width] if e == TOPK - 1 else acc[i][:, e % 2, 0:width]
                        if e == TOPK - 1:
                            if layer == 1:
                                dve.wait_ge(comb_out[1][i], 16 * (k - 1) + 1)
                            elif not (isinstance(k, int) and k == 1):
                                dve.wait_ge(comb_out[0][i], 64 * (k - 1))
                            if layer == 0:
                                dve.tensor_copy(slot_put[i][:], slots[:, bass.ds(t, 1), :].rearrange("p a b -> p (a b)"))
                        ins = dve.scalar_tensor_tensor(dst, g, we, prev, ALU.mult, ALU.add)
                    if e < TOPK - 1:
                        ins.then_inc(comb_step[layer], 1)
                        dve.wait_ge(comb_step[layer], (TOPK - 1) * t + e + 1)
                    else:
                        ins.then_inc(comb_ready[layer], 1)

            def indices(layer, t, i):
                dve.tensor_copy(slot_get[i][:], slots[:, bass.ds(t, 1), :].rearrange("p a b -> p (a b)"))\
                   .then_inc(idx_ready[layer], 1)

            def tiles(layer):
                for i in range(2):
                    indices(layer, i, i)
                for i in range(2):
                    combine(layer, i, i, 1)
                    indices(layer, 2 + i, i)
                with dve.Fori(0, PAIRS - 2) as p:
                    for i in range(2):
                        combine(layer, 2 * p + 2 + i, i, p + 2)
                        indices(layer, 2 * p + 4 + i, i)
                combine(layer, PAIRED - 2, 0, PAIRS)
                indices(layer, PAIRED, 0)
                combine(layer, PAIRED - 1, 1, PAIRS)
                combine(layer, PAIRED, 0, PAIRS + 1)

            def experts(layer):
                width = (RANK, D)[layer]
                used = dve.value_load(steps_used[0:1, layer:layer + 1], min_val=1, max_val=STEPS)

                def step(s):
                    for q in range(PAIRS_OF_STEP):
                        r = q // 2
                        dve.wait_ge(y_filled[layer], s * (PAIRS_OF_STEP) + q + 1 + 2 * RING)
                        if q % 2 == 0 and not isinstance(s, int):
                            dve.wait_ge(y_stored[layer][r], 16 * s)
                        src = bank[2 + q % 2][:].rearrange("p (k w) -> p k w", k=2)[:, :, 0:width]
                        dve.tensor_copy(os_[r][:, 2 * (q % 2):2 * (q % 2) + 2, 0:width], src)\
                           .then_inc(y_copied[layer], 1)

                step(0)
                with dve.Fori(0, STEPS - 1) as s, dve.If(s + 1 < used):
                    step(s + 1)

            dve.wait_ge(plan_ev, 4)
            for layer in range(2):
                experts(layer)
                tiles(layer)


_INS = ['x', 'cls_tok', 'L0_tok_W', 'L0_tok_b', 'L0_attn_qkv_w', 'L0_attn_qkv_b', 'L0_attn_ln_g', 'L0_attn_ln_b',
        'L0_ffn_f_know', 'L0_ffn_r_know', 'L0_ffn_W_fk', 'L0_ffn_b_fk', 'L0_ffn_W_rk', 'L0_ffn_b_rk',
        'L0_ffn_emb_fk', 'L0_ffn_emb_rk']


def kernel(**inputs):
    import concourse.bacc as bacc
    from concourse.bass_utils import run_bass_kernel_spmd

    nc = bacc.Bacc("TRN2", target_bir_lowering=False, num_devices=1)
    arrays, args = {}, []
    for name in _INS:
        a = np.ascontiguousarray(inputs[name])
        arrays[f"in_{name}"] = a
        args.append(nc.dram_tensor(f"in_{name}", a.shape, mybir.dt.from_np(a.dtype), kind="ExternalInput").ap())
    res = nc.dram_tensor("out_0", (TOKENS, D), F32, kind="ExternalOutput").ap()
    tower(nc, *args, res)
    r = run_bass_kernel_spmd(nc, [arrays], core_ids=[0])
    return r.results[0]["out_0"].reshape(BATCH, TOK, D)
```
